# Optimizing a Trainium2 kernel written in Bass

```python
import numpy as np
import jax
import jax.numpy as jnp

def _softmax(x, axis=-1):
    return jax.nn.softmax(x, axis=axis)

def _gelu(x):
    return jax.nn.gelu(x, approximate=True)

def _silu(x):
    return jax.nn.silu(x)

def _sigmoid(x):
    return jax.nn.sigmoid(x)

def _layernorm(x, axis=-1, eps=1e-05):
    m = jnp.mean(x, axis=axis, keepdims=True)
    v = jnp.var(x, axis=axis, keepdims=True)
    return (x - m) / jnp.sqrt(v + eps)

def _scatter_add(tgt, idx, src, axis=0):
    return tgt.at[idx].add(src)

def _segment_sum(src, seg, n):
    return jax.ops.segment_sum(src, seg, n)
kernel_name = 'mk_adaln_d2_jaxref_r8_f8740c'

def setup_inputs(seed: int=0):
    np.random.seed(seed)
    _w = jnp.asarray

    def _L0_attn_setup():
        import jax, jax.numpy as jnp
        import numpy as np
        DIMS = 128
        HEAD = 16
        HD = DIMS // HEAD
        MAX_ITER = 3
        MIN_SIZE = 64
        MAX_SIZE = 256
        UP_WIN, DOWN_WIN = (1.1, 0.9)
        UP_DIFF, DOWN_DIFF = (0.05, 0.001)
        B, T = (2, 128)

        def _ln(x, w, eps=1e-05):
            m = jnp.mean(x, axis=-1, keepdims=True)
            v = jnp.var(x, axis=-1, keepdims=True)
            return (x - m) * jax.lax.rsqrt(v + eps) * w

        def _focus(x, Wq, bq, Wk, Wv, bv, Wo, bo, lna_w, lnb_w, lnc_w, lnd_w, lq_w, lq_b, lk_w, lk_b, lv_w, lv_b, threshold, temp_base, factor):
            b, t, d = x.shape
            q = _ln(x, lna_w) @ Wq.T + bq
            kk = _ln(x, lnb_w) @ Wk.T
            v = _ln(x, lnb_w) @ Wv.T + bv
            sc = HD ** (-0.25)

            def _shape(u):
                return u.reshape(b, t, HEAD, HD).transpose(0, 2, 1, 3)
            q_full = _shape(q * sc)
            k_full = _shape(kk * sc)
            v_full = _shape(v)
            thr = jax.lax.stop_gradient(threshold)
            fac = jax.lax.stop_gradient(factor)
            t0 = jax.lax.stop_gradient(temp_base)
            cw0 = jnp.int32(max(min(t, MAX_SIZE), MIN_SIZE))
            inv_sqrt_e = jnp.float32(1.0 / np.sqrt(HD))
            pos = jnp.arange(t)

            def step(carry, i):
                qcur, prev, attn, cw, temp, done = carry
                qp = qcur @ lq_w.T + lq_b
                kp = k_full @ lk_w.T + lk_b
                vp = v_full @ lv_w.T + lv_b
                sq = _ln(qp, lnc_w)
                sk = _ln(kp, lnd_w)
                tscale = jnp.where(temp > 0, jax.lax.rsqrt(temp), jnp.float32(1.0))
                sq = sq * tscale
                scores = jnp.einsum('bhqd,bhkd->bhqk', sq, sk) * inv_sqrt_e
                in_win = pos < cw
                scores = jnp.where(in_win[None, None, None, :], scores, -jnp.inf)
                probs = jax.nn.softmax(scores, axis=-1)
                out = jnp.einsum('bhqk,bhkd->bhqd', probs, vp)
                iter_out = jnp.where(in_win[None, None, :, None], out, 0.0)
                diff = jnp.mean(jnp.abs(iter_out - prev))
                converged = (diff < thr + fac * diff) & (i > 0)
                upd = ~done & ~converged
                new_done = done | converged
                attn_n = jnp.where(done, attn, iter_out)
                prev_n = jnp.where(upd, iter_out, prev)
                qcur_n = jnp.where(upd, qcur + iter_out, qcur)
                up = (cw.astype(jnp.float32) * UP_WIN).astype(jnp.int32)
                down = (cw.astype(jnp.float32) * DOWN_WIN).astype(jnp.int32)
                nw = jnp.where(diff > UP_DIFF, up, jnp.where((diff < DOWN_DIFF) & (cw > MIN_SIZE), down, cw))
                nw = jnp.clip(nw, MIN_SIZE, t)
                cw_n = jnp.where(upd, nw, cw)
                temp_n = jnp.where(upd, temp + jnp.float32(0.005), temp)
                return ((qcur_n, prev_n, attn_n, cw_n, temp_n, new_done), None)
            zeros = jnp.zeros_like(q_full)
            carry0 = (q_full, zeros, zeros, cw0, t0, jnp.array(False))
            (_, _, attn_out, _, _, _), _ = jax.lax.scan(step, carry0, jnp.arange(MAX_ITER))
            output = attn_out.transpose(0, 2, 1, 3).reshape(b, t, d)
            return output @ Wo.T + bo
        key = jax.random.key(seed)
        ks = jax.random.split(key, 12)

        def lin_w(k, o, i):
            return (jax.random.normal(k, (o, i), dtype=jnp.float32) / np.sqrt(i)).astype(jnp.float32)
        return {'x': jax.random.normal(ks[0], (B, T, DIMS), dtype=jnp.float32), 'Wq': lin_w(ks[1], DIMS, DIMS), 'bq': jnp.zeros((DIMS,), jnp.float32), 'Wk': lin_w(ks[2], DIMS, DIMS), 'Wv': lin_w(ks[3], DIMS, DIMS), 'bv': jnp.zeros((DIMS,), jnp.float32), 'Wo': lin_w(ks[4], DIMS, DIMS), 'bo': jnp.zeros((DIMS,), jnp.float32), 'lna_w': jnp.ones((DIMS,), jnp.float32), 'lnb_w': jnp.ones((DIMS,), jnp.float32), 'lnc_w': jnp.ones((HD,), jnp.float32), 'lnd_w': jnp.ones((HD,), jnp.float32), 'lq_w': lin_w(ks[5], HD, HD), 'lq_b': jnp.zeros((HD,), jnp.float32), 'lk_w': lin_w(ks[6], HD, HD), 'lk_b': jnp.zeros((HD,), jnp.float32), 'lv_w': lin_w(ks[7], HD, HD), 'lv_b': jnp.zeros((HD,), jnp.float32), 'threshold': jnp.float32(0.01), 'temp_base': jnp.float32(1.0), 'factor': jnp.float32(0.1)}
    _L0_attn_in = _L0_attn_setup()

    def _L0_ffn_setup():
        import math
        import jax, jax.numpy as jnp
        import numpy as np
        TOP_K = 2
        _GELU_C = math.sqrt(2.0 / math.pi)

        def gelu_new(x):
            return 0.5 * x * (1.0 + jnp.tanh(_GELU_C * (x + 0.044715 * x * x * x)))
        key = jax.random.key(seed)
        ks = jax.random.split(key, 6)
        B, T, C, E, H = (2, 256, 128, 8, 512)
        s_in = 1.0 / math.sqrt(C)
        s_hid = 1.0 / math.sqrt(H)
        return {'x': jax.random.normal(ks[0], (B, T, C), dtype=jnp.float32), 'router_w': jax.random.normal(ks[1], (E, C), dtype=jnp.float32) * s_in, 'w_fc': jax.random.normal(ks[2], (E, C, H), dtype=jnp.float32) * s_in, 'b_fc': jax.random.normal(ks[3], (E, H), dtype=jnp.float32) * 0.02, 'w_proj': jax.random.normal(ks[4], (E, H, C), dtype=jnp.float32) * s_hid, 'b_proj': jax.random.normal(ks[5], (E, C), dtype=jnp.float32) * 0.02}
    _L0_ffn_in = _L0_ffn_setup()
    _L0_c = _w((lambda *s: np.random.randn(*s).astype(np.float32) * 0.05)(1, 128))
    _L0_wmod = _w((lambda *s: np.random.randn(*s).astype(np.float32) * 0.05)(128, 6 * 128) * 128 ** (-0.5))

    def _L1_attn_setup():
        import jax, jax.numpy as jnp
        import numpy as np
        B, S, D, NF = (4, 1024, 128, 32)
        key = jax.random.key(seed)
        k1, k2, k3, k4 = jax.random.split(key, 4)
        x = jax.random.normal(k1, (B, S, D), dtype=jnp.float32)
        W_in = jax.random.normal(k2, (2 * NF, D), dtype=jnp.float32) * 0.02
        W_out = jax.random.normal(k3, (D, 2 * NF), dtype=jnp.float32) * 0.02
        log_decay = jnp.linspace(-3.0, -0.001, NF).astype(jnp.float32)
        frequencies = jax.random.normal(k4, (NF,), dtype=jnp.float32)
        return {'x': x, 'W_in': W_in, 'W_out': W_out, 'log_decay': log_decay, 'frequencies': frequencies}
    _L1_attn_in = _L1_attn_setup()

    def _L1_ffn_setup():
        import jax, jax.numpy as jnp
        import numpy as np
        B, S, D, F, E = (4, 256, 128, 512, 8)
        LN_EPS = 1e-05
        key = jax.random.key(seed)
        ks = jax.random.split(key, 6)
        sc = 0.02
        return {'x': jax.random.normal(ks[0], (B, S, D), dtype=jnp.float32), 'Wr': jax.random.normal(ks[1], (D, E), dtype=jnp.float32) * sc, 'br': jnp.zeros((E,), jnp.float32), 'ln_g': jnp.ones((D,), jnp.float32), 'ln_b': jnp.zeros((D,), jnp.float32), 'W1': jax.random.normal(ks[2], (E, D, F), dtype=jnp.float32) * sc, 'b1': jnp.zeros((E, F), jnp.float32), 'W2': jax.random.normal(ks[3], (E, F, D), dtype=jnp.float32) * sc, 'b2': jnp.zeros((E, D), jnp.float32)}
    _L1_ffn_in = _L1_ffn_setup()
    _L1_c = _w((lambda *s: np.random.randn(*s).astype(np.float32) * 0.05)(1, 128))
    _L1_wmod = _w((lambda *s: np.random.randn(*s).astype(np.float32) * 0.05)(128, 6 * 128) * 128 ** (-0.5))
    _d = {'L0_attn_x': _L0_attn_in['x'], 'L0_attn_Wq': _L0_attn_in['Wq'], 'L0_attn_bq': _L0_attn_in['bq'], 'L0_attn_Wk': _L0_attn_in['Wk'], 'L0_attn_Wv': _L0_attn_in['Wv'], 'L0_attn_bv': _L0_attn_in['bv'], 'L0_attn_Wo': _L0_attn_in['Wo'], 'L0_attn_bo': _L0_attn_in['bo'], 'L0_attn_lna_w': _L0_attn_in['lna_w'], 'L0_attn_lnb_w': _L0_attn_in['lnb_w'], 'L0_attn_lnc_w': _L0_attn_in['lnc_w'], 'L0_attn_lnd_w': _L0_attn_in['lnd_w'], 'L0_attn_lq_w': _L0_attn_in['lq_w'], 'L0_attn_lq_b': _L0_attn_in['lq_b'], 'L0_attn_lk_w': _L0_attn_in['lk_w'], 'L0_attn_lk_b': _L0_attn_in['lk_b'], 'L0_attn_lv_w': _L0_attn_in['lv_w'], 'L0_attn_lv_b': _L0_attn_in['lv_b'], 'L0_attn_threshold': _L0_attn_in['threshold'], 'L0_attn_temp_base': _L0_attn_in['temp_base'], 'L0_attn_factor': _L0_attn_in['factor'], 'L0_ffn_router_w': _L0_ffn_in['router_w'], 'L0_ffn_w_fc': _L0_ffn_in['w_fc'], 'L0_ffn_b_fc': _L0_ffn_in['b_fc'], 'L0_ffn_w_proj': _L0_ffn_in['w_proj'], 'L0_ffn_b_proj': _L0_ffn_in['b_proj'], 'L0_c': _L0_c, 'L0_wmod': _L0_wmod, 'L1_attn_W_in': _L1_attn_in['W_in'], 'L1_attn_W_out': _L1_attn_in['W_out'], 'L1_attn_log_decay': _L1_attn_in['log_decay'], 'L1_attn_frequencies': _L1_attn_in['frequencies'], 'L1_ffn_Wr': _L1_ffn_in['Wr'], 'L1_ffn_br': _L1_ffn_in['br'], 'L1_ffn_ln_g': _L1_ffn_in['ln_g'], 'L1_ffn_ln_b': _L1_ffn_in['ln_b'], 'L1_ffn_W1': _L1_ffn_in['W1'], 'L1_ffn_b1': _L1_ffn_in['b1'], 'L1_ffn_W2': _L1_ffn_in['W2'], 'L1_ffn_b2': _L1_ffn_in['b2'], 'L1_c': _L1_c, 'L1_wmod': _L1_wmod}
    _x0 = _d['L0_attn_x']
    _d['L0_attn_x'] = jax.random.normal(jax.random.fold_in(jax.random.key(seed), 1), (1, 2048, 128), dtype=_x0.dtype)
    del _x0
    return _d

def reference(L0_attn_x, L0_attn_Wq, L0_attn_bq, L0_attn_Wk, L0_attn_Wv, L0_attn_bv, L0_attn_Wo, L0_attn_bo, L0_attn_lna_w, L0_attn_lnb_w, L0_attn_lnc_w, L0_attn_lnd_w, L0_attn_lq_w, L0_attn_lq_b, L0_attn_lk_w, L0_attn_lk_b, L0_attn_lv_w, L0_attn_lv_b, L0_attn_threshold, L0_attn_temp_base, L0_attn_factor, L0_ffn_router_w, L0_ffn_w_fc, L0_ffn_b_fc, L0_ffn_w_proj, L0_ffn_b_proj, L0_c, L0_wmod, L1_attn_W_in, L1_attn_W_out, L1_attn_log_decay, L1_attn_frequencies, L1_ffn_Wr, L1_ffn_br, L1_ffn_ln_g, L1_ffn_ln_b, L1_ffn_W1, L1_ffn_b1, L1_ffn_W2, L1_ffn_b2, L1_c, L1_wmod):

    def _L0_attn_ref(x, Wq, bq, Wk, Wv, bv, Wo, bo, lna_w, lnb_w, lnc_w, lnd_w, lq_w, lq_b, lk_w, lk_b, lv_w, lv_b, threshold, temp_base, factor):
        import jax, jax.numpy as jnp
        import numpy as np
        DIMS = 128
        HEAD = 16
        HD = DIMS // HEAD
        MAX_ITER = 3
        MIN_SIZE = 64
        MAX_SIZE = 256
        UP_WIN, DOWN_WIN = (1.1, 0.9)
        UP_DIFF, DOWN_DIFF = (0.05, 0.001)
        B, T = (2, 128)

        def _ln(x, w, eps=1e-05):
            m = jnp.mean(x, axis=-1, keepdims=True)
            v = jnp.var(x, axis=-1, keepdims=True)
            return (x - m) * jax.lax.rsqrt(v + eps) * w

        def _focus(x, Wq, bq, Wk, Wv, bv, Wo, bo, lna_w, lnb_w, lnc_w, lnd_w, lq_w, lq_b, lk_w, lk_b, lv_w, lv_b, threshold, temp_base, factor):
            b, t, d = x.shape
            q = _ln(x, lna_w) @ Wq.T + bq
            kk = _ln(x, lnb_w) @ Wk.T
            v = _ln(x, lnb_w) @ Wv.T + bv
            sc = HD ** (-0.25)

            def _shape(u):
                return u.reshape(b, t, HEAD, HD).transpose(0, 2, 1, 3)
            q_full = _shape(q * sc)
            k_full = _shape(kk * sc)
            v_full = _shape(v)
            thr = jax.lax.stop_gradient(threshold)
            fac = jax.lax.stop_gradient(factor)
            t0 = jax.lax.stop_gradient(temp_base)
            cw0 = jnp.int32(max(min(t, MAX_SIZE), MIN_SIZE))
            inv_sqrt_e = jnp.float32(1.0 / np.sqrt(HD))
            pos = jnp.arange(t)

            def step(carry, i):
                qcur, prev, attn, cw, temp, done = carry
                qp = qcur @ lq_w.T + lq_b
                kp = k_full @ lk_w.T + lk_b
                vp = v_full @ lv_w.T + lv_b
                sq = _ln(qp, lnc_w)
                sk = _ln(kp, lnd_w)
                tscale = jnp.where(temp > 0, jax.lax.rsqrt(temp), jnp.float32(1.0))
                sq = sq * tscale
                scores = jnp.einsum('bhqd,bhkd->bhqk', sq, sk) * inv_sqrt_e
                in_win = pos < cw
                scores = jnp.where(in_win[None, None, None, :], scores, -jnp.inf)
                probs = jax.nn.softmax(scores, axis=-1)
                out = jnp.einsum('bhqk,bhkd->bhqd', probs, vp)
                iter_out = jnp.where(in_win[None, None, :, None], out, 0.0)
                diff = jnp.mean(jnp.abs(iter_out - prev))
                converged = (diff < thr + fac * diff) & (i > 0)
                upd = ~done & ~converged
                new_done = done | converged
                attn_n = jnp.where(done, attn, iter_out)
                prev_n = jnp.where(upd, iter_out, prev)
                qcur_n = jnp.where(upd, qcur + iter_out, qcur)
                up = (cw.astype(jnp.float32) * UP_WIN).astype(jnp.int32)
                down = (cw.astype(jnp.float32) * DOWN_WIN).astype(jnp.int32)
                nw = jnp.where(diff > UP_DIFF, up, jnp.where((diff < DOWN_DIFF) & (cw > MIN_SIZE), down, cw))
                nw = jnp.clip(nw, MIN_SIZE, t)
                cw_n = jnp.where(upd, nw, cw)
                temp_n = jnp.where(upd, temp + jnp.float32(0.005), temp)
                return ((qcur_n, prev_n, attn_n, cw_n, temp_n, new_done), None)
            zeros = jnp.zeros_like(q_full)
            carry0 = (q_full, zeros, zeros, cw0, t0, jnp.array(False))
            (_, _, attn_out, _, _, _), _ = jax.lax.scan(step, carry0, jnp.arange(MAX_ITER))
            output = attn_out.transpose(0, 2, 1, 3).reshape(b, t, d)
            return output @ Wo.T + bo
        return _focus(x, Wq, bq, Wk, Wv, bv, Wo, bo, lna_w, lnb_w, lnc_w, lnd_w, lq_w, lq_b, lk_w, lk_b, lv_w, lv_b, threshold, temp_base, factor)

    def _L0_ffn_ref(x, router_w, w_fc, b_fc, w_proj, b_proj):
        import math
        import jax, jax.numpy as jnp
        import numpy as np
        TOP_K = 2
        _GELU_C = math.sqrt(2.0 / math.pi)

        def gelu_new(x):
            return 0.5 * x * (1.0 + jnp.tanh(_GELU_C * (x + 0.044715 * x * x * x)))
        B, T, C = x.shape
        E = router_w.shape[0]
        N = B * T
        xf = x.reshape(N, C)
        logits = xf @ router_w.T
        probs = jax.nn.softmax(logits, axis=-1)
        topk_probs, topk_idx = jax.lax.top_k(probs, TOP_K)
        topk_probs = topk_probs / jnp.sum(topk_probs, axis=-1, keepdims=True)
        combine = jnp.zeros((N, E), dtype=x.dtype).at[jnp.arange(N)[:, None], topk_idx].add(topk_probs)
        h = gelu_new(jnp.einsum('nc,ech->neh', xf, w_fc) + b_fc)
        out = jnp.einsum('neh,ehc->nec', h, w_proj) + b_proj
        y = jnp.einsum('nec,ne->nc', out, combine)
        return y.reshape(B, T, C)

    def _L1_attn_ref(x, W_in, W_out, log_decay, frequencies):
        import jax, jax.numpy as jnp
        import numpy as np
        B, S, D, NF = (4, 1024, 128, 32)
        b, s, d = x.shape
        nf = log_decay.shape[0]
        dt = jnp.float32(1.0)
        decay = jax.nn.sigmoid(log_decay)
        omega = frequencies * 0.1 * dt
        rot = jax.lax.complex(jnp.cos(omega), jnp.sin(omega))
        A = decay * rot
        spectral = jnp.einsum('bsd,fd->bsf', x, W_in)
        u = jax.lax.complex(spectral[..., :nf], spectral[..., nf:])
        ones = jnp.ones((1, nf), dtype=A.dtype)
        A_rep = jnp.broadcast_to(A[None, :], (s - 1, nf))
        powers = jnp.cumprod(jnp.concatenate([ones, A_rep], axis=0), axis=0)
        kernel = powers * rot[None, :]
        n_fft = 2 * s
        U_f = jnp.fft.fft(u, n=n_fft, axis=1)
        K_f = jnp.fft.fft(kernel, n=n_fft, axis=0)
        y = jnp.fft.ifft(U_f * K_f[None, :, :], axis=1)[:, :s, :]
        feats = jnp.concatenate([y.real, y.imag], axis=-1)
        return jnp.einsum('bsf,df->bsd', feats, W_out)

    def _L1_ffn_ref(x, Wr, br, ln_g, ln_b, W1, b1, W2, b2):
        import jax, jax.numpy as jnp
        import numpy as np
        B, S, D, F, E = (4, 256, 128, 512, 8)
        LN_EPS = 1e-05
        tokens_shape = x.shape[:-1]
        xt = x.reshape(-1, x.shape[-1])
        router_logits = xt @ Wr + br
        router_probs = jax.nn.softmax(router_logits, axis=-1)
        gates = jnp.max(router_probs, axis=-1, keepdims=True)
        idx = jnp.argmax(router_probs, axis=-1)
        onehot = jax.nn.one_hot(idx, E, dtype=xt.dtype)
        mu = jnp.mean(xt, axis=-1, keepdims=True)
        var = jnp.mean(jnp.square(xt - mu), axis=-1, keepdims=True)
        xn = (xt - mu) * jax.lax.rsqrt(var + LN_EPS) * ln_g + ln_b
        h = jnp.einsum('te,td,edf->tf', onehot, xn, W1) + b1[idx]
        h = jax.nn.relu(h)
        y = jnp.einsum('te,tf,efd->td', onehot, h, W2) + b2[idx]
        y = y * gates
        return y.reshape(tokens_shape + (y.shape[-1],))
    x = L0_attn_x
    mod = (_silu(L0_c) @ L0_wmod).reshape(L0_c.shape[0], 6, 1, -1)
    sa, ca, ga, sb, cb, gb = (mod[:, 0], mod[:, 1], mod[:, 2], mod[:, 3], mod[:, 4], mod[:, 5])
    ga = (2 * (ga >= 0) - 1) * jnp.maximum(jnp.abs(ga), 0.25)
    gb = (2 * (gb >= 0) - 1) * jnp.maximum(jnp.abs(gb), 0.25)
    h = _layernorm(x, axis=-1) * (1 + ca) + sa
    x = x + ga * _L0_attn_ref(h, L0_attn_Wq, L0_attn_bq, L0_attn_Wk, L0_attn_Wv, L0_attn_bv, L0_attn_Wo, L0_attn_bo, L0_attn_lna_w, L0_attn_lnb_w, L0_attn_lnc_w, L0_attn_lnd_w, L0_attn_lq_w, L0_attn_lq_b, L0_attn_lk_w, L0_attn_lk_b, L0_attn_lv_w, L0_attn_lv_b, L0_attn_threshold, L0_attn_temp_base, L0_attn_factor)
    h = _layernorm(x, axis=-1) * (1 + cb) + sb
    x = x + gb * _L0_ffn_ref(h, L0_ffn_router_w, L0_ffn_w_fc, L0_ffn_b_fc, L0_ffn_w_proj, L0_ffn_b_proj)
    mod = (_silu(L1_c) @ L1_wmod).reshape(L1_c.shape[0], 6, 1, -1)
    sa, ca, ga, sb, cb, gb = (mod[:, 0], mod[:, 1], mod[:, 2], mod[:, 3], mod[:, 4], mod[:, 5])
    ga = (2 * (ga >= 0) - 1) * jnp.maximum(jnp.abs(ga), 0.25)
    gb = (2 * (gb >= 0) - 1) * jnp.maximum(jnp.abs(gb), 0.25)
    h = _layernorm(x, axis=-1) * (1 + ca) + sa
    x = x + ga * _L1_attn_ref(h, L1_attn_W_in, L1_attn_W_out, L1_attn_log_decay, L1_attn_frequencies)
    h = _layernorm(x, axis=-1) * (1 + cb) + sb
    x = x + gb * _L1_ffn_ref(h, L1_ffn_Wr, L1_ffn_br, L1_ffn_ln_g, L1_ffn_ln_b, L1_ffn_W1, L1_ffn_b1, L1_ffn_W2, L1_ffn_b2)
    return x

_drawn_inputs = setup_inputs


def setup_inputs(seed=0):
    import zlib

    import numpy as np

    out = dict(_drawn_inputs(seed))
    spreads = {'L0_attn_bq': (0.0, 0.8),
     'L0_attn_bv': (0.0, 0.718),
     'L0_attn_bo': (0.0, 0.288),
     'L0_attn_lna_w': (1.0, 0.6),
     'L0_attn_lnb_w': (1.0, 0.6),
     'L0_attn_lnc_w': (1.0, 0.6),
     'L0_attn_lnd_w': (1.0, 0.6),
     'L0_attn_lq_b': (0.0, 2.0),
     'L0_attn_lk_b': (0.0, 2.0),
     'L0_attn_lv_b': (0.0, 0.764),
     'L1_ffn_br': (0.0, 0.8),
     'L1_ffn_ln_g': (1.0, 0.6),
     'L1_ffn_ln_b': (0.0, 0.8),
     'L1_ffn_b1': (0.0, 0.8),
     'L1_ffn_b2': (0.0, 0.8)}
    factors = {'L0_attn_Wq': 5.99,
     'L0_attn_Wk': 5.696,
     'L0_attn_Wv': 4.541,
     'L0_attn_Wo': 3.166,
     'L0_attn_lq_w': 5.447,
     'L0_attn_lk_w': 5.679,
     'L0_attn_lv_w': 3.334,
     'L0_ffn_b_fc': 8.0,
     'L0_ffn_b_proj': 8.0,
     'L1_attn_W_in': 5.963,
     'L1_attn_W_out': 5.861,
     'L1_attn_log_decay': 8.0,
     'L1_attn_frequencies': 8.0,
     'L1_ffn_Wr': 8.0,
     'L1_ffn_W1': 8.0,
     'L1_ffn_W2': 8.0,
     'L1_c': 4.931,
     'L1_wmod': 5.092}
    for name, (base, spread) in spreads.items():
        noise = np.random.default_rng([zlib.crc32(name.encode()), seed]).standard_normal(out[name].shape)
        drawn = base * np.exp(spread * noise) if base else spread * noise
        out[name] = jnp.asarray(drawn.astype(out[name].dtype))
    for name, factor in factors.items():
        out[name] = (out[name] * factor).astype(out[name].dtype)
    return out
```

```python
from contextlib import ExitStack

import numpy as np
import concourse.bass as bass
from concourse import mybir

F32 = mybir.dt.float32
BF16 = mybir.dt.bfloat16
I32 = mybir.dt.int32
U32 = mybir.dt.uint32
ALU = mybir.AluOpType
ACT = mybir.ActivationFunctionType
AX = mybir.AxisListType

P = 128
D = 128
N = 2048
NT = N // P
HEADS, HD = 16, 8
NE, HID = 8, 512
NB = HID // P
NF = 32
LN_EPS = 1e-5

W0 = 256


def _up(w):
    return int(np.float32(w) * np.float32(1.1))


def _down(w):
    return int(np.float32(w) * np.float32(0.9))


WINDOWS = [W0, _up(W0), _up(_up(W0))]
WMIN = _down(_down(W0))
NA = -(-WINDOWS[2] // P)
NATT = NA * P
MASKED = -1e30
RSQRT_MAGIC = float(0x5F3759DF)

def tiles_bound(rows):
    return (rows + NE * (P - 1)) // P


T0 = tiles_bound(2 * N)
T1 = tiles_bound(N)
RING = 4

SLOT = 8
STK = 64
Q_FIRST = {0: 1, 1: 4, 2: 6}
K_FIRST = {0: 1, 1: 2, 2: 3}
Q_COPIES = [(1, 2), (1, 3), (4, 5)]
K_COPIES = [(1, 4), (2, 5), (1, 6)]

ROW_C0, ROW_C1, ROW_BQ, ROW_BV, ROW_LNA, ROW_LNB, ROW_G, ROW_B, ROW_ROUTER = 0, 1, 2, 3, 4, 5, 6, 7, 8
NROW = ROW_ROUTER + NE
SA, CA, GA, SB, CB, GB = range(6)

TWO_PI = 2 * np.pi
TP1 = 6.28125
TP2 = float(np.float32(round((TWO_PI - TP1) * 2 ** 21) / 2 ** 21))
TP3 = float(np.float32(TWO_PI - TP1 - TP2))


def build_adaln(nc, A, out, rows0, rows1, back0, back1):
    ctx = ExitStack()
    with ctx:
        def sb(name, shape, dt=F32):
            return ctx.enter_context(nc.sbuf_tensor(name, shape, dt))

        sems = {}

        def sem(name):
            if name not in sems:
                sems[name] = ctx.enter_context(nc.semaphore(name))
            return sems[name]

        x = sb("x", [P, NT, D])
        xn = sb("xn", [P, NT, D])
        feat = sb("feat", [P, HEADS * NATT // 2])
        hT = feat[:, 0:N]
        y0 = sb("y0", [P, NT, D])
        wide = sb("wide", [P, 2 * NA * NATT])
        y1 = wide[:, 0:N].rearrange("p (j c) -> p j c", c=D)
        w_in = sb("w_in", [P, NE, HID])
        w_out = sb("w_out", [P, NE * NB, D])
        b_in = sb("b_in", [P, NE, HID])
        b_out = sb("b_out", [P, NE, D])
        ident = sb("ident", [P, P])
        identb = sb("identb", [P, P], BF16)
        ones = sb("ones", [P, P])
        onesb = sb("onesb", [P, P], BF16)
        zerob = sb("zerob", [P, P], BF16)
        before = sb("before", [P, P], BF16)
        zeros = sb("zeros", [P, 1024])
        rows = sb("rows", [NROW, P])
        cols = sb("cols", [P, NROW])
        wmod = sb("wmod", [P, 2, 6 * D])
        modrow = [sb(f"modrow{l}", [P, 6, D]) for l in range(2)]
        modcol = [sb(f"modcol{l}", [P, 6]) for l in range(2)]
        silu = sb("silu", [P, 3, 2])
        siluw = sb("siluw", [P, 2, P])
        gsign = sb("gsign", [P, 2, D])
        stats = sb("stats", [P, NT, 6])
        mv = sb("mv", [P, NT, 2])
        rstd = sb("rstd", [P, NT])
        rs_v = sb("rs_v", [P, 48])
        rs_a = sb("rs_a", [P, 48])
        rs_y = sb("rs_y", [P, 48])
        wnat = sb("wnat", [P, 4, D])
        wT = sb("wT", [P, 4, D])
        ln = sb("ln", [3 * HD, HD])
        lT = sb("lT", [HD, 3 * HD])
        pick = sb("pick", [HD, HEADS, HD])
        blockm = sb("blockm", [P, HEADS, HD])
        bd = sb("bd", [P, 3, HEADS, HD])
        small = sb("small", [P, 5, HD])
        scal = sb("scal", [P, 3])
        bo_row = sb("bo_row", [P, D])
        br_row = sb("br_row", [P, NE])
        ah = sb("ah", [P, NA, D])
        ahn = sb("ahn", [P, NA, D])
        n2T = sb("n2T", [P, NATT])
        qT = sb("qT", [P, NATT])
        kT = sb("kT", [P, NATT])
        vT = sb("vT", [P, NATT])
        gl_in = sb("gl_in", [P, NA * HEADS, HD])
        gl_c = sb("gl_c", [P, NA * HEADS, HD])
        gl_s = sb("gl_s", [P, NA * HEADS, HD])
        gl_m = sb("gl_m", [P, NA * HEADS])
        stack = sb("stack", [P, NA * HEADS, STK], BF16)
        qs = sb("qs", [P, HEADS // 2, NATT], BF16)
        ks = feat[:].bitcast(BF16).rearrange("p (h n) -> p h n", h=HEADS)
        vpx = sb("vpx", [P, NA, HEADS, HD + 1])
        probs = wide[:].rearrange("p (b j n) -> p b j n", b=2, j=NA)
        mx = sb("mx", [P, NA, HEADS])
        mr = sb("mr", [P, NA * HEADS])
        den = sb("den", [P, NA * HEADS])
        att = [sb(f"att{i}", [P, NA, D]) for i in range(3)]
        att_d = sb("att_d", [P, NA * D])
        asum = sb("asum", [P, 1])
        diff = sb("diff", [P, 2])
        flags = sb("flags", [P, 8])
        cw = sb("cw", [P, 3])
        tsc = sb("tsc", [P, 8])
        kidx_i = sb("kidx_i", [P, NATT], I32)
        kidx = sb("kidx", [P, NATT])
        ridx = sb("ridx", [P, NA])
        rowm = sb("rowm", [P, NA])
        lg = sb("lg", [P, NT, NE])
        lg2 = sb("lg2", [P, NT, NE])
        cand = sb("cand", [P, NT, NE])
        first = [sb(f"first{k}", [P, NT, NE]) for k in range(2)]
        top = sb("top", [P, 3, NT])
        gate = sb("gate", [P, 2, NT])
        chosen = sb("chosen", [P, NT, NE], BF16)
        e_rank = sb("e_rank", [P, NE])
        tot = sb("tot", [P, NE, NT])
        inc = sb("inc", [P, NE, NT])
        keep = sb("keep", [P, NE, NT])
        pose = sb("pose", [P, NT, NE])
        step128 = sb("step128", [P, NT])
        cmp_t = sb("cmp_t", [P, NE, NT])
        ntile = sb("ntile", [P, NE])
        tend = sb("tend", [P, NE])
        tbase = sb("tbase", [P, NE])
        posf = sb("posf", [P, NT])
        posu = sb("posu", [P, 2, NT], U32)
        tidx = sb("tidx", [P, 40])
        cmp_e = sb("cmp_e", [P, 40, NE])
        eidf = sb("eidf", [P, 40])
        eid = sb("eid", [P, 40], I32)
        xs = sb("xs", [P, RING, D])
        xsT = sb("xsT", [P, 2, P])
        hb = sb("hb", [P, 2, HID])
        hg = sb("hg", [P, 2, HID])
        ys = sb("ys", [P, RING, D])
        rotx = sb("rotx", [P, N + 1])
        roty = sb("roty", [P, N + 1])
        win_n = sb("win_n", [P, D])
        winT = sb("winT", [P, D])
        wo_s = sb("wo_s", [P, 2 * NF])
        wo_n = sb("wo_n", [P, 2, 4 * NF])
        wrl = sb("wrl", [P, NE])
        tmp_c = y0[:].rearrange("p j c -> p (j c)")[:, 0:N // 2]
        tmp_s = y0[:].rearrange("p j c -> p (j c)")[:, N // 2:N]
        turn = sb("turn", [P, 8])
        wox = sb("wox", [P, D])
        woy = sb("woy", [P, D])
        fcol = sb("fcol", [P, 2])
        ph = sb("ph", [P, 12])
        phi = sb("phi", [P, 4], I32)
        decay = sb("decay", [P, 2])

        ps = ctx.enter_context(nc.psum_tensor("ps", [P, 8, 512], F32))
        psb = ps[:].bitcast(BF16)

        block = ctx.enter_context(nc.Block())

        def load(eng, dst, src, what):
            eng.dma_start(dst, src).then_inc(sem("ld_" + what), 16)

        def col(ap):
            return ap.rearrange("(a n) -> a n", a=1)

        x_tiles = A["L0_attn_x"].rearrange("a (j p) c -> p (a j) c", p=P)
        out_tiles = out.rearrange("a (j p) c -> p (a j) c", p=P)
        NTILE = {0: T0, 1: T1}
        ROWS = {0: rows0, 1: rows1}
        BACK = {0: back0, 1: back1}

        def load_experts(eng, l):
            names = (("L0_ffn_w_fc", "L0_ffn_w_proj", "L0_ffn_b_fc", "L0_ffn_b_proj"),
                     ("L1_ffn_W1", "L1_ffn_W2", "L1_ffn_b1", "L1_ffn_b2"))[l]
            eng.dma_start(w_in[:], A[names[0]].rearrange("e c h -> c e h")).then_inc(sem(f"ld_experts{l}"), 16)
            eng.dma_start(w_out[:], A[names[1]].rearrange("e (b p) c -> p (e b) c", p=P)).then_inc(sem(f"ld_experts{l}"), 16)
            eng.dma_start(b_in[:], A[names[2]].partition_broadcast(P)).then_inc(sem(f"ld_experts{l}"), 16)
            eng.dma_start(b_out[:], A[names[3]].partition_broadcast(P)).then_inc(sem(f"ld_experts{l}"), 16)

        def clear_rows(eng, l):
            flat = ROWS[l].rearrange("(p r) c -> p (r c)", p=P)
            left, at = flat.shape[1], 0
            while left:
                n = min(left, 1024)
                eng.dma_start(flat[:, at:at + n], zeros[:, 0:n]).then_inc(sem(f"cleared{l}"), 16)
                at, left = at + n, left - n

        def clears(l):
            return -(-NTILE[l] * P // 1024)

        @block.sync
        def _(sp):
            load(sp, x[:, 0:NA, :], x_tiles[:, 0:NA, :], "x_attn")
            for r, a in ((ROW_C0, A["L0_c"]), (ROW_C1, A["L1_c"]), (ROW_BQ, col(A["L0_attn_bq"])),
                         (ROW_BV, col(A["L0_attn_bv"])), (ROW_LNA, col(A["L0_attn_lna_w"])),
                         (ROW_LNB, col(A["L0_attn_lnb_w"])), (ROW_G, col(A["L1_ffn_ln_g"])),
                         (ROW_B, col(A["L1_ffn_ln_b"]))):
                load(sp, rows[r:r + 1, :], a, "rows")
            load(sp, rows[ROW_ROUTER:NROW, :], A["L0_ffn_router_w"], "rows")
            load(sp, wmod[:, 0, :], A["L0_wmod"], "wmod")
            load(sp, wmod[:, 1, :], A["L1_wmod"], "wmod")
            for k, w in enumerate(("Wq", "Wk", "Wv", "Wo")):
                load(sp, wnat[:, k, :], A["L0_attn_" + w], "wnat")
            load(sp, x[:, NA:NT, :], x_tiles[:, NA:NT, :], "x_rest")
            sp.wait_ge(sem("zeros_set"), 1)
            clear_rows(sp, 0)
            clear_rows(sp, 1)
            load_experts(sp, 0)

            def sorted_tiles(l):
                T = NTILE[l]
                src = ROWS[l].rearrange("(t p) c -> p t c", p=P)
                dst = BACK[l].rearrange("(t p) c -> p t c", p=P)

                def load_tile(k, c):
                    sp.dma_start(xs[:, c % RING, :], src[:, bass.ds(RING * k + c, 1), :]).then_inc(
                        sem(f"xs_loaded{l}_{c % RING}"), 16)

                def store_tile(k, c):
                    sp.dma_start(dst[:, bass.ds(RING * k + c, 1), :], ys[:, c % RING, :]).then_inc(
                        sem(f"ys_stored{l}_{c % RING}"), 16)

                sp.wait_ge(sem(f"scattered{l}"), 16 * NT * (2 - l))
                for c in range(RING):
                    load_tile(0, c)
                whole = (T - RING) // RING
                with sp.Fori(0, whole) as k:
                    for c in range(RING):
                        sp.wait_ge(sem(f"xs_used{l}"), RING * k + (c + 1))
                        load_tile(k, c + RING)
                        sp.wait_ge(sem(f"ys_ready{l}"), RING * k + (c + 1))
                        store_tile(k, c)
                for t in range(RING * whole, T):
                    if t + RING < T:
                        sp.wait_ge(sem(f"xs_used{l}"), t + 1)
                        load_tile(0, t + RING)
                    sp.wait_ge(sem(f"ys_ready{l}"), t + 1)
                    store_tile(0, t)

            sorted_tiles(0)
            sp.wait_ge(sem("ys_ready0"), T0)
            load_experts(sp, 1)
            sorted_tiles(1)
            for j in range(4):
                sp.wait_ge(sem("x_final"), j + 1)
                s = slice(4 * j, 4 * j + 4)
                sp.dma_start(out_tiles[:, s, :], x[:, s, :]).then_inc(sem("stored"), 16)
            sp.wait_ge(sem("stored"), 64)

        @block.gpsimd
        def _(pool):
            pool.memset(zeros[:], 0.0).then_inc(sem("zeros_set"), 1)
            pool.memset(ident[:], 0.0).then_inc(sem("p_fill"), 1)
            pool.memset(ones[:], 1.0).then_inc(sem("p_fill"), 1)
            pool.memset(blockm[:], 1.0).then_inc(sem("p_fill"), 1)
            pool.memset(pick[:], 0.0).then_inc(sem("p_fill"), 1)
            pool.memset(keep[:], 1.0).then_inc(sem("p_fill"), 1)
            pool.memset(ks[:, :, :], 0.0).then_inc(sem("ks_zero"), 1)
            pool.wait_ge(sem("p_fill"), 5)
            pool.affine_select(out=ident[:], in_=ident[:], compare_op=ALU.not_equal, fill=1.0, base=0,
                               pattern=[[-1, P]], channel_multiplier=1).then_inc(sem("ident_set"), 1)
            pool.affine_select(out=pick[:], in_=pick[:], compare_op=ALU.not_equal, fill=1.0, base=0,
                               pattern=[[0, HEADS], [-1, HD]], channel_multiplier=1).then_inc(sem("pick_set"), 1)
            pool.affine_select(out=blockm[:], in_=blockm[:], compare_op=ALU.is_ge, fill=0.0, base=0,
                               pattern=[[-HD, HEADS], [0, HD]], channel_multiplier=1).then_inc(sem("p_block"), 1)
            pool.wait_ge(sem("p_block"), 1)
            pool.affine_select(out=blockm[:], in_=blockm[:], compare_op=ALU.is_ge, fill=0.0, base=HD - 1,
                               pattern=[[HD, HEADS], [0, HD]], channel_multiplier=-1).then_inc(sem("pick_set"), 1)
            pool.affine_select(out=before[:], in_=ones[:], compare_op=ALU.is_gt, fill=0.0, base=0,
                               pattern=[[1, P]], channel_multiplier=-1).then_inc(sem("tables_set"), 1)
            pool.affine_select(out=keep[:], in_=keep[:], compare_op=ALU.is_gt, fill=0.0, base=0,
                               pattern=[[0, NE], [1, NT]], channel_multiplier=0).then_inc(sem("tables_set"), 1)
            pool.iota(kidx_i[:], pattern=[[1, NATT]], base=0, channel_multiplier=0).then_inc(sem("kidx_set"), 1)
            exact = dict(allow_small_or_imprecise_dtypes=True)
            pool.iota(ridx[:], pattern=[[P, NA]], base=0, channel_multiplier=1, **exact).then_inc(sem("kidx_set"), 1)
            pool.iota(e_rank[:], pattern=[[-1, NE]], base=NE, channel_multiplier=0, **exact).then_inc(sem("tables_set"), 1)
            pool.iota(step128[:], pattern=[[P, NT]], base=0, channel_multiplier=0, **exact).then_inc(sem("tables_set"), 1)
            pool.iota(tidx[:], pattern=[[1, 40]], base=0, channel_multiplier=0, **exact).then_inc(sem("tables_set"), 1)

            for k, name in enumerate(("lq_b", "lk_b", "lv_b", "lnc_w", "lnd_w")):
                load(pool, small[:, k, :], A["L0_attn_" + name].partition_broadcast(P), "small")
            for k, name in enumerate(("threshold", "factor", "temp_base")):
                load(pool, scal[:, k:k + 1], A["L0_attn_" + name].partition_broadcast(P), "small")
            load(pool, bo_row[:], A["L0_attn_bo"].partition_broadcast(P), "small")
            load(pool, br_row[:], A["L1_ffn_br"].partition_broadcast(P), "small")
            for k, name in enumerate(("lq_w", "lk_w", "lv_w")):
                load(pool, ln[k * HD:(k + 1) * HD, :], A["L0_attn_" + name], "lmaps")

            def move_rows(l):
                K = 2 - l
                pool.wait_ge(sem(f"slots{l}"), 1)
                pool.wait_ge(sem(("rows_ready0f", "ffn_rows1")[l]), 1)
                pool.wait_ge(sem(f"cleared{l}"), 16 * clears(l))
                for j in range(NT):
                    for k in range(K):
                        pool.indirect_dma_start(ROWS[l], bass.IndirectOffsetOnAxis(ap=posu[:, k, j:j + 1], axis=0),
                                                xn[:, j, :], None).then_inc(sem(f"scattered{l}"), 16)
                for r in range(RING):
                    pool.wait_ge(sem(f"ys_stored{l}_{r}"), 16 * len(range(r, NTILE[l], RING)))
                for j in range(NT):
                    for k in range(K):
                        pool.indirect_dma_start((y0, y1)[k][:, j, :], None, BACK[l],
                                                bass.IndirectOffsetOnAxis(ap=posu[:, k, j:j + 1], axis=0)
                                                ).then_inc(sem(f"gathered{l}_{j // 4}"), 16)

            steps = [0]

            def then(ins):
                steps[0] += 1
                ins.then_inc(sem("p_step"), 1)
                pool.wait_ge(sem("p_step"), steps[0])

            H = P // 2
            pool.wait_ge(sem("tables_set"), 5)
            then(pool.memset(rotx[0:H, 0:1], 1.0))
            then(pool.memset(rotx[H:P, 0:1], 0.0))
            then(pool.memset(roty[0:H, 0:1], 0.0))
            then(pool.memset(roty[H:P, 0:1], -1.0))
            pool.wait_ge(sem("sines"), 1)
            then(pool.tensor_copy(turn[:, 0:1], ph[:, 7:8]))
            then(pool.tensor_copy(turn[:, 1:2], ph[:, 6:7]))
            c_, s_, cc, ss, t_ = (turn[:, k:k + 1] for k in range(5))

            def unit():
                then(pool.tensor_tensor(cc, c_, c_, ALU.mult))
                then(pool.tensor_tensor(ss, s_, s_, ALU.mult))
                then(pool.tensor_tensor(t_, cc, ss, ALU.add))
                then(pool.tensor_scalar(t_, t_, -0.5, 1.5, ALU.mult, ALU.add))
                then(pool.tensor_tensor(c_, c_, t_, ALU.mult))
                then(pool.tensor_tensor(s_, s_, t_, ALU.mult))

            unit()
            L = 1
            while L <= N:
                n = min(L, N + 1 - L)
                X, Y, tc, ts = rotx[:, 0:n], roty[:, 0:n], tmp_c[:, 0:n], tmp_s[:, 0:n]
                pool.tensor_scalar(tc, X, c_, None, ALU.mult)
                then(pool.tensor_scalar(ts, Y, s_, None, ALU.mult))
                then(pool.tensor_tensor(rotx[:, L:L + n], tc, ts, ALU.subtract))
                pool.tensor_scalar(tc, X, s_, None, ALU.mult)
                then(pool.tensor_scalar(ts, Y, c_, None, ALU.mult))
                ins = pool.tensor_tensor(roty[:, L:L + n], tc, ts, ALU.add)
                L *= 2
                if L > N:
                    ins.then_inc(sem("rotations"), 1)
                    break
                then(ins)
                then(pool.tensor_tensor(cc, c_, c_, ALU.mult))
                then(pool.tensor_tensor(ss, s_, s_, ALU.mult))
                then(pool.tensor_tensor(t_, c_, s_, ALU.mult))
                then(pool.tensor_tensor(c_, cc, ss, ALU.subtract))
                then(pool.tensor_tensor(s_, t_, t_, ALU.add))
                unit()
            pool.wait_ge(sem("rotations"), 1)
            move_rows(0)
            move_rows(1)

        @block.scalar
        def _(act):
            for f in range(4):
                load(act, fcol[f * NF:(f + 1) * NF, 0:1], A["L1_attn_frequencies"].rearrange("(n a) -> n a", a=1), "recur")
                load(act, fcol[f * NF:(f + 1) * NF, 1:2], A["L1_attn_log_decay"].rearrange("(n a) -> n a", a=1), "recur")
            for f, r in enumerate((0, 1, 1, 0)):
                load(act, win_n[f * NF:(f + 1) * NF, :], A["L1_attn_W_in"][r * NF:(r + 1) * NF, :], "recur")
            load(act, wo_s[:], A["L1_attn_W_out"], "recur")
            load(act, wrl[:], A["L1_ffn_Wr"], "router1")

            act.wait_ge(sem("angles"), 1)
            act.activation(ph[:, 6:8], ph[:, 4:6], ACT.Sin).then_inc(sem("sines"), 1)
            act.wait_ge(sem("cols_set"), 1)
            act.activation(silu[:, 0, :], cols[:, 0:2], ACT.Exp, scale=-1.0).then_inc(sem("silu_exp"), 1)
            act.activation(decay[:, 0:1], fcol[:, 1:2], ACT.Exp, scale=-1.0).then_inc(sem("decay_exp"), 1)

            def softmax_exp(it):
                nj, nw = -(-WINDOWS[it] // P), WINDOWS[it]
                with act.Fori(0, HEADS // 2) as i:
                    for b in range(2):
                        act.wait_ge(sem("st_ready"), 2 * i + (HEADS * it + b + 1))
                        act.wait_ge(sem("probs_free"), 2 * i + (HEADS * it + b + 1))
                        act.activation(probs[:, b, 0:nj, 0:nw], ps[:, 3 * b:3 * b + nj, 0:nw], ACT.Exp
                                       ).then_inc(sem("probs_ready"), 1)

            def stack_copies(n):
                for g in range(2, 4):
                    act.wait_ge(sem("stackT"), 4 * n + g + 1)
                    act.copy(qs[:, 2 * g:2 * g + 2, :], psb[:, g, 0:2 * NATT].rearrange("p (a n) -> p a n", a=2)
                             ).then_inc(sem("qs_act"), 1)

            for it in range(3):
                stack_copies(2 * it)
                stack_copies(2 * it + 1)
                softmax_exp(it)

            def turned(l, stage, scale, bias):
                for g in range(NT // 4):
                    act.wait_ge(sem(f"turned{l}{stage}"), g + 1)
                    kw = {} if scale is None else dict(scale=scale, bias=bias)
                    act.activation(hT[:, 512 * g:512 * g + 512], ps[:, g % 2, :], ACT.Identity, **kw
                                   ).then_inc(sem(f"hT{l}{stage}"), 1)

            def experts(l):
                T = NTILE[l]
                fn = (ACT.Gelu_apprx_tanh, ACT.Relu)[l]
                sc, bi = ((modcol[0][:, CB:CB + 1], modcol[0][:, SB:SB + 1]),
                          (cols[:, ROW_G:ROW_G + 1], cols[:, ROW_B:ROW_B + 1]))[l]

                def modulate(k, c):
                    act.wait_ge(sem(f"xs_used{l}"), RING * k + (c + 1))
                    if not isinstance(k, int) or k * RING + c >= 2:
                        act.wait_ge(sem(f"h_ready{l}"), RING * k + (c - 1))
                    act.activation(xsT[:, c % 2, :], ps[:, 4 + c % 2, 0:P], ACT.Identity, scale=sc, bias=bi
                                   ).then_inc(sem(f"xsT_ready{l}"), 1)

                def nonlinear(k, c):
                    act.wait_ge(sem(f"hT_ready{l}"), RING * k + (c + 1))
                    if not isinstance(k, int) or k * RING + c >= 2:
                        act.wait_ge(sem(f"o_ready{l}"), RING * k + (c - 1))
                    act.activation(hg[:, c % 2, :], ps[:, 2 + c % 2, :], fn).then_inc(sem(f"hg_ready{l}"), 1)

                modulate(0, 0)
                modulate(0, 1)
                nonlinear(0, 0)
                modulate(0, 2)
                nonlinear(0, 1)
                modulate(0, 3)
                nloop = (T - 4) // RING
                with act.Fori(0, nloop) as k:
                    for c in range(2, 2 + RING):
                        nonlinear(k, c)
                        modulate(k, c + 2)
                for t in range(RING * nloop + 2, T):
                    nonlinear(0, t)
                    if t + 2 < T:
                        modulate(0, t + 2)

            turned(0, "f", modcol[0][:, CB:CB + 1], modcol[0][:, SB:SB + 1])
            act.wait_ge(sem("top_gap"), 1)
            act.activation(top[:, 2, :], top[:, 2, :], ACT.Exp).then_inc(sem("gap_exp"), 1)
            experts(0)
            turned(1, "a", modcol[1][:, CA:CA + 1], modcol[1][:, SA:SA + 1])
            turned(1, "f", None, None)
            act.wait_ge(sem("lg_shifted"), 1)
            act.activation(lg2[:], lg2[:], ACT.Exp).then_inc(sem("lg_exp"), 1)
            experts(1)

        @block.tensor
        def _(pe):
            pe.wait_ge(sem("ident_set"), 1)
            pe.wait_ge(sem("ld_rows"), 16 * 9)
            pe.transpose(ps[:, 0, 0:NROW], rows[:], ident[0:NROW, 0:NROW]).then_inc(sem("t_cols"), 1)
            pe.wait_ge(sem("ld_wnat"), 64)
            for k in range(4):
                mm = pe.transpose(ps[:, 1, k * D:(k + 1) * D], wnat[:, k, :], ident[:])
            mm.then_inc(sem("t_wT"), 1)
            pe.wait_ge(sem("ld_lmaps"), 48)
            pe.transpose(ps[0:HD, 2, 64:64 + 3 * HD], ln[:], ident[0:3 * HD, 0:3 * HD]).then_inc(sem("t_lT"), 1)
            pe.wait_ge(sem("pick_set"), 2)
            pe.wait_ge(sem("lT_set"), 1)
            pe.matmul(ps[:, 2, 0:3 * HD], pick[:], lT[:], start=True, stop=True).then_inc(sem("t_bd"), 1)
            pe.wait_ge(sem("ld_wmod"), 32)
            pe.wait_ge(sem("silu_set"), 1)
            for l in range(2):
                if l:
                    pe.wait_ge(sem("mod_read"), 2)
                pe.matmul(ps[:, 3, :], siluw[:, l, :], wmod[:, l, 0:512], start=True, stop=True)
                pe.matmul(ps[:, 4, 0:256], siluw[:, l, :], wmod[:, l, 512:768], start=True, stop=True)
                for c in range(6):
                    mm = pe.matmul(ps[:, 5, c:c + 1], wmod[:, l, c * D:(c + 1) * D], silu[:, 2, l:l + 1],
                                   start=True, stop=True)
                mm.then_inc(sem("mod_made"), 1)
            pe.wait_ge(sem("recur_rows"), 1)
            pe.transpose(ps[:, 6, 0:D], win_n[:], ident[:])
            pe.transpose(ps[:, 6, D:2 * D], wo_n[:, 0, :], ident[:])
            pe.transpose(ps[:, 6, 2 * D:3 * D], wo_n[:, 1, :], ident[:]).then_inc(sem("t_recur"), 1)

            pe.wait_ge(sem("n2"), 1)
            for j in range(NA):
                mm = pe.transpose(ps[:, 0, j * P:(j + 1) * P], ahn[:, j, :], ident[:])
            mm.then_inc(sem("t_n2"), 1)
            pe.wait_ge(sem("n2T"), 1)
            pe.wait_ge(sem("wT_set"), 1)
            for k, bank in enumerate((1, 2, 3)):
                pe.matmul(ps[:, bank, 0:NATT], wT[:, k, :], n2T[:], start=True, stop=True).then_inc(sem("qkv"), 1)

            def heads_map(k, srcT, bank, when, value, done):
                pe.wait_ge(sem(when), value)
                for j in range(NA):
                    mm = pe.matmul(ps[:, bank, j * D:(j + 1) * D], srcT[:, j * P:(j + 1) * P],
                                   bd[:, k, :, :].rearrange("p h o -> p (h o)"), start=True, stop=True)
                mm.then_inc(sem(done), 1)

            heads_map(1, kT, 4, "kT", 1, "kp")
            heads_map(2, vT, 5, "vT", 1, "vp")

            def turn_stack(name):
                for g in range(4):
                    for a in range(2):
                        for j in range(NA):
                            pr = 2 * g + a
                            mm = pe.transpose(psb[:, g, a * NATT + j * P:a * NATT + (j + 1) * P],
                                              stack[:, j * HEADS + 2 * pr:j * HEADS + 2 * pr + 2, :].rearrange("p h s -> p (h s)"),
                                              identb[:])
                    mm.then_inc(sem(name), 1)

            pe.wait_ge(sem("k_stack"), 1)
            turn_stack("kstackT")

            def attend(it):
                nj, nw = -(-WINDOWS[it] // P), WINDOWS[it]
                heads_map(0, qT, 7, "qT", it + 1, "qp")
                pe.wait_ge(sem("q_stack"), 2 * it + 1)
                turn_stack("stackT")
                pe.wait_ge(sem("qs_vec"), 2 * (2 * it + 1))
                pe.wait_ge(sem("qs_act"), 2 * (2 * it + 1))
                pe.wait_ge(sem("ks_set"), it + 1)
                with pe.Fori(0, HEADS // 2) as i:
                    for b in range(2):
                        pe.wait_ge(sem("max_free"), 2 * i + (HEADS * it + b + 1))
                        for j in range(nj):
                            mm = pe.matmul(ps[:, 3 * b + j, 0:nw], qs[:, bass.ds(i, 1), j * P:(j + 1) * P],
                                           ks[:, bass.ds(2 * i + b, 1), 0:nw], start=True, stop=True)
                        mm.then_inc(sem("s_ready"), 1)
                pe.wait_ge(sem("q_stack"), 2 * it + 2)
                turn_stack("stackT")
                pe.wait_ge(sem("qs_vec"), 2 * (2 * it + 2))
                pe.wait_ge(sem("qs_act"), 2 * (2 * it + 2))
                pe.matmul(ps[:, 6, 0:NA * HEADS * (HD + 1)], zerob[:], qs[:, 0:2, :].rearrange("p a n -> p (a n)")[:, 0:NA * HEADS * (HD + 1)],
                          start=True, stop=True)

                def scores_t(i, b):
                    pe.wait_ge(sem("probs_ready"), 2 * i + (HEADS * it + b - 1)) if not (isinstance(i, int) and HEADS * it + 2 * i + b < 2) else None
                    for j in range(nj):
                        mm = pe.matmul(ps[:, 3 * b + j, 0:nw], ks[:, bass.ds(2 * i + b, 1), j * P:(j + 1) * P],
                                       qs[:, bass.ds(i, 1), 0:nw], start=True, stop=True)
                    mm.then_inc(sem("st_ready"), 1)

                def weigh(i, b):
                    pe.wait_ge(sem("probs_ready"), 2 * i + (HEADS * it + b + 1))
                    for jq in range(nj):
                        m = min(P, nw - jq * P)
                        for jk in range(nj):
                            mm = pe.matmul(ps[0:m, 6, bass.ds((2 * i + b) * (HD + 1) + jq * HEADS * (HD + 1), HD + 1)],
                                           probs[:, b, jk, jq * P:jq * P + m], vpx[:, jk, bass.ds(2 * i + b, 1), :],
                                           start=(jk == 0), stop=(jk == nj - 1))
                    mm.then_inc(sem("probs_free"), 1)

                scores_t(0, 0)
                scores_t(0, 1)
                with pe.Fori(0, HEADS // 2 - 1) as i:
                    weigh(i, 0)
                    scores_t(i + 1, 0)
                    weigh(i, 1)
                    scores_t(i + 1, 1)
                weigh(HEADS // 2 - 1, 0)
                weigh(HEADS // 2 - 1, 1)
                if it < 2:
                    pe.wait_ge(sem("asum"), it + 1)
                    pe.matmul(ps[:, 7, 0:1], ones[:], asum[:], start=True, stop=True).then_inc(sem("change"), 1)
                    for j in range(NA):
                        mm = pe.transpose(ps[:, 5, j * P:(j + 1) * P], att[it][:, j, :], ident[:])
                    mm.then_inc(sem("attT"), 1)

            for it in range(3):
                attend(it)
            pe.wait_ge(sem("att_final"), 1)
            for j in range(NA):
                mm = pe.transpose(ps[:, 5, j * P:(j + 1) * P], att[2][:, j, :], ident[:])
            mm.then_inc(sem("attT"), 1)
            pe.wait_ge(sem("attT_copied"), 1)
            for j in range(NA):
                mm = pe.matmul(ps[:, 7, j * D:(j + 1) * D], kT[:, j * P:(j + 1) * P], wT[:, 3, :], start=True, stop=True)
            mm.then_inc(sem("att_out"), 1)

            def turn_rows(l, stage, src, value):
                for g in range(NT // 4):
                    pe.wait_ge(sem(f"rows_ready{l}{stage}"), value(g))
                    if g >= 2:
                        pe.wait_ge(sem(f"hT{l}{stage}"), g - 1)
                    for j in range(4):
                        mm = pe.transpose(ps[:, g % 2, j * P:(j + 1) * P], src[:, 4 * g + j, :], ident[:])
                    mm.then_inc(sem(f"turned{l}{stage}"), 1)

            def route(l):
                for g in range(NT // 4):
                    pe.wait_ge(sem(f"hT{l}f"), g + 1)
                    for j in range(4 * g, 4 * g + 4):
                        rhs = cols[:, ROW_ROUTER:NROW] if l == 0 else wrl[:]
                        mm = pe.matmul(ps[:, 2, j * NE:(j + 1) * NE], hT[:, j * P:(j + 1) * P], rhs, start=True, stop=True)
                mm.then_inc(sem(f"logits{l}"), 1)
                pe.wait_ge(sem(f"chosen{l}"), 1)
                ch = chosen[:].rearrange("p j e -> p (j e)")
                pe.matmul(ps[:, 3, 0:NT * NE], before[:], ch, start=True, stop=True)
                pe.matmul(ps[:, 4, 0:NT * NE], onesb[:], ch, start=True, stop=True).then_inc(sem(f"counts{l}"), 1)

            def experts(l):
                T = NTILE[l]
                regs = [pe.alloc_register(f"pe_expert{l}_{c}") for c in range(2 * RING - 1)]

                def ids(k, c, n):
                    pe.reg_load(regs[0:n], eid[0:1, bass.ds(RING * k + c, n)])
                    return [pe.snap(r, min_val=0, max_val=NE - 1) for r in regs[0:n]]

                def turn_x(k, c):
                    pe.wait_ge(sem(f"xs_loaded{l}_{c % RING}"), 16 * (k + (c // RING + 1)))
                    pe.transpose(ps[:, 4 + c % 2, 0:P], xs[:, c % RING, :], ident[:]).then_inc(sem(f"xs_used{l}"), 1)

                def up(k, c, e):
                    pe.wait_ge(sem(f"xsT_ready{l}"), RING * k + (c + 1))
                    pe.matmul(ps[:, c % 2, :], xsT[:, c % 2, :], w_in[:, bass.ds(e, 1), :], start=True, stop=True
                              ).then_inc(sem(f"h_ready{l}"), 1)

                def down(k, c, e):
                    pe.wait_ge(sem(f"hg_ready{l}"), RING * k + (c + 1))
                    if not isinstance(k, int) or RING * k + c >= 2:
                        pe.wait_ge(sem(f"ys_ready{l}"), RING * k + (c - 1))
                    for n in range(NB):
                        mm = pe.matmul(ps[:, 6 + c % 2, 0:D], hg[:, c % 2, n * P:(n + 1) * P],
                                       w_out[:, bass.ds(e * NB + n, 1), :], start=(n == 0), stop=(n == NB - 1))
                    mm.then_inc(sem(f"o_ready{l}"), 1)

                def turn_h(k, c):
                    pe.wait_ge(sem(f"hb_ready{l}"), RING * k + (c + 1))
                    for n in range(NB):
                        mm = pe.transpose(ps[:, 2 + c % 2, n * P:(n + 1) * P], hb[:, c % 2, n * P:(n + 1) * P], ident[:])
                    mm.then_inc(sem(f"hT_ready{l}"), 1)

                pe.wait_ge(sem(f"ld_experts{l}"), 64)
                pe.wait_ge(sem(f"slots{l}"), 1)
                def slot(k, c, e, last):
                    up(k, c, e[1])
                    down(k, c - 1, e[0])
                    turn_h(k, c)
                    if not last:
                        turn_x(k, c + 2)

                turn_x(0, 0)
                turn_x(0, 1)
                e = ids(0, 0, 2)
                up(0, 0, e[0])
                turn_h(0, 0)
                turn_x(0, 2)
                slot(0, 1, e, False)
                nloop = (T - 4) // RING
                with pe.Fori(0, nloop) as k:
                    e = ids(k, 1, RING + 1)
                    for c in range(RING):
                        slot(k, c + 2, e[c:c + 2], False)
                n = T - RING * nloop
                e = ids(nloop, 1, n - 1)
                for c in range(2, n):
                    slot(nloop, c, e[c - 2:c], c + 2 >= n)
                down(nloop, n - 1, e[n - 2])

            turn_rows(0, "f", xn, lambda g: 1)
            route(0)
            experts(0)
            turn_rows(1, "a", xn, lambda g: 1)
            for g in range(4):
                pe.wait_ge(sem("hT1a"), g + 1)
                pe.matmul(ps[:, 2 + g, :], winT[:], hT[:, 512 * g:512 * g + 512], start=True, stop=True
                          ).then_inc(sem("modes_in"), 1)
            pe.wait_ge(sem("rotated_back"), 2)
            for g in range(4):
                for j in range(4):
                    t = 4 * g + j
                    pe.matmul(ps[:, 2 + g, j * D:(j + 1) * D], y0[:].rearrange("p j c -> p (j c)")[:, t * P:(t + 1) * P], wox[:], start=True, stop=False)
                    mm = pe.matmul(ps[:, 2 + g, j * D:(j + 1) * D], xn[:].rearrange("p j c -> p (j c)")[:, t * P:(t + 1) * P], woy[:], start=False, stop=True)
                mm.then_inc(sem("modes_out"), 1)
            turn_rows(1, "f", y0, lambda g: 1)
            pe.wait_ge(sem("ld_router1"), 16)
            route(1)
            experts(1)

        @block.vector
        def _(v):
            steps = [0]

            def then(ins):
                steps[0] += 1
                ins.then_inc(sem("v_step"), 1)
                v.wait_ge(sem("v_step"), steps[0])

            def signal(ins, name, value):
                ins.then_inc(sem(name), 1)
                v.wait_ge(sem(name), value)

            def rsqrt(src, dst, n):
                yv, a = rs_y[:, 0:n], rs_a[:, 0:n]
                then(v.tensor_scalar(yv.bitcast(I32), src.bitcast(I32), -0.5, RSQRT_MAGIC, ALU.mult, ALU.add))
                for k in range(3):
                    then(v.scalar_tensor_tensor(out=a, in0=yv, scalar=-0.5, in1=yv, op0=ALU.mult, op1=ALU.mult))
                    then(v.tensor_tensor(a, a, src, ALU.mult))
                    then(v.scalar_tensor_tensor(out=dst if k == 2 else yv, in0=a, scalar=1.5, in1=yv, op0=ALU.add, op1=ALU.mult))

            def layernorm(src, dst, lo, hi, done=None):
                for j in range(lo, hi):
                    ins = v.bn_stats(stats[:, j, :], src[:, j, :])
                then(ins)
                for j in range(lo, hi):
                    ins = v.bn_aggr(mv[:, j, :], stats[:, j, :])
                then(ins)
                then(v.tensor_scalar(rs_v[:, 0:hi - lo], mv[:, lo:hi, 1], LN_EPS, None, ALU.add))
                rsqrt(rs_v[:, 0:hi - lo], rstd[:, lo:hi], hi - lo)
                for j in range(lo, hi):
                    ins = v.tensor_scalar(dst[:, j, :], src[:, j, :], mv[:, j, 0:1], rstd[:, j:j + 1], ALU.subtract, ALU.mult)
                if done:
                    signal(ins, done, 1)
                else:
                    then(ins)

            def rowwise(ap, n):
                return ap.unsqueeze(1).to_broadcast([P, n, D])

            then(v.memset(onesb[:], 1.0))
            then(v.memset(zerob[:], 0.0))
            v.wait_ge(sem("ident_set"), 1)
            then(v.tensor_copy(identb[:], ident[:]))
            v.wait_ge(sem("kidx_set"), 2)
            then(v.tensor_copy(kidx[:], kidx_i[:]))
            v.wait_ge(sem("ld_recur"), 16 * 13)
            then(v.tensor_scalar(ph[:, 0:1], fcol[:, 0:1], float(np.float32(0.1)), None, ALU.mult))
            then(v.tensor_scalar(ph[:, 1:2], ph[:, 0:1], float(np.pi / 2), None, ALU.add))
            then(v.tensor_scalar(phi[:, 0:2], ph[:, 0:2], float(1 / TWO_PI), None, ALU.mult))
            then(v.tensor_copy(ph[:, 2:4], phi[:, 0:2]))
            then(v.scalar_tensor_tensor(out=ph[:, 4:6], in0=ph[:, 2:4], scalar=-TP1, in1=ph[:, 0:2], op0=ALU.mult, op1=ALU.add))
            then(v.scalar_tensor_tensor(out=ph[:, 4:6], in0=ph[:, 2:4], scalar=-TP2, in1=ph[:, 4:6], op0=ALU.mult, op1=ALU.add))
            then(v.scalar_tensor_tensor(out=ph[:, 4:6], in0=ph[:, 2:4], scalar=-TP3, in1=ph[:, 4:6], op0=ALU.mult, op1=ALU.add))
            lim = 3.1415925
            signal(v.tensor_scalar(ph[:, 4:6], ph[:, 4:6], lim, -lim, ALU.min, ALU.max), "angles", 1)
            then(v.tensor_scalar(win_n[96:128, :], win_n[96:128, :], -1.0, None, ALU.mult))
            wr, wi = wo_s[:, 0:NF], wo_s[:, NF:2 * NF]
            for a, parts in enumerate((((wr, 1.0), (wi, 1.0), (wi, 1.0), (wr, -1.0)),
                                       ((wi, 1.0), (wr, -1.0), (wr, -1.0), (wi, -1.0)))):
                for q, (src, sign) in enumerate(parts):
                    ins = v.tensor_scalar(wo_n[:, a, q * NF:(q + 1) * NF], src, sign, None, ALU.mult)
            ins.then_inc(sem("recur_rows"), 1)
            v.wait_ge(sem("t_cols"), 1)
            signal(v.tensor_copy(cols[:], ps[:, 0, 0:NROW]), "cols_set", 1)
            v.wait_ge(sem("silu_exp"), 1)
            then(v.tensor_scalar(silu[:, 1, :], silu[:, 0, :], 1.0, None, ALU.add))
            then(v.reciprocal(silu[:, 1, :], silu[:, 1, :]))
            then(v.tensor_tensor(silu[:, 2, :], silu[:, 1, :], cols[:, 0:2], ALU.mult))
            for l in range(2):
                ins = v.tensor_scalar(siluw[:, l, :], ones[:], silu[:, 2, l:l + 1], None, ALU.mult)
            ins.then_inc(sem("silu_set"), 1)
            v.wait_ge(sem("t_wT"), 1)
            v.tensor_scalar(wT[:, 0, :], ps[:, 1, 0:D], cols[:, ROW_LNA:ROW_LNA + 1], None, ALU.mult)
            for k in (1, 2):
                v.tensor_scalar(wT[:, k, :], ps[:, 1, k * D:(k + 1) * D], cols[:, ROW_LNB:ROW_LNB + 1], None, ALU.mult)
            signal(v.tensor_copy(wT[:, 3, :], ps[:, 1, 3 * D:4 * D]), "wT_set", 1)
            v.wait_ge(sem("t_lT"), 1)
            v.tensor_copy(lT[:], ps[0:HD, 2, 64:64 + 3 * HD]).then_inc(sem("lT_set"), 1)
            v.wait_ge(sem("t_bd"), 1)
            for k in range(3):
                ins = v.tensor_tensor(bd[:, k, :, :], blockm[:], ps[:, 2, k * HD:(k + 1) * HD].unsqueeze(1).to_broadcast([P, HEADS, HD]), ALU.mult)
            then(ins)
            for l in range(2):
                v.wait_ge(sem("mod_made"), l + 1)
                mr_f = modrow[l][:].rearrange("p a c -> p (a c)")
                v.tensor_copy(mr_f[:, 0:512], ps[:, 3, :])
                signal(v.tensor_copy(mr_f[:, 512:768], ps[:, 4, 0:256]), "mod_read", 2 * l + 1)
                signal(v.tensor_copy(modcol[l][:], ps[:, 5, 0:6]), "mod_read", 2 * l + 2)
                for c in (CA, CB):
                    v.tensor_scalar(modrow[l][:, c, :], modrow[l][:, c, :], 1.0, None, ALU.add)
                    v.tensor_scalar(modcol[l][:, c:c + 1], modcol[l][:, c:c + 1], 1.0, None, ALU.add)
                g = modrow[l][:, GA:GB + 1:GB - GA, :]
                then(v.tensor_scalar(gsign[:], g, 0.0, 2.0, ALU.is_ge, ALU.mult))
                then(v.tensor_scalar(gsign[:], gsign[:], -1.0, None, ALU.add))
                then(v.scalar_tensor_tensor(out=g, in0=g, scalar=-1.0, in1=g, op0=ALU.mult, op1=ALU.max))
                then(v.scalar_tensor_tensor(out=g, in0=g, scalar=0.25, in1=gsign[:], op0=ALU.max, op1=ALU.mult))

            v.wait_ge(sem("t_recur"), 1)
            v.tensor_copy(winT[:], ps[:, 6, 0:D])
            v.tensor_copy(wox[:], ps[:, 6, D:2 * D])
            then(v.tensor_copy(woy[:], ps[:, 6, 2 * D:3 * D]))
            v.wait_ge(sem("decay_exp"), 1)
            then(v.tensor_scalar(decay[:, 1:2], decay[:, 0:1], 1.0, None, ALU.add))
            then(v.reciprocal(decay[:, 1:2], decay[:, 1:2]))

            v.wait_ge(sem("ld_x_attn"), 16)
            layernorm(x, xn, 0, NA)
            then(v.tensor_tensor(ah[:], xn[:, 0:NA, :], rowwise(modrow[0][:, CA, :], NA), ALU.mult))
            then(v.tensor_tensor(ah[:], ah[:], rowwise(modrow[0][:, SA, :], NA), ALU.add))
            layernorm(ah, ahn, 0, NA, "n2")
            v.wait_ge(sem("t_n2"), 1)
            signal(v.tensor_copy(n2T[:], ps[:, 0, 0:NATT]), "n2T", 1)
            sc = float(HD ** -0.25)
            v.wait_ge(sem("qkv"), 1)
            signal(v.tensor_scalar(qT[:], ps[:, 1, 0:NATT], cols[:, ROW_BQ:ROW_BQ + 1], sc, ALU.add, ALU.mult), "qT", 1)
            v.wait_ge(sem("qkv"), 2)
            signal(v.tensor_scalar(kT[:], ps[:, 2, 0:NATT], sc, None, ALU.mult), "kT", 1)
            v.wait_ge(sem("qkv"), 3)
            signal(v.tensor_scalar(vT[:], ps[:, 3, 0:NATT], cols[:, ROW_BV:ROW_BV + 1], None, ALU.add), "vT", 1)
            v.wait_ge(sem("ld_small"), 16 * 10)

            def grouped(t, nj):
                return t[:, 0:nj * HEADS, :]

            def each(ap8, nj):
                return ap8.unsqueeze(1).to_broadcast([P, nj * HEADS, HD])

            def per(ap, nj):
                return ap[:, 0:nj * HEADS].unsqueeze(2).to_broadcast([P, nj * HEADS, HD])

            def head_norm(bank, bias, weight, nj, tscale=None):
                gi, gc, gs = grouped(gl_in, nj), grouped(gl_c, nj), grouped(gl_s, nj)
                n = nj * HEADS
                then(v.tensor_tensor(gi, ps[:, bank, 0:n * HD].rearrange("p (g o) -> p g o", o=HD), each(small[:, bias, :], nj), ALU.add))
                then(v.tensor_reduce(gl_m[:, 0:n], gi, AX.X, ALU.add))
                then(v.tensor_scalar(gl_m[:, 0:n], gl_m[:, 0:n], 1.0 / HD, None, ALU.mult))
                then(v.tensor_tensor(gc, gi, per(gl_m, nj), ALU.subtract))
                then(v.tensor_tensor(gs, gc, gc, ALU.mult))
                then(v.tensor_reduce(rs_v[:, 0:n], gs, AX.X, ALU.add))
                then(v.tensor_scalar(rs_v[:, 0:n], rs_v[:, 0:n], 1.0 / HD, LN_EPS, ALU.mult, ALU.add))
                rsqrt(rs_v[:, 0:n], gl_m[:, 0:n], n)
                if tscale is not None:
                    then(v.tensor_scalar(gl_m[:, 0:n], gl_m[:, 0:n], tscale, float(np.float32(1 / np.sqrt(HD))), ALU.mult, ALU.mult))
                then(v.tensor_tensor(gc, gc, per(gl_m, nj), ALU.mult))
                then(v.tensor_tensor(gc, gc, each(small[:, weight, :], nj), ALU.mult))

            def slot(s, nj):
                return stack[:, 0:nj * HEADS, s * SLOT:(s + 1) * SLOT]

            def split(nj, firsts, copies):
                gc, r1 = grouped(gl_c, nj), grouped(gl_s, nj)
                then(v.tensor_copy(slot(firsts[0], nj), gc))
                then(v.tensor_tensor(r1, gc, slot(firsts[0], nj), ALU.subtract))
                then(v.tensor_copy(slot(firsts[1], nj), r1))
                then(v.tensor_tensor(r1, r1, slot(firsts[1], nj), ALU.subtract))
                then(v.tensor_copy(slot(firsts[2], nj), r1))
                for a, b in copies:
                    ins = v.tensor_copy(slot(b, nj), slot(a, nj))
                return ins

            then(v.memset(stack[:], 0.0))
            then(v.memset(stack[:, :, 1:4], -1.0))
            v.wait_ge(sem("kp"), 1)
            head_norm(4, 1, 4, NA)
            signal(split(NA, K_FIRST, K_COPIES), "k_stack", 1)
            v.wait_ge(sem("vp"), 1)
            then(v.memset(vpx[:], 1.0))
            then(v.tensor_tensor(vpx[:, :, :, 0:HD].rearrange("p j h o -> p (j h) o"), ps[:, 5, 0:NATT].rearrange("p (g o) -> p g o", o=HD), each(small[:, 2, :], NA), ALU.add))
            v.wait_ge(sem("ks_zero"), 1)
            for g in range(4):
                v.wait_ge(sem("kstackT"), g + 1)
                src = psb[:, g, 0:2 * NATT].rearrange("p (a n) -> p a n", a=2)
                v.tensor_copy(ks[0:STK, 4 * g:4 * g + 4:2, :], src[0:STK])
                ins = v.tensor_copy(ks[STK:P, 4 * g + 1:4 * g + 4:2, :], src[STK:P])
            signal(ins, "ks_set", 1)
            then(v.memset(stack[:], 0.0))
            then(v.memset(stack[:, :, 0:1], 1.0))
            v.memset(cw[:, 0:1], float(W0))
            then(v.memset(att[0][:], 0.0))
            ins = v.memset(mx[:], 0.0)
            ins.then_inc(sem("max_free"), 2)
            ins = v.memset(flags[:], 0.0)
            ins.then_inc(sem("probs_free"), 2)
            v.wait_ge(sem("max_free"), 2)
            v.wait_ge(sem("probs_free"), 2)
            then(v.tensor_copy(tsc[:, 0:1], scal[:, 2:3]))
            then(v.tensor_scalar(tsc[:, 1:2], tsc[:, 0:1], 0.005, None, ALU.add))
            then(v.tensor_scalar(tsc[:, 2:3], tsc[:, 1:2], 0.005, None, ALU.add))
            then(v.tensor_scalar(rs_v[:, 0:3], tsc[:, 0:3], 1e-37, None, ALU.max))
            rsqrt(rs_v[:, 0:3], tsc[:, 3:6], 3)
            then(v.tensor_scalar(rs_v[:, 0:3], tsc[:, 0:3], 0.0, None, ALU.is_gt))
            then(v.tensor_scalar(tsc[:, 3:6], tsc[:, 3:6], -1.0, None, ALU.add))
            then(v.tensor_tensor(tsc[:, 3:6], tsc[:, 3:6], rs_v[:, 0:3], ALU.mult))
            then(v.tensor_scalar(tsc[:, 3:6], tsc[:, 3:6], 1.0, None, ALU.add))

            def stack_copies(n):
                for g in range(2):
                    v.wait_ge(sem("stackT"), 4 * n + g + 1)
                    v.tensor_copy(qs[:, 2 * g:2 * g + 2, :], psb[:, g, 0:2 * NATT].rearrange("p (a n) -> p a n", a=2)
                                  ).then_inc(sem("qs_vec"), 1)

            up_, dn_, conv_ = 0, 2, 4

            def attend(it):
                nj, nw = -(-WINDOWS[it] // P), WINDOWS[it]
                n = nj * HEADS
                if it:
                    for p0, h0 in ((0, 0), (STK, 1)):
                        ins = v.tensor_scalar(ks[p0:p0 + 1, h0::2, WMIN:NATT], kidx[p0:p0 + 1, WMIN:NATT].unsqueeze(1).to_broadcast([1, HEADS // 2, NATT - WMIN]),
                                              cw[p0:p0 + 1, it:it + 1], MASKED, ALU.is_ge, ALU.mult)
                    signal(ins, "ks_set", it + 1)
                then(v.tensor_scalar(rowm[:], ridx[:], cw[:, it:it + 1], None, ALU.is_lt))
                v.wait_ge(sem("qp"), it + 1)
                head_norm(7, 0, 3, nj, tsc[:, 3 + it:4 + it])
                if it:
                    then(v.memset(stack[:, :, 1:4], 0.0))
                signal(split(nj, Q_FIRST, Q_COPIES), "q_stack", 2 * it + 1)
                stack_copies(2 * it)
                with v.Fori(0, HEADS // 2) as i:
                    for b in range(2):
                        v.wait_ge(sem("s_ready"), 2 * i + (HEADS * it + b + 1))
                        v.tensor_reduce(mx[:, 0:nj, bass.ds(2 * i + b, 1)], ps[:, 3 * b:3 * b + nj, 0:nw], AX.X, ALU.max
                                        ).then_inc(sem("max_free"), 1)
                v.wait_ge(sem("max_free"), 2 + HEADS * (it + 1))
                m, r = mx[:, 0:nj, :].rearrange("p j h -> p (j h)"), mr[:, 0:n]
                for k in range(3):
                    dst = stack[:, 0:n, 1 + k]
                    src = m if k == 0 else r
                    ins = v.tensor_copy(dst, src)
                    if k < 2:
                        then(ins)
                        then(v.tensor_tensor(r, src, dst, ALU.subtract))
                signal(ins, "q_stack", 2 * it + 2)
                stack_copies(2 * it + 1)
                v.wait_ge(sem("probs_free"), 2 + HEADS * (it + 1))
                o = ps[:, 6, 0:NA * HEADS * (HD + 1)].rearrange("p (g o) -> p g o", o=HD + 1)[:, 0:n, :]
                then(v.tensor_scalar(den[:, 0:n], o[:, :, HD], 0.5, None, ALU.max))
                then(v.reciprocal(den[:, 0:n], den[:, 0:n]))
                a3 = att[it][:].rearrange("p j (h o) -> p (j h) o", o=HD)[:, 0:n, :]
                then(v.tensor_tensor(a3, o[:, :, 0:HD], per(den, nj), ALU.mult))
                then(v.tensor_tensor(att[it][:, 0:nj, :], att[it][:, 0:nj, :], rowm[:, 0:nj].unsqueeze(2).to_broadcast([P, nj, D]), ALU.mult))
                if it == 2:
                    return
                af = att[it][:].rearrange("p j c -> p (j c)")
                if it:
                    then(v.tensor_tensor(att_d[:], af, att[it - 1][:].rearrange("p j c -> p (j c)"), ALU.subtract))
                    af = att_d[:]
                signal(v.tensor_reduce(asum[:], af, AX.X, ALU.add, apply_absolute_value=True), "asum", it + 1)
                v.wait_ge(sem("change"), it + 1)
                df = diff[:, it:it + 1]
                then(v.tensor_scalar(df, ps[:, 7, 0:1], 1.0 / (N * D), None, ALU.mult))
                up, dn = flags[:, up_ + it:up_ + it + 1], flags[:, dn_ + it:dn_ + it + 1]
                v.tensor_scalar(up, df, 0.05, None, ALU.is_gt)
                then(v.tensor_scalar(dn, df, 0.001, None, ALU.is_lt))
                nxt = cw[:, it + 1:it + 2]
                if it == 0:
                    then(v.tensor_scalar(nxt, up, float(_up(W0) - W0), float(W0), ALU.mult, ALU.add))
                    then(v.scalar_tensor_tensor(out=nxt, in0=dn, scalar=float(_down(W0) - W0), in1=nxt, op0=ALU.mult, op1=ALU.add))
                else:
                    def change(f, dst):
                        base, a, b = f(W0) - W0, f(_up(W0)) - _up(W0), f(_down(W0)) - _down(W0)
                        then(v.tensor_scalar(dst, flags[:, up_:up_ + 1], float(a - base), float(base), ALU.mult, ALU.add))
                        then(v.scalar_tensor_tensor(out=dst, in0=flags[:, dn_:dn_ + 1], scalar=float(b - base), in1=dst, op0=ALU.mult, op1=ALU.add))
                    change(_up, tsc[:, 6:7])
                    change(_down, tsc[:, 7:8])
                    then(v.scalar_tensor_tensor(out=nxt, in0=tsc[:, 6:7], scalar=up, in1=cw[:, it:it + 1], op0=ALU.mult, op1=ALU.add))
                    then(v.scalar_tensor_tensor(out=nxt, in0=tsc[:, 7:8], scalar=dn, in1=nxt, op0=ALU.mult, op1=ALU.add))
                    then(v.scalar_tensor_tensor(out=tsc[:, 6:7], in0=df, scalar=scal[:, 1:2], in1=scal[:, 0:1], op0=ALU.mult, op1=ALU.add))
                    then(v.tensor_tensor(flags[:, conv_:conv_ + 1], df, tsc[:, 6:7], ALU.is_lt))
                    then(v.tensor_scalar(flags[:, conv_ + 1:conv_ + 2], flags[:, conv_:conv_ + 1], -1.0, 1.0, ALU.mult, ALU.add))
                v.wait_ge(sem("attT"), it + 1)
                signal(v.tensor_tensor(qT[:], qT[:], ps[:, 5, 0:NATT], ALU.add), "qT", it + 2)

            for it in range(3):
                attend(it)
            then(v.tensor_scalar(att[1][:], att[1][:], flags[:, conv_:conv_ + 1], None, ALU.mult))
            signal(v.scalar_tensor_tensor(out=att[2][:], in0=att[2][:], scalar=flags[:, conv_ + 1:conv_ + 2], in1=att[1][:], op0=ALU.mult, op1=ALU.add), "att_final", 1)
            v.wait_ge(sem("attT"), 3)
            signal(v.tensor_copy(kT[:], ps[:, 5, 0:NATT]), "attT_copied", 1)
            v.wait_ge(sem("ld_x_rest"), 16)
            v.wait_ge(sem("att_out"), 1)
            then(v.tensor_tensor(ah[:], ps[:, 7, 0:NATT].rearrange("p (j c) -> p j c", c=D), rowwise(bo_row[:], NA), ALU.add))
            then(v.tensor_tensor(ah[:], ah[:], rowwise(modrow[0][:, GA, :], NA), ALU.mult))
            then(v.tensor_tensor(x[:, 0:NA, :], x[:, 0:NA, :], ah[:], ALU.add))
            then(v.tensor_tensor(ahn[:, 0, :], bo_row[:], modrow[0][:, GA, :], ALU.mult))
            then(v.tensor_tensor(x[:, NA:NT, :], x[:, NA:NT, :], rowwise(ahn[:, 0, :], NT - NA), ALU.add))

            def lowest(lgt, m, dst):
                bc = lambda t: t.unsqueeze(2).to_broadcast([P, NT, NE])
                then(v.tensor_reduce(m, lgt, AX.X, ALU.max))
                then(v.tensor_tensor(cand[:], lgt, bc(m), ALU.is_equal))
                then(v.tensor_tensor(cand[:], cand[:], e_rank[:].unsqueeze(1).to_broadcast([P, NT, NE]), ALU.mult))
                then(v.tensor_reduce(posf[:], cand[:], AX.X, ALU.max))
                then(v.tensor_tensor(dst, cand[:], bc(posf[:]), ALU.is_equal))

            def route(l):
                v.wait_ge(sem(f"logits{l}"), 1)
                pl = ps[:, 2, 0:NT * NE].rearrange("p (j e) -> p j e", e=NE)
                if l == 0:
                    v.wait_ge(sem("tables_set"), 5)
                    then(v.tensor_copy(lg[:], pl))
                else:
                    then(v.tensor_tensor(lg[:], pl, br_row[:].unsqueeze(1).to_broadcast([P, NT, NE]), ALU.add))
                lowest(lg[:], top[:, 0, :], first[0][:])
                if l == 0:
                    then(v.scalar_tensor_tensor(out=lg2[:], in0=first[0][:], scalar=-3e38, in1=lg[:], op0=ALU.mult, op1=ALU.add))
                    lowest(lg2[:], top[:, 1, :], first[1][:])
                    signal(v.tensor_tensor(chosen[:], first[0][:], first[1][:], ALU.add), "chosen0", 1)
                    signal(v.tensor_tensor(top[:, 2, :], top[:, 1, :], top[:, 0, :], ALU.subtract), "top_gap", 1)
                else:
                    signal(v.tensor_copy(chosen[:], first[0][:]), "chosen1", 1)
                    signal(v.tensor_tensor(lg2[:], lg[:], top[:, 0, :].unsqueeze(2).to_broadcast([P, NT, NE]), ALU.subtract), "lg_shifted", 1)
                v.wait_ge(sem(f"counts{l}"), 1)
                then(v.tensor_copy(tot[:], ps[:, 4, 0:NT * NE].rearrange("p (j e) -> p e j", e=NE)))
                fl = lambda t: t[:].rearrange("p e j -> p (e j)")
                then(v.tensor_tensor_scan(fl(inc), fl(keep), fl(tot), 0.0, ALU.mult, ALU.add))
                then(v.tensor_tensor(cmp_t[:], inc[:, :, NT - 1:NT].to_broadcast([P, NE, NT]), step128[:].unsqueeze(1).to_broadcast([P, NE, NT]), ALU.is_gt))
                then(v.tensor_reduce(ntile[:], cmp_t[:], AX.X, ALU.add))
                then(v.tensor_tensor_scan(tend[:], ones[:, 0:NE], ntile[:], 0.0, ALU.mult, ALU.add))
                then(v.tensor_tensor(tbase[:], tend[:], ntile[:], ALU.subtract))
                then(v.tensor_scalar(tbase[:], tbase[:], float(P), None, ALU.mult))
                then(v.tensor_tensor(inc[:], inc[:], tot[:], ALU.subtract))
                then(v.tensor_tensor(inc[:], inc[:], tbase[:].unsqueeze(2).to_broadcast([P, NE, NT]), ALU.add))
                then(v.tensor_tensor(pose[:], ps[:, 3, 0:NT * NE].rearrange("p (j e) -> p j e", e=NE), inc[:].rearrange("p e j -> p j e"), ALU.add))
                T = NTILE[l]
                then(v.tensor_tensor(cmp_e[:, 0:T, :], tidx[:, 0:T].unsqueeze(2).to_broadcast([P, T, NE]), tend[:].unsqueeze(1).to_broadcast([P, T, NE]), ALU.is_ge))
                then(v.tensor_reduce(eidf[:, 0:T], cmp_e[:, 0:T, :], AX.X, ALU.add))
                then(v.tensor_scalar(eid[:, 0:T], eidf[:, 0:T], float(NE - 1), None, ALU.min))
                for k in range(2 - l):
                    then(v.tensor_tensor(cand[:], pose[:], first[k][:], ALU.mult))
                    then(v.tensor_reduce(posf[:], cand[:], AX.X, ALU.add))
                    ins = v.tensor_copy(posu[:, k, :], posf[:])
                    if k < 1 - l:
                        then(ins)
                signal(ins, f"slots{l}", 1)
                if l == 0:
                    v.wait_ge(sem("gap_exp"), 1)
                    then(v.tensor_scalar(gate[:, 1, :], top[:, 2, :], 1.0, None, ALU.add))
                    then(v.reciprocal(gate[:, 0, :], gate[:, 1, :]))
                    then(v.tensor_tensor(gate[:, 1, :], top[:, 2, :], gate[:, 0, :], ALU.mult))
                else:
                    v.wait_ge(sem("lg_exp"), 1)
                    then(v.tensor_reduce(posf[:], lg2[:], AX.X, ALU.add))
                    then(v.reciprocal(gate[:, 0, :], posf[:]))

            def experts(l):
                T = NTILE[l]
                regs = [v.alloc_register(f"v_expert{l}_{c}") for c in range(RING + 1)]

                def ids(k, n):
                    v.reg_load(regs[0:n], eid[0:1, bass.ds(RING * k, n)])
                    return [v.snap(r, min_val=0, max_val=NE - 1) for r in regs[0:n]]

                def bias_up(k, c, e):
                    if not isinstance(k, int) or RING * k + c >= 2:
                        v.wait_ge(sem(f"hT_ready{l}"), RING * k + (c - 1))
                    v.wait_ge(sem(f"h_ready{l}"), RING * k + (c + 1))
                    v.tensor_tensor(hb[:, c % 2, :], ps[:, c % 2, :], b_in[:, bass.ds(e, 1), :], ALU.add
                                    ).then_inc(sem(f"hb_ready{l}"), 1)

                def bias_down(k, c, e):
                    if not isinstance(k, int) or k > 0:
                        v.wait_ge(sem(f"ys_stored{l}_{c % RING}"), 16 * k)
                    v.wait_ge(sem(f"o_ready{l}"), RING * k + (c + 1))
                    v.tensor_tensor(ys[:, c % RING, :], ps[:, 6 + c % 2, 0:D], b_out[:, bass.ds(e, 1), :], ALU.add
                                    ).then_inc(sem(f"ys_ready{l}"), 1)

                v.wait_ge(sem(f"ld_experts{l}"), 64)
                e = ids(0, 1)
                bias_up(0, 0, e[0])
                e = ids(0, RING)
                for c in range(1, RING):
                    bias_up(0, c, e[c])
                    bias_down(0, c - 1, e[c - 1])
                nloop = (T - RING) // RING
                with v.Fori(0, nloop) as k0:
                    k = k0 + 1
                    v.reg_load(regs[0:RING + 1], eid[0:1, bass.ds(RING * k - 1, RING + 1)])
                    e = [v.snap(r, min_val=0, max_val=NE - 1) for r in regs]
                    bias_up(k, 0, e[1])
                    bias_down(k0, RING - 1, e[0])
                    for c in range(1, RING):
                        bias_up(k, c, e[c + 1])
                        bias_down(k, c - 1, e[c])
                base = RING * (nloop + 1)
                n = T - base
                v.reg_load(regs[0:n + 1], eid[0:1, bass.ds(base - 1, n + 1)])
                e = [v.snap(r, min_val=0, max_val=NE - 1) for r in regs[0:n + 1]]
                for c in range(n):
                    bias_up(nloop + 1, c, e[c + 1])
                    if c == 0:
                        bias_down(nloop, RING - 1, e[0])
                    else:
                        bias_down(nloop + 1, c - 1, e[c])
                bias_down(nloop + 1, n - 1, e[n])

            def add_ffn(l):
                for q in range(4):
                    s = slice(4 * q, 4 * q + 4)
                    v.wait_ge(sem(f"gathered{l}_{q}"), 16 * 4 * (2 - l))
                    for j in range(4 * q, 4 * q + 4):
                        ins = v.tensor_scalar(y0[:, j, :], y0[:, j, :], gate[:, 0, j:j + 1], None, ALU.mult)
                    then(ins)
                    if l == 0:
                        for j in range(4 * q, 4 * q + 4):
                            ins = v.scalar_tensor_tensor(out=y0[:, j, :], in0=y1[:, j, :], scalar=gate[:, 1, j:j + 1], in1=y0[:, j, :], op0=ALU.mult, op1=ALU.add)
                        then(ins)
                    then(v.tensor_tensor(y0[:, s, :], y0[:, s, :], rowwise(modrow[l][:, GB, :], 4), ALU.mult))
                    ins = v.tensor_tensor(x[:, s, :], x[:, s, :], y0[:, s, :], ALU.add)
                    if l:
                        signal(ins, "x_final", q + 1)
                    else:
                        then(ins)

            layernorm(x, xn, 0, NT, "rows_ready0f")
            route(0)
            experts(0)

            add_ffn(0)
            layernorm(x, xn, 0, NT, "rows_ready1a")
            v.wait_ge(sem("rotations"), 1)
            flat = lambda t: t[:, :, :].rearrange("p j c -> p (j c)")
            for g in range(4):
                s = slice(512 * g, 512 * g + 512)
                v.wait_ge(sem("modes_in"), g + 1)
                ins = v.tensor_tensor(flat(y0)[:, s], ps[:, 2 + g, :], rotx[:, s], ALU.mult)
            then(ins)
            then(v.tensor_tensor_scan(flat(y1), decay[:, 1:2].to_broadcast([P, N]), flat(y0), 0.0, ALU.mult, ALU.add))
            v.tensor_tensor(flat(y0), flat(y1), rotx[:, 1:N + 1], ALU.mult).then_inc(sem("rotated_back"), 1)
            signal(v.tensor_tensor(flat(xn), flat(y1), roty[:, 1:N + 1], ALU.mult), "rotated_back", 2)
            for g in range(4):
                s = slice(4 * g, 4 * g + 4)
                v.wait_ge(sem("modes_out"), g + 1)
                then(v.tensor_tensor(y1[:, s, :], ps[:, 2 + g, :].rearrange("p (j c) -> p j c", c=D), rowwise(modrow[1][:, GA, :], 4), ALU.mult))
                then(v.tensor_tensor(x[:, s, :], x[:, s, :], y1[:, s, :], ALU.add))
            layernorm(x, xn, 0, NT)
            then(v.tensor_tensor(y0[:], xn[:], rowwise(modrow[1][:, CB, :], NT), ALU.mult))
            signal(v.tensor_tensor(y0[:], y0[:], rowwise(modrow[1][:, SB, :], NT), ALU.add), "rows_ready1f", 1)
            layernorm(y0, xn, 0, NT, "ffn_rows1")
            route(1)
            experts(1)
            add_ffn(1)


_OUT = ("out", (1, N, D))
_SCRATCH = (("rows0", (T0 * P, D)), ("rows1", (T1 * P, D)), ("back0", (T0 * P, D)), ("back1", (T1 * P, D)))


def kernel(**inputs):
    import concourse.bacc as bacc
    from concourse.bass_utils import run_bass_kernel_spmd

    nc = bacc.Bacc("TRN2", target_bir_lowering=False, num_devices=1)
    arrays, aps = {}, {}
    for name, value in inputs.items():
        a = np.ascontiguousarray(value)
        if a.ndim == 0:
            a = a.reshape(1)
        arrays["in_" + name] = a
        aps[name] = nc.dram_tensor("in_" + name, a.shape, mybir.dt.from_np(a.dtype), kind="ExternalInput").ap()
    out = nc.dram_tensor(_OUT[0], _OUT[1], F32, kind="ExternalOutput").ap()
    scratch = [nc.dram_tensor(name, shape, F32, kind="Internal").ap() for name, shape in _SCRATCH]
    build_adaln(nc, aps, out, *scratch)
    r = run_bass_kernel_spmd(nc, [arrays], core_ids=[0])
    return r.results[0][_OUT[0]]
```

```python
from contextlib import ExitStack

import numpy as np
import concourse.bass as bass
from concourse import mybir

F32 = mybir.dt.float32
BF16 = mybir.dt.bfloat16
I32 = mybir.dt.int32
U32 = mybir.dt.uint32
ALU = mybir.AluOpType
ACT = mybir.ActivationFunctionType
AX = mybir.AxisListType

P = 128
D = 128
N = 2048
NT = N // P
HEADS, HD = 16, 8
NE, HID = 8, 512
NB = HID // P
NF = 32
LN_EPS = 1e-5

W0 = 256


def _up(w):
    return int(np.float32(w) * np.float32(1.1))


def _down(w):
    return int(np.float32(w) * np.float32(0.9))


WINDOWS = [W0, _up(W0), _up(_up(W0))]
WMIN = _down(_down(W0))
NA = -(-WINDOWS[2] // P)
NATT = NA * P
MASKED = -1e30
RSQRT_MAGIC = float(0x5F3759DF)

def tiles_bound(rows):
    return (rows + NE * (P - 1)) // P


GROUPS = {"far": (NA, NT, 2), "near": (0, NA, 2), "all": (0, NT, 1)}
TFAR = tiles_bound(2 * (N - NATT))
TNEAR = tiles_bound(2 * NATT)
T0 = TFAR + TNEAR
T1 = tiles_bound(N)
SORTED = {"far": (0, TFAR), "near": (TFAR, T0), "all": (0, T1)}
TMAX = 48
CHUNKS = {"far": [(a, min(a + 4, NT)) for a in range(NA, NT, 4)], "near": [(0, NA)],
          "all": [(a, a + 4) for a in range(0, NT, 4)]}
RING = 4

SLOT = 8
STK = 64
OROW = 32
Q_FIRST = {0: 1, 1: 4, 2: 6}
K_FIRST = {0: 1, 1: 2, 2: 3}
Q_COPIES = [(1, 2), (1, 3), (4, 5)]
K_COPIES = [(1, 4), (2, 5), (1, 6)]

ROW_C0, ROW_C1, ROW_BQ, ROW_BV, ROW_LNA, ROW_LNB, ROW_G, ROW_B, ROW_ROUTER = 0, 1, 2, 3, 4, 5, 6, 7, 8
NROW = ROW_ROUTER + NE
SA, CA, GA, SB, CB, GB = range(6)

TWO_PI = 2 * np.pi
TP1 = 6.28125
TP2 = float(np.float32(round((TWO_PI - TP1) * 2 ** 21) / 2 ** 21))
TP3 = float(np.float32(TWO_PI - TP1 - TP2))


def build_adaln(nc, A, out, rows0, rows1, back0, back1):
    ctx = ExitStack()
    with ctx:
        def sb(name, shape, dt=F32):
            return ctx.enter_context(nc.sbuf_tensor(name, shape, dt))

        sems = {}

        def sem(name):
            if name not in sems:
                sems[name] = ctx.enter_context(nc.semaphore(name))
            return sems[name]

        x = sb("x", [P, NT, D])
        xn = sb("xn", [P, NT, D])
        feat = sb("feat", [P, HEADS * NATT // 2])
        hT = feat[:, 0:N]
        y0 = sb("y0", [P, NT, D])
        wide = sb("wide", [P, 2 * NA * NATT])
        y1 = wide[:, 0:N].rearrange("p (j c) -> p j c", c=D)
        w_in = sb("w_in", [P, NE, HID])
        w_out = sb("w_out", [P, NE * NB, D])
        b_in = sb("b_in", [P, NE, HID])
        b_out = sb("b_out", [P, NE, D])
        ident = sb("ident", [P, P])
        identb = sb("identb", [P, P], BF16)
        ones = sb("ones", [P, P])
        onesb = sb("onesb", [P, P], BF16)
        before = sb("before", [P, P], BF16)
        zeros = sb("zeros", [P, 512])
        rows = sb("rows", [NROW, P])
        cols = sb("cols", [P, NROW])
        wmod = sb("wmod", [P, 2, 6 * D])
        modrow = [sb(f"modrow{l}", [P, 6, D]) for l in range(2)]
        modcol = [sb(f"modcol{l}", [P, 6]) for l in range(2)]
        silu = sb("silu", [P, 3, 2])
        siluw = sb("siluw", [P, 2, P])
        gsign = sb("gsign", [P, 2, D])
        stats = sb("stats", [P, NT, 6])
        mv = sb("mv", [P, NT, 2])
        rstd = sb("rstd", [P, NT])
        rs_v = sb("rs_v", [P, 48])
        rs_a = sb("rs_a", [P, 48])
        rs_y = sb("rs_y", [P, 48])
        wnat = sb("wnat", [P, 4, D])
        wT = sb("wT", [P, 4, D])
        ln = sb("ln", [3 * HD, HD])
        lT = sb("lT", [HD, 3 * HD])
        pick = sb("pick", [HD, HEADS, HD])
        blockm = sb("blockm", [P, HEADS, HD])
        bd = sb("bd", [P, 3, HEADS, HD])
        small = sb("small", [P, 5, HD])
        scal = sb("scal", [P, 3])
        bo_row = sb("bo_row", [P, D])
        br_row = sb("br_row", [P, NE])
        ah = sb("ah", [P, NA, D])
        ahn = sb("ahn", [P, NA, D])
        n2T = sb("n2T", [P, NATT])
        qT = sb("qT", [P, NATT])
        kT = sb("kT", [P, NATT])
        vT = sb("vT", [P, NATT])
        gl_in = sb("gl_in", [P, NA * HEADS, HD])
        gl_c = sb("gl_c", [P, NA * HEADS, HD])
        gl_s = sb("gl_s", [P, NA * HEADS, HD])
        gl_m = sb("gl_m", [P, NA * HEADS])
        stack = sb("stack", [P, NA * HEADS, STK], BF16)
        qs = sb("qs", [P, HEADS // 2, NATT], BF16)
        ks = feat[:].bitcast(BF16).rearrange("p (h n) -> p h n", h=HEADS)
        vpx = sb("vpx", [P, NA, HEADS, HD + 1])
        probs = wide[:].rearrange("p (b j n) -> p b j n", b=2, j=NA)
        v_now = sb("v_now", [P, 4, NA, OROW])
        oT = wmod[:].rearrange("p l c -> p (l c)").rearrange("p (g n) -> p g n", g=HEADS // 4)
        mx = sb("mx", [P, NA, HEADS])
        mr = sb("mr", [P, NA * HEADS])
        den = sb("den", [P, NA * HEADS])
        att = [sb(f"att{i}", [P, NA, D]) for i in range(3)]
        att_d = sb("att_d", [P, NA * D])
        asum = sb("asum", [P, 1])
        diff = sb("diff", [P, 2])
        flags = sb("flags", [P, 8])
        cw = sb("cw", [P, 3])
        tsc = sb("tsc", [P, 8])
        kidx_i = sb("kidx_i", [P, NATT], I32)
        kidx = sb("kidx", [P, NATT])
        ridx = sb("ridx", [P, NA])
        rowm = sb("rowm", [P, NA])
        lg = sb("lg", [P, NT, NE])
        lg2 = sb("lg2", [P, NT, NE])
        cand = sb("cand", [P, NT, NE])
        first = [sb(f"first{k}", [P, NT, NE]) for k in range(2)]
        top = sb("top", [P, 3, NT])
        gate = sb("gate", [P, 2, NT])
        chosen = sb("chosen", [P, NT, NE], BF16)
        e_rank = sb("e_rank", [P, NE])
        tot_f = sb("tot", [P, NE * NT])
        inc_f = sb("inc", [P, NE * NT])
        keep = {g: sb(f"keep_{g}", [P, NE, hi - lo]) for g, (lo, hi, _) in GROUPS.items()}
        pose = sb("pose", [P, NT, NE])
        step128 = sb("step128", [P, NT])
        cmp_f = sb("cmp_t", [P, NE * NT])
        ntile = sb("ntile", [P, NE])
        tend = sb("tend", [P, NE])
        tbase = sb("tbase", [P, NE])
        posf = sb("posf", [P, NT])
        posu = sb("posu", [P, 2, NT], U32)
        tidx = sb("tidx", [P, TMAX])
        cmp_e = sb("cmp_e", [P, TMAX, NE])
        eidf = sb("eidf", [P, TMAX])
        eid = sb("eid", [P, TMAX], I32)
        xs = sb("xs", [P, RING, D])
        xsT = sb("xsT", [P, 2, P])
        hb = sb("hb", [P, 2, HID])
        hTr = hb
        hg = sb("hg", [P, 2, HID])
        ys = sb("ys", [P, RING, D])
        rotx = sb("rotx", [P, N + 1])
        roty = sb("roty", [P, N + 1])
        win_n = sb("win_n", [P, D])
        winT = sb("winT", [P, D])
        wo_s = sb("wo_s", [P, 2 * NF])
        wo_n = sb("wo_n", [P, 2, 4 * NF])
        wrl = sb("wrl", [P, NE])
        tmp_c = y0[:].rearrange("p j c -> p (j c)")[:, 0:N // 2]
        tmp_s = y0[:].rearrange("p j c -> p (j c)")[:, N // 2:N]
        turn = sb("turn", [P, 8])
        wox = sb("wox", [P, D])
        woy = sb("woy", [P, D])
        fcol = sb("fcol", [P, 2])
        ph = sb("ph", [P, 12])
        phi = sb("phi", [P, 4], I32)
        decay = sb("decay", [P, 2])

        ps = ctx.enter_context(nc.psum_tensor("ps", [P, 8, 512], F32))
        psb = ps[:].bitcast(BF16)

        block = ctx.enter_context(nc.Block())

        def load(eng, dst, src, what):
            eng.dma_start(dst, src).then_inc(sem("ld_" + what), 16)

        def col(ap):
            return ap.rearrange("(a n) -> a n", a=1)

        x_tiles = A["L0_attn_x"].rearrange("a (j p) c -> p (a j) c", p=P)
        out_tiles = out.rearrange("a (j p) c -> p (a j) c", p=P)
        NTILE = {0: T0, 1: T1}
        ROWS = {0: rows0, 1: rows1}

        def earlier(l, r):
            return len(range(r, T0, RING)) if l else 0

        BACK = {0: back0, 1: back1}

        def load_experts(eng, l):
            names = (("L0_ffn_w_fc", "L0_ffn_w_proj", "L0_ffn_b_fc", "L0_ffn_b_proj"),
                     ("L1_ffn_W1", "L1_ffn_W2", "L1_ffn_b1", "L1_ffn_b2"))[l]
            eng.dma_start(w_in[:], A[names[0]].rearrange("e c h -> c e h")).then_inc(sem(f"ld_experts{l}"), 16)
            eng.dma_start(w_out[:], A[names[1]].rearrange("e (b p) c -> p (e b) c", p=P)).then_inc(sem(f"ld_experts{l}"), 16)
            eng.dma_start(b_in[:], A[names[2]].partition_broadcast(P)).then_inc(sem(f"ld_experts{l}"), 16)
            eng.dma_start(b_out[:], A[names[3]].partition_broadcast(P)).then_inc(sem(f"ld_experts{l}"), 16)

        def clear_rows(eng, l):
            flat = ROWS[l].rearrange("(p r) c -> p (r c)", p=P)
            left, at = flat.shape[1], 0
            while left:
                n = min(left, 512)
                eng.dma_start(flat[:, at:at + n], zeros[:, 0:n]).then_inc(sem(f"cleared{l}"), 16)
                at, left = at + n, left - n

        def clears(l):
            return -(-NTILE[l] * P // 512)

        @block.sync
        def _(sp):
            load(sp, x[:, 0:NA, :], x_tiles[:, 0:NA, :], "x_attn")
            for r, a in ((ROW_C0, A["L0_c"]), (ROW_C1, A["L1_c"]), (ROW_BQ, col(A["L0_attn_bq"])),
                         (ROW_BV, col(A["L0_attn_bv"])), (ROW_LNA, col(A["L0_attn_lna_w"])),
                         (ROW_LNB, col(A["L0_attn_lnb_w"])), (ROW_G, col(A["L1_ffn_ln_g"])),
                         (ROW_B, col(A["L1_ffn_ln_b"]))):
                load(sp, rows[r:r + 1, :], a, "rows")
            load(sp, rows[ROW_ROUTER:NROW, :], A["L0_ffn_router_w"], "rows")
            load(sp, wmod[:, 0, :], A["L0_wmod"], "wmod0")
            for k, w in enumerate(("Wq", "Wk", "Wv", "Wo")):
                load(sp, wnat[:, k, :], A["L0_attn_" + w], "wnat")
            for f in range(4):
                load(sp, fcol[f * NF:(f + 1) * NF, 0:1], A["L1_attn_frequencies"].rearrange("(n a) -> n a", a=1), "recur")
                load(sp, fcol[f * NF:(f + 1) * NF, 1:2], A["L1_attn_log_decay"].rearrange("(n a) -> n a", a=1), "recur")
            for f, r in enumerate((0, 1, 1, 0)):
                load(sp, win_n[f * NF:(f + 1) * NF, :], A["L1_attn_W_in"][r * NF:(r + 1) * NF, :], "recur")
            load(sp, wo_s[:], A["L1_attn_W_out"], "recur")
            load(sp, wrl[:], A["L1_ffn_Wr"], "router1")
            load(sp, wmod[:, 1, :], A["L1_wmod"], "wmod1")
            load(sp, x[:, NA:NT, :], x_tiles[:, NA:NT, :], "x_rest")
            sp.wait_ge(sem("zeros_set"), 1)
            clear_rows(sp, 0)
            clear_rows(sp, 1)
            load_experts(sp, 0)

            def sorted_tiles(l):
                T = NTILE[l]
                src = ROWS[l].rearrange("(t p) c -> p t c", p=P)
                dst = BACK[l].rearrange("(t p) c -> p t c", p=P)

                def load_tile(k, c):
                    sp.dma_start(xs[:, c % RING, :], src[:, bass.ds(RING * k + c, 1), :]).then_inc(
                        sem(f"xs_loaded{c % RING}"), 16)

                def store_tile(k, c):
                    sp.dma_start(dst[:, bass.ds(RING * k + c, 1), :], ys[:, c % RING, :]).then_inc(
                        sem(f"ys_stored{c % RING}"), 16)

                def rounds(lo, hi):
                    with sp.Fori(lo, hi) as k:
                        for c in range(RING):
                            sp.wait_ge(sem(f"xs_used{l}"), RING * k + (c + 1))
                            load_tile(k, c + RING)
                            sp.wait_ge(sem(f"ys_ready{l}"), RING * k + (c + 1))
                            store_tile(k, c)

                def wait_scattered(g):
                    lo, hi, experts = GROUPS[g]
                    sp.wait_ge(sem("scattered_" + g), 16 * (hi - lo) * experts)

                wait_scattered(("far", "all")[l])
                for c in range(RING):
                    load_tile(0, c)
                whole = (T - RING) // RING
                if l == 0:
                    turn = (TFAR - RING) // RING
                    rounds(0, turn)
                    wait_scattered("near")
                    rounds(turn, whole)
                else:
                    rounds(0, whole)
                for t in range(RING * whole, T):
                    if t + RING < T:
                        sp.wait_ge(sem(f"xs_used{l}"), t + 1)
                        load_tile(0, t + RING)
                    sp.wait_ge(sem(f"ys_ready{l}"), t + 1)
                    store_tile(0, t)

            sorted_tiles(0)
            sp.wait_ge(sem("ys_ready0"), T0)
            load_experts(sp, 1)
            sorted_tiles(1)
            for j in range(4):
                sp.wait_ge(sem("x_final"), j + 1)
                s = slice(4 * j, 4 * j + 4)
                sp.dma_start(out_tiles[:, s, :], x[:, s, :]).then_inc(sem("stored"), 16)
            sp.wait_ge(sem("stored"), 64)

        @block.gpsimd
        def _(pool):
            pool.memset(zeros[:], 0.0).then_inc(sem("zeros_set"), 1)
            pool.memset(ident[:], 0.0).then_inc(sem("p_fill"), 1)
            pool.memset(ones[:], 1.0).then_inc(sem("p_fill"), 1)
            pool.memset(blockm[:], 1.0).then_inc(sem("p_fill"), 1)
            pool.memset(pick[:], 0.0).then_inc(sem("p_fill"), 1)
            for g in GROUPS:
                pool.memset(keep[g][:], 1.0).then_inc(sem("p_fill"), 1)
            pool.memset(ks[:, :, :], 0.0).then_inc(sem("ks_zero"), 1)
            pool.wait_ge(sem("p_fill"), 4 + len(GROUPS))
            pool.affine_select(out=ident[:], in_=ident[:], compare_op=ALU.not_equal, fill=1.0, base=0,
                               pattern=[[-1, P]], channel_multiplier=1).then_inc(sem("ident_set"), 1)
            pool.affine_select(out=pick[:], in_=pick[:], compare_op=ALU.not_equal, fill=1.0, base=0,
                               pattern=[[0, HEADS], [-1, HD]], channel_multiplier=1).then_inc(sem("pick_set"), 1)
            pool.affine_select(out=blockm[:], in_=blockm[:], compare_op=ALU.is_ge, fill=0.0, base=0,
                               pattern=[[-HD, HEADS], [0, HD]], channel_multiplier=1).then_inc(sem("p_block"), 1)
            pool.wait_ge(sem("p_block"), 1)
            pool.affine_select(out=blockm[:], in_=blockm[:], compare_op=ALU.is_ge, fill=0.0, base=HD - 1,
                               pattern=[[HD, HEADS], [0, HD]], channel_multiplier=-1).then_inc(sem("pick_set"), 1)
            pool.affine_select(out=before[:], in_=ones[:], compare_op=ALU.is_gt, fill=0.0, base=0,
                               pattern=[[1, P]], channel_multiplier=-1).then_inc(sem("tables_set"), 1)
            for g, (lo, hi, _) in GROUPS.items():
                pool.affine_select(out=keep[g][:], in_=keep[g][:], compare_op=ALU.is_gt, fill=0.0, base=0,
                                   pattern=[[0, NE], [1, hi - lo]], channel_multiplier=0).then_inc(sem("tables_set"), 1)
            pool.iota(kidx_i[:], pattern=[[1, NATT]], base=0, channel_multiplier=0).then_inc(sem("kidx_set"), 1)
            exact = dict(allow_small_or_imprecise_dtypes=True)
            pool.iota(ridx[:], pattern=[[P, NA]], base=0, channel_multiplier=1, **exact).then_inc(sem("kidx_set"), 1)
            pool.iota(e_rank[:], pattern=[[-1, NE]], base=NE, channel_multiplier=0, **exact).then_inc(sem("tables_set"), 1)
            pool.iota(step128[:], pattern=[[P, NT]], base=0, channel_multiplier=0, **exact).then_inc(sem("tables_set"), 1)
            pool.iota(tidx[:], pattern=[[1, TMAX]], base=0, channel_multiplier=0, **exact).then_inc(sem("tables_set"), 1)

            for k, name in enumerate(("lq_b", "lk_b", "lv_b", "lnc_w", "lnd_w")):
                load(pool, small[:, k, :], A["L0_attn_" + name].partition_broadcast(P), "small")
            for k, name in enumerate(("threshold", "factor", "temp_base")):
                load(pool, scal[:, k:k + 1], A["L0_attn_" + name].partition_broadcast(P), "small")
            load(pool, bo_row[:], A["L0_attn_bo"].partition_broadcast(P), "small")
            load(pool, br_row[:], A["L1_ffn_br"].partition_broadcast(P), "small")

            def scatter_rows(g, l):
                lo, hi, experts = GROUPS[g]
                pool.wait_ge(sem("slots_" + g), 1)
                pool.wait_ge(sem("rows_" + g), 1)
                pool.wait_ge(sem(f"cleared{l}"), 16 * clears(l))
                for j in range(lo, hi):
                    for k in range(experts):
                        pool.indirect_dma_start(ROWS[l], bass.IndirectOffsetOnAxis(ap=posu[:, k, j:j + 1], axis=0),
                                                xn[:, j, :], None).then_inc(sem("scattered_" + g), 16)

            def gather_rows(g, l):
                for r in range(RING):
                    pool.wait_ge(sem(f"ys_stored{r}"), 16 * (earlier(l, r) + len(range(r, SORTED[g][1], RING))))
                for q, (lo, hi) in enumerate(CHUNKS[g]):
                    for j in range(lo, hi):
                        for k in range(GROUPS[g][2]):
                            pool.indirect_dma_start((y0, y1)[k][:, j, :], None, BACK[l][0:SORTED[g][1] * P, :],
                                                    bass.IndirectOffsetOnAxis(ap=posu[:, k, j:j + 1], axis=0)
                                                    ).then_inc(sem(f"gathered_{g}{q}"), 16)

            steps = [0]

            def then(ins):
                steps[0] += 1
                ins.then_inc(sem("p_step"), 1)
                pool.wait_ge(sem("p_step"), steps[0])

            H = P // 2
            pool.wait_ge(sem("tables_set"), 4 + len(GROUPS))
            then(pool.memset(rotx[0:H, 0:1], 1.0))
            then(pool.memset(rotx[H:P, 0:1], 0.0))
            then(pool.memset(roty[0:H, 0:1], 0.0))
            then(pool.memset(roty[H:P, 0:1], -1.0))
            pool.wait_ge(sem("sines"), 1)
            then(pool.tensor_copy(turn[:, 0:1], ph[:, 7:8]))
            then(pool.tensor_copy(turn[:, 1:2], ph[:, 6:7]))
            c_, s_, cc, ss, t_ = (turn[:, k:k + 1] for k in range(5))

            def unit():
                then(pool.tensor_tensor(cc, c_, c_, ALU.mult))
                then(pool.tensor_tensor(ss, s_, s_, ALU.mult))
                then(pool.tensor_tensor(t_, cc, ss, ALU.add))
                then(pool.tensor_scalar(t_, t_, -0.5, 1.5, ALU.mult, ALU.add))
                then(pool.tensor_tensor(c_, c_, t_, ALU.mult))
                then(pool.tensor_tensor(s_, s_, t_, ALU.mult))

            unit()
            L = 1
            while L <= N:
                n = min(L, N + 1 - L)
                X, Y, tc, ts = rotx[:, 0:n], roty[:, 0:n], tmp_c[:, 0:n], tmp_s[:, 0:n]
                pool.tensor_scalar(tc, X, c_, None, ALU.mult)
                then(pool.tensor_scalar(ts, Y, s_, None, ALU.mult))
                then(pool.tensor_tensor(rotx[:, L:L + n], tc, ts, ALU.subtract))
                pool.tensor_scalar(tc, X, s_, None, ALU.mult)
                then(pool.tensor_scalar(ts, Y, c_, None, ALU.mult))
                ins = pool.tensor_tensor(roty[:, L:L + n], tc, ts, ALU.add)
                L *= 2
                if L > N:
                    ins.then_inc(sem("rotations"), 1)
                    break
                then(ins)
                then(pool.tensor_tensor(cc, c_, c_, ALU.mult))
                then(pool.tensor_tensor(ss, s_, s_, ALU.mult))
                then(pool.tensor_tensor(t_, c_, s_, ALU.mult))
                then(pool.tensor_tensor(c_, cc, ss, ALU.subtract))
                then(pool.tensor_tensor(s_, t_, t_, ALU.add))
                unit()
            pool.wait_ge(sem("rotations"), 1)
            scatter_rows("far", 0)
            scatter_rows("near", 0)
            gather_rows("far", 0)
            gather_rows("near", 0)
            scatter_rows("all", 1)
            gather_rows("all", 1)

        @block.scalar
        def _(act):
            for k, name in enumerate(("lq_w", "lk_w", "lv_w")):
                load(act, ln[k * HD:(k + 1) * HD, :], A["L0_attn_" + name], "lmaps")

            act.wait_ge(sem("cols_set"), 1)
            act.activation(silu[:, 0, :], cols[:, 0:2], ACT.Exp, scale=-1.0).then_inc(sem("silu_exp"), 1)
            act.wait_ge(sem("qkv"), 1)
            act.activation(kT[:], ps[:, 1, 0:NATT], ACT.Copy, scale=float(HD ** -0.25)).then_inc(sem("kT"), 1)
            act.wait_ge(sem("qkv"), 3)
            act.activation(vT[:], ps[:, 3, 0:NATT], ACT.Identity, bias=cols[:, ROW_BV:ROW_BV + 1]).then_inc(sem("vT"), 1)
            act.wait_ge(sem("mod_made"), 2)
            mr_f = modrow[1][:].rearrange("p a c -> p (a c)")
            act.copy(mr_f[:, 0:512], ps[:, 1, :]).then_inc(sem("late_read"), 1)
            act.copy(mr_f[:, 512:768], ps[:, 2, 0:256]).then_inc(sem("late_read"), 1)
            act.copy(modcol[1][:], ps[:, 3, 0:6]).then_inc(sem("late_read"), 1)
            act.wait_ge(sem("t_recur"), 1)
            for k, t in enumerate((winT, wox, woy)):
                act.copy(t[:], ps[:, 0, k * D:(k + 1) * D]).then_inc(sem("late_read"), 1)
            act.wait_ge(sem("ks_zero"), 1)
            for g in range(4):
                act.wait_ge(sem("kstackT"), g + 1)
                act.copy(ks[STK:P, 4 * g + 1:4 * g + 4:2, :], psb[STK:P, g, 0:2 * NATT].rearrange("p (a n) -> p a n", a=2)
                         ).then_inc(sem("ks_odd"), 1)

            def softmax_exp(it):
                nj, nw = -(-WINDOWS[it] // P), WINDOWS[it]

                def head(i, q):
                    h = 4 * i + q
                    b = q % 2
                    act.wait_ge(sem("probs_free"), 4 * i + (HEADS * it + q + 1))
                    act.copy(v_now[:, q, :, 0:HD + 1], vpx[:, :, bass.ds(h, 1), :])
                    act.wait_ge(sem("st_ready"), 4 * i + (HEADS * it + q + 1))
                    act.activation(probs[:, b, 0:nj, 0:nw], ps[:, 3 * b:3 * b + nj, 0:nw], ACT.Exp
                                   ).then_inc(sem("probs_ready"), 1)

                def take(i):
                    act.wait_ge(sem("probs_free"), 4 * i + (HEADS * it + 6))
                    act.copy(oT[:, bass.ds(i, 1), 0:nw], ps[:, 6, 0:nw]).then_inc(sem("o_taken"), 1)

                for q in range(4):
                    head(0, q)
                with act.Fori(0, HEADS // 4 - 1) as i:
                    head(i + 1, 0)
                    take(i)
                    for q in range(1, 4):
                        head(i + 1, q)
                take(HEADS // 4 - 1)

            def stack_copies(n):
                for g in range(2, 4):
                    act.wait_ge(sem("stackT"), 4 * n + g + 1)
                    act.copy(qs[:, 2 * g:2 * g + 2, :], psb[:, g, 0:2 * NATT].rearrange("p (a n) -> p a n", a=2)
                             ).then_inc(sem("qs_act"), 1)

            def router_rows(g):
                lo, hi, _ = GROUPS[g]
                for q in range(-(-(hi - lo) // 4)):
                    n = min(4, hi - lo - 4 * q) * P
                    act.wait_ge(sem("turned_" + g), q + 1)
                    if q >= 2:
                        act.wait_ge(sem("hT_used_" + g), q - 1)
                    act.activation(hTr[:, q % 2, 0:n], ps[:, q % 2, 0:n], ACT.Identity, scale=modcol[0][:, CB:CB + 1],
                                   bias=modcol[0][:, SB:SB + 1]).then_inc(sem("hT_" + g), 1)

            def gap_exp(g):
                lo, hi, _ = GROUPS[g]
                act.wait_ge(sem("top_gap_" + g), 1)
                act.activation(top[:, 2, lo:hi], top[:, 2, lo:hi], ACT.Exp).then_inc(sem("gap_exp_" + g), 1)

            for it in range(3):
                if it == 1:
                    act.wait_ge(sem("angles"), 1)
                    act.activation(ph[:, 6:8], ph[:, 4:6], ACT.Sin).then_inc(sem("sines"), 1)
                    act.activation(decay[:, 0:1], fcol[:, 1:2], ACT.Exp, scale=-1.0).then_inc(sem("decay_exp"), 1)
                    router_rows("far")
                if it == 2:
                    gap_exp("far")
                stack_copies(2 * it)
                stack_copies(2 * it + 1)
                softmax_exp(it)

            def turned(l, stage, scale, bias):
                for g in range(NT // 4):
                    act.wait_ge(sem(f"turned{l}{stage}"), g + 1)
                    kw = {} if scale is None else dict(scale=scale, bias=bias)
                    act.activation(hT[:, 512 * g:512 * g + 512], ps[:, g % 2, :], ACT.Identity, **kw
                                   ).then_inc(sem(f"hT{l}{stage}"), 1)

            def experts(l):
                T = NTILE[l]
                fn = (ACT.Gelu_apprx_tanh, ACT.Relu)[l]
                sc, bi = ((modcol[0][:, CB:CB + 1], modcol[0][:, SB:SB + 1]),
                          (cols[:, ROW_G:ROW_G + 1], cols[:, ROW_B:ROW_B + 1]))[l]

                def modulate(k, c):
                    act.wait_ge(sem(f"xs_used{l}"), RING * k + (c + 1))
                    if not isinstance(k, int) or k * RING + c >= 2:
                        act.wait_ge(sem(f"h_ready{l}"), RING * k + (c - 1))
                    act.activation(xsT[:, c % 2, :], ps[:, 4 + c % 2, 0:P], ACT.Identity, scale=sc, bias=bi
                                   ).then_inc(sem(f"xsT_ready{l}"), 1)

                def nonlinear(k, c):
                    act.wait_ge(sem(f"hT_ready{l}"), RING * k + (c + 1))
                    if not isinstance(k, int) or k * RING + c >= 2:
                        act.wait_ge(sem(f"o_ready{l}"), RING * k + (c - 1))
                    act.activation(hg[:, c % 2, :], ps[:, 2 + c % 2, :], fn).then_inc(sem(f"hg_ready{l}"), 1)

                modulate(0, 0)
                modulate(0, 1)
                nonlinear(0, 0)
                modulate(0, 2)
                nonlinear(0, 1)
                modulate(0, 3)
                nloop = (T - 4) // RING
                with act.Fori(0, nloop) as k:
                    for c in range(2, 2 + RING):
                        nonlinear(k, c)
                        modulate(k, c + 2)
                for t in range(RING * nloop + 2, T):
                    nonlinear(0, t)
                    if t + 2 < T:
                        modulate(0, t + 2)

            router_rows("near")
            gap_exp("near")
            experts(0)
            turned(1, "a", modcol[1][:, CA:CA + 1], modcol[1][:, SA:SA + 1])
            turned(1, "f", None, None)
            act.wait_ge(sem("lg_shifted"), 1)
            act.activation(lg2[:], lg2[:], ACT.Exp).then_inc(sem("lg_exp"), 1)
            experts(1)

        @block.tensor
        def _(pe):
            pe.wait_ge(sem("ident_set"), 1)
            pe.wait_ge(sem("ld_rows"), 16 * 9)
            pe.transpose(ps[:, 0, 0:NROW], rows[:], ident[0:NROW, 0:NROW]).then_inc(sem("t_cols"), 1)

            def modulation(l, b0, b1, b2):
                pe.wait_ge(sem(f"ld_wmod{l}"), 16)
                pe.matmul(ps[:, b0, :], siluw[:, l, :], wmod[:, l, 0:512], start=True, stop=True)
                for c in range(6):
                    pe.matmul(ps[:, b2, c:c + 1], wmod[:, l, c * D:(c + 1) * D], silu[:, 2, l:l + 1],
                              start=True, stop=True)
                pe.matmul(ps[:, b1, 0:256], siluw[:, l, :], wmod[:, l, 512:768], start=True, stop=True
                          ).then_inc(sem("mod_made"), 1)

            pe.wait_ge(sem("ld_lmaps"), 48)
            pe.transpose(ps[0:HD, 2, 64:64 + 3 * HD], ln[:], ident[0:3 * HD, 0:3 * HD]).then_inc(sem("t_lT"), 1)
            pe.wait_ge(sem("silu_set"), 1)
            modulation(0, 3, 4, 5)
            pe.wait_ge(sem("ld_wnat"), 64)
            for k in range(4):
                mm = pe.transpose(ps[:, 1, k * D:(k + 1) * D], wnat[:, k, :], ident[:])
            mm.then_inc(sem("t_wT"), 1)
            pe.wait_ge(sem("pick_set"), 2)
            pe.wait_ge(sem("lT_set"), 1)
            pe.matmul(ps[:, 2, 0:3 * HD], pick[:], lT[:], start=True, stop=True).then_inc(sem("t_bd"), 1)

            pe.wait_ge(sem("n2"), 1)
            for j in range(NA):
                mm = pe.transpose(ps[:, 0, j * P:(j + 1) * P], ahn[:, j, :], ident[:])
            mm.then_inc(sem("t_n2"), 1)
            pe.wait_ge(sem("n2T"), 1)
            pe.wait_ge(sem("wT_set"), 1)
            pe.wait_ge(sem("mod_read"), 1)
            pe.wait_ge(sem("bd_set"), 1)
            for k, bank in ((1, 1), (0, 2), (2, 3)):
                pe.matmul(ps[:, bank, 0:NATT], wT[:, k, :], n2T[:], start=True, stop=True).then_inc(sem("qkv"), 1)

            def heads_map(k, srcT, bank, when, value, done):
                pe.wait_ge(sem(when), value)
                for j in range(NA):
                    mm = pe.matmul(ps[:, bank, j * D:(j + 1) * D], srcT[:, j * P:(j + 1) * P],
                                   bd[:, k, :, :].rearrange("p h o -> p (h o)"), start=True, stop=True)
                mm.then_inc(sem(done), 1)

            pe.wait_ge(sem("mod_read"), 2)
            heads_map(1, kT, 4, "kT", 1, "kp")
            heads_map(0, qT, 7, "qT", 1, "qp")
            heads_map(2, vT, 5, "vT", 1, "vp")
            modulation(1, 1, 2, 3)
            pe.wait_ge(sem("recur_rows"), 1)
            pe.transpose(ps[:, 0, 0:D], win_n[:], ident[:])
            pe.transpose(ps[:, 0, D:2 * D], wo_n[:, 0, :], ident[:])
            pe.transpose(ps[:, 0, 2 * D:3 * D], wo_n[:, 1, :], ident[:]).then_inc(sem("t_recur"), 1)
            pe.wait_ge(sem("late_read"), 6)

            def turn_stack(name):
                for g in range(4):
                    for a in range(2):
                        for j in range(NA):
                            pr = 2 * g + a
                            mm = pe.transpose(psb[:, g, a * NATT + j * P:a * NATT + (j + 1) * P],
                                              stack[:, j * HEADS + 2 * pr:j * HEADS + 2 * pr + 2, :].rearrange("p h s -> p (h s)"),
                                              identb[:])
                    mm.then_inc(sem(name), 1)

            pe.wait_ge(sem("k_stack"), 1)
            turn_stack("kstackT")

            def attend(it):
                nj, nw = -(-WINDOWS[it] // P), WINDOWS[it]
                pe.wait_ge(sem("q_stack"), 2 * it + 1)
                if it == 0:
                    pe.wait_ge(sem("ks_set"), 1)
                    pe.wait_ge(sem("ks_odd"), 4)
                if it == 1:
                    pe.wait_ge(sem("lg_read_far"), 1)
                if it == 2:
                    pe.wait_ge(sem("counts_read_far"), 1)
                turn_stack("stackT")
                pe.wait_ge(sem("qs_vec"), 2 * (2 * it + 1))
                pe.wait_ge(sem("qs_act"), 2 * (2 * it + 1))
                pe.wait_ge(sem("ks_set"), it + 1)
                pe.wait_ge(sem("ks_odd"), 4)
                with pe.Fori(0, HEADS // 2) as i:
                    for b in range(2):
                        pe.wait_ge(sem("max_free"), 2 * i + (HEADS * it + b + 1))
                        for j in range(nj):
                            mm = pe.matmul(ps[:, 3 * b + j, 0:nw], qs[:, bass.ds(i, 1), j * P:(j + 1) * P],
                                           ks[:, bass.ds(2 * i + b, 1), 0:nw], start=True, stop=True)
                        mm.then_inc(sem("s_ready"), 1)
                pe.wait_ge(sem("q_stack"), 2 * it + 2)
                turn_stack("stackT")
                pe.wait_ge(sem("qs_vec"), 2 * (2 * it + 2))
                pe.wait_ge(sem("qs_act"), 2 * (2 * it + 2))
                def scores_t(i, q):
                    pair, b = 2 * i + q // 2, q % 2
                    if not (isinstance(i, int) and HEADS * it + 4 * i + q < 2):
                        pe.wait_ge(sem("probs_ready"), 4 * i + (HEADS * it + q - 1))
                    for j in range(nj):
                        mm = pe.matmul(ps[:, 3 * b + j, 0:nw], ks[:, bass.ds(4 * i + q, 1), j * P:(j + 1) * P],
                                       qs[:, bass.ds(pair, 1), 0:nw], start=True, stop=True)
                    mm.then_inc(sem("st_ready"), 1)

                def weigh(i, q):
                    if q == 0 and not (isinstance(i, int) and i == 0):
                        pe.wait_ge(sem("o_taken"), i + (HEADS // 4 * it))
                    pe.wait_ge(sem("probs_ready"), 4 * i + (HEADS * it + q + 1))
                    for jk in range(nj):
                        mm = pe.matmul(ps[q * OROW:(q + 1) * OROW, 6, 0:nw], v_now[:, q, jk, :], probs[:, q % 2, jk, 0:nw],
                                       start=(jk == 0), stop=(jk == nj - 1))
                    mm.then_inc(sem("probs_free"), 1)

                scores_t(0, 0)
                scores_t(0, 1)
                weigh(0, 0)
                scores_t(0, 2)
                weigh(0, 1)
                scores_t(0, 3)
                with pe.Fori(0, HEADS // 4 - 1) as i:
                    weigh(i, 2)
                    scores_t(i + 1, 0)
                    weigh(i, 3)
                    scores_t(i + 1, 1)
                    weigh(i + 1, 0)
                    scores_t(i + 1, 2)
                    weigh(i + 1, 1)
                    scores_t(i + 1, 3)
                weigh(HEADS // 4 - 1, 2)
                weigh(HEADS // 4 - 1, 3)
                pe.wait_ge(sem("o_taken"), HEADS // 4 * (it + 1))
                for j in range(nj):
                    for g in range(HEADS // 4):
                        mm = pe.transpose(ps[:, j, g * P:(g + 1) * P], oT[:, g, j * P:(j + 1) * P], ident[:])
                mm.then_inc(sem("o_turned"), 1)
                if it < 2:
                    pe.wait_ge(sem("asum"), it + 1)
                    pe.matmul(ps[:, 7, 0:1], ones[:], asum[:], start=True, stop=True).then_inc(sem("change"), 1)
                    for j in range(NA):
                        mm = pe.transpose(ps[:, 5, j * P:(j + 1) * P], att[it][:, j, :], ident[:])
                    mm.then_inc(sem("attT"), 1)
                    heads_map(0, qT, 7, "qT", it + 2, "qp")

            def router0(g):
                lo, hi, _ = GROUPS[g]
                pe.wait_ge(sem("rows_" + g), 1)
                steps = -(-(hi - lo) // 4)

                def turn(q):
                    if q >= 2:
                        pe.wait_ge(sem("hT_" + g), q - 1)
                    for j in range(4 * q, min(4 * q + 4, hi - lo)):
                        mm = pe.transpose(ps[:, q % 2, (j % 4) * P:(j % 4 + 1) * P], xn[:, lo + j, :], ident[:])
                    mm.then_inc(sem("turned_" + g), 1)

                turn(0)
                for q in range(steps):
                    if q + 1 < steps:
                        turn(q + 1)
                    pe.wait_ge(sem("hT_" + g), q + 1)
                    for j in range(4 * q, min(4 * q + 4, hi - lo)):
                        mm = pe.matmul(ps[:, 2, j * NE:(j + 1) * NE], hTr[:, q % 2, (j % 4) * P:(j % 4 + 1) * P],
                                       cols[:, ROW_ROUTER:NROW], start=True, stop=True)
                    mm.then_inc(sem("hT_used_" + g), 1)

            def count(g):
                lo, hi, _ = GROUPS[g]
                pe.wait_ge(sem("chosen_" + g), 1)
                ch = chosen[:, lo:hi, :].rearrange("p j e -> p (j e)")
                pe.matmul(ps[:, 3, 0:(hi - lo) * NE], before[:], ch, start=True, stop=True)
                pe.matmul(ps[:, 4, 0:(hi - lo) * NE], onesb[:], ch, start=True, stop=True).then_inc(sem("counts_" + g), 1)

            attend(0)
            router0("far")
            attend(1)
            count("far")
            attend(2)
            pe.wait_ge(sem("att_final"), 1)
            for j in range(NA):
                mm = pe.transpose(ps[:, 5, j * P:(j + 1) * P], att[2][:, j, :], ident[:])
            mm.then_inc(sem("attT"), 1)
            pe.wait_ge(sem("attT_copied"), 1)
            for j in range(NA):
                mm = pe.matmul(ps[:, 7, j * D:(j + 1) * D], kT[:, j * P:(j + 1) * P], wT[:, 3, :], start=True, stop=True)
            mm.then_inc(sem("att_out"), 1)

            def turn_rows(l, stage, src, value):
                for g in range(NT // 4):
                    pe.wait_ge(sem(f"rows_ready{l}{stage}"), value(g))
                    if g >= 2:
                        pe.wait_ge(sem(f"hT{l}{stage}"), g - 1)
                    for j in range(4):
                        mm = pe.transpose(ps[:, g % 2, j * P:(j + 1) * P], src[:, 4 * g + j, :], ident[:])
                    mm.then_inc(sem(f"turned{l}{stage}"), 1)

            def router1():
                for g in range(NT // 4):
                    pe.wait_ge(sem("hT1f"), g + 1)
                    for j in range(4 * g, 4 * g + 4):
                        mm = pe.matmul(ps[:, 2, j * NE:(j + 1) * NE], hT[:, j * P:(j + 1) * P], wrl[:], start=True, stop=True)
                mm.then_inc(sem("hT_used_all"), 1)

            def experts(l):
                T = NTILE[l]
                regs = [pe.alloc_register(f"pe_expert{l}_{c}") for c in range(2 * RING - 1)]

                def ids(k, c, n):
                    pe.reg_load(regs[0:n], eid[0:1, bass.ds(RING * k + c, n)])
                    return [pe.snap(r, min_val=0, max_val=NE - 1) for r in regs[0:n]]

                def turn_x(k, c):
                    pe.wait_ge(sem(f"xs_loaded{c % RING}"), 16 * (k + (c // RING + 1 + earlier(l, c % RING))))
                    pe.transpose(ps[:, 4 + c % 2, 0:P], xs[:, c % RING, :], ident[:]).then_inc(sem(f"xs_used{l}"), 1)

                def up(k, c, e):
                    pe.wait_ge(sem(f"xsT_ready{l}"), RING * k + (c + 1))
                    pe.matmul(ps[:, c % 2, :], xsT[:, c % 2, :], w_in[:, bass.ds(e, 1), :], start=True, stop=True
                              ).then_inc(sem(f"h_ready{l}"), 1)

                def down(k, c, e):
                    pe.wait_ge(sem(f"hg_ready{l}"), RING * k + (c + 1))
                    if not isinstance(k, int) or RING * k + c >= 2:
                        pe.wait_ge(sem(f"ys_ready{l}"), RING * k + (c - 1))
                    for n in range(NB):
                        mm = pe.matmul(ps[:, 6 + c % 2, 0:D], hg[:, c % 2, n * P:(n + 1) * P],
                                       w_out[:, bass.ds(e * NB + n, 1), :], start=(n == 0), stop=(n == NB - 1))
                    mm.then_inc(sem(f"o_ready{l}"), 1)

                def turn_h(k, c):
                    pe.wait_ge(sem(f"hb_ready{l}"), RING * k + (c + 1))
                    for n in range(NB):
                        mm = pe.transpose(ps[:, 2 + c % 2, n * P:(n + 1) * P], hb[:, c % 2, n * P:(n + 1) * P], ident[:])
                    mm.then_inc(sem(f"hT_ready{l}"), 1)

                pe.wait_ge(sem(f"ld_experts{l}"), 64)
                pe.wait_ge(sem("slots_" + ("near", "all")[l]), 1)

                def slot(k, c, e, last):
                    up(k, c, e[1])
                    down(k, c - 1, e[0])
                    turn_h(k, c)
                    if not last:
                        turn_x(k, c + 2)

                turn_x(0, 0)
                turn_x(0, 1)
                e = ids(0, 0, 2)
                up(0, 0, e[0])
                turn_h(0, 0)
                turn_x(0, 2)
                slot(0, 1, e, False)
                nloop = (T - 4) // RING
                with pe.Fori(0, nloop) as k:
                    e = ids(k, 1, RING + 1)
                    for c in range(RING):
                        slot(k, c + 2, e[c:c + 2], False)
                n = T - RING * nloop
                e = ids(nloop, 1, n - 1)
                for c in range(2, n):
                    slot(nloop, c, e[c - 2:c], c + 2 >= n)
                down(nloop, n - 1, e[n - 2])

            router0("near")
            count("near")
            experts(0)
            turn_rows(1, "a", xn, lambda g: 1)
            for g in range(4):
                pe.wait_ge(sem("hT1a"), g + 1)
                pe.matmul(ps[:, 2 + g, :], winT[:], hT[:, 512 * g:512 * g + 512], start=True, stop=True
                          ).then_inc(sem("modes_in"), 1)
            pe.wait_ge(sem("rotated_back"), 2)
            for g in range(4):
                for j in range(4):
                    t = 4 * g + j
                    pe.matmul(ps[:, 2 + g, j * D:(j + 1) * D], y0[:].rearrange("p j c -> p (j c)")[:, t * P:(t + 1) * P], wox[:], start=True, stop=False)
                    mm = pe.matmul(ps[:, 2 + g, j * D:(j + 1) * D], xn[:].rearrange("p j c -> p (j c)")[:, t * P:(t + 1) * P], woy[:], start=False, stop=True)
                mm.then_inc(sem("modes_out"), 1)
            turn_rows(1, "f", y0, lambda g: 1)
            pe.wait_ge(sem("ld_router1"), 16)
            router1()
            count("all")
            experts(1)

        @block.vector
        def _(v):
            steps = [0]

            def then(ins):
                steps[0] += 1
                ins.then_inc(sem("v_step"), 1)
                v.wait_ge(sem("v_step"), steps[0])

            def signal(ins, name, value):
                ins.then_inc(sem(name), 1)
                v.wait_ge(sem(name), value)

            def rsqrt(src, dst, n):
                yv, a = rs_y[:, 0:n], rs_a[:, 0:n]
                then(v.tensor_scalar(yv.bitcast(I32), src.bitcast(I32), -0.5, RSQRT_MAGIC, ALU.mult, ALU.add))
                for k in range(3):
                    then(v.scalar_tensor_tensor(out=a, in0=yv, scalar=-0.5, in1=yv, op0=ALU.mult, op1=ALU.mult))
                    then(v.tensor_tensor(a, a, src, ALU.mult))
                    then(v.scalar_tensor_tensor(out=dst if k == 2 else yv, in0=a, scalar=1.5, in1=yv, op0=ALU.add, op1=ALU.mult))

            def layernorm(src, dst, lo, hi, done=None):
                for j in range(lo, hi):
                    ins = v.bn_stats(stats[:, j, :], src[:, j, :])
                then(ins)
                for j in range(lo, hi):
                    ins = v.bn_aggr(mv[:, j, :], stats[:, j, :])
                then(ins)
                then(v.tensor_scalar(rs_v[:, 0:hi - lo], mv[:, lo:hi, 1], LN_EPS, None, ALU.add))
                rsqrt(rs_v[:, 0:hi - lo], rstd[:, lo:hi], hi - lo)
                for j in range(lo, hi):
                    ins = v.tensor_scalar(dst[:, j, :], src[:, j, :], mv[:, j, 0:1], rstd[:, j:j + 1], ALU.subtract, ALU.mult)
                if done:
                    signal(ins, done, 1)
                else:
                    then(ins)

            def rowwise(ap, n):
                return ap.unsqueeze(1).to_broadcast([P, n, D])

            then(v.memset(onesb[:], 1.0))
            then(v.memset(v_now[:], 0.0))
            then(v.memset(stack[:], 0.0))
            then(v.memset(stack[:, :, 1:4], -1.0))
            then(v.memset(vpx[:], 1.0))
            v.wait_ge(sem("ld_x_attn"), 16)
            layernorm(x, xn, 0, NA)
            v.wait_ge(sem("t_cols"), 1)
            signal(v.tensor_copy(cols[:], ps[:, 0, 0:NROW]), "cols_set", 1)
            v.wait_ge(sem("silu_exp"), 1)
            then(v.tensor_scalar(silu[:, 1, :], silu[:, 0, :], 1.0, None, ALU.add))
            then(v.reciprocal(silu[:, 1, :], silu[:, 1, :]))
            then(v.tensor_tensor(silu[:, 2, :], silu[:, 1, :], cols[:, 0:2], ALU.mult))
            for l in range(2):
                ins = v.tensor_scalar(siluw[:, l, :], ones[:], silu[:, 2, l:l + 1], None, ALU.mult)
            ins.then_inc(sem("silu_set"), 1)
            v.wait_ge(sem("t_lT"), 1)
            v.tensor_copy(lT[:], ps[0:HD, 2, 64:64 + 3 * HD]).then_inc(sem("lT_set"), 1)
            then(v.tensor_copy(identb[:], ident[:]))
            v.wait_ge(sem("mod_made"), 1)
            m0 = modrow[0][:].rearrange("p a c -> p (a c)")
            signal(v.tensor_copy(m0[:, 0:512], ps[:, 3, :]), "mod_read", 1)
            then(v.scalar_tensor_tensor(out=ah[:], in0=rowwise(modrow[0][:, CA, :], NA), scalar=1.0, in1=xn[:, 0:NA, :], op0=ALU.add, op1=ALU.mult))
            then(v.tensor_tensor(ah[:], ah[:], rowwise(modrow[0][:, SA, :], NA), ALU.add))
            layernorm(ah, ahn, 0, NA, "n2")
            v.wait_ge(sem("t_wT"), 1)
            v.tensor_scalar(wT[:, 0, :], ps[:, 1, 0:D], cols[:, ROW_LNA:ROW_LNA + 1], None, ALU.mult)
            for k in (1, 2):
                v.tensor_scalar(wT[:, k, :], ps[:, 1, k * D:(k + 1) * D], cols[:, ROW_LNB:ROW_LNB + 1], None, ALU.mult)
            signal(v.tensor_copy(wT[:, 3, :], ps[:, 1, 3 * D:4 * D]), "wT_set", 1)
            v.wait_ge(sem("t_n2"), 1)
            signal(v.tensor_copy(n2T[:], ps[:, 0, 0:NATT]), "n2T", 1)
            v.wait_ge(sem("t_bd"), 1)
            for k in range(3):
                ins = v.tensor_tensor(bd[:, k, :, :], blockm[:], ps[:, 2, k * HD:(k + 1) * HD].unsqueeze(1).to_broadcast([P, HEADS, HD]), ALU.mult)
            signal(ins, "bd_set", 1)
            v.tensor_copy(modcol[0][:], ps[:, 5, 0:6])
            signal(v.tensor_copy(m0[:, 512:768], ps[:, 4, 0:256]), "mod_read", 2)

            def clamp_gates(l):
                for c in (CA, CB):
                    v.tensor_scalar(modrow[l][:, c, :], modrow[l][:, c, :], 1.0, None, ALU.add)
                    v.tensor_scalar(modcol[l][:, c:c + 1], modcol[l][:, c:c + 1], 1.0, None, ALU.add)
                g = modrow[l][:, GA:GB + 1:GB - GA, :]
                then(v.tensor_scalar(gsign[:], g, 0.0, 2.0, ALU.is_ge, ALU.mult))
                then(v.tensor_scalar(gsign[:], gsign[:], -1.0, None, ALU.add))
                then(v.scalar_tensor_tensor(out=g, in0=g, scalar=-1.0, in1=g, op0=ALU.mult, op1=ALU.max))
                then(v.scalar_tensor_tensor(out=g, in0=g, scalar=0.25, in1=gsign[:], op0=ALU.max, op1=ALU.mult))

            def recurrence_maps():
                v.wait_ge(sem("ld_recur"), 16 * 13)
                then(v.tensor_scalar(win_n[96:128, :], win_n[96:128, :], -1.0, None, ALU.mult))
                wr, wi = wo_s[:, 0:NF], wo_s[:, NF:2 * NF]
                for a, parts in enumerate((((wr, 1.0), (wi, 1.0), (wi, 1.0), (wr, -1.0)),
                                           ((wi, 1.0), (wr, -1.0), (wr, -1.0), (wi, -1.0)))):
                    for q, (src, sign) in enumerate(parts):
                        ins = v.tensor_scalar(wo_n[:, a, q * NF:(q + 1) * NF], src, sign, None, ALU.mult)
                ins.then_inc(sem("recur_rows"), 1)

            def recurrence_angles():
                then(v.tensor_scalar(ph[:, 0:1], fcol[:, 0:1], float(np.float32(0.1)), None, ALU.mult))
                then(v.tensor_scalar(ph[:, 1:2], ph[:, 0:1], float(np.pi / 2), None, ALU.add))
                then(v.tensor_scalar(phi[:, 0:2], ph[:, 0:2], float(1 / TWO_PI), None, ALU.mult))
                then(v.tensor_copy(ph[:, 2:4], phi[:, 0:2]))
                for part in (TP1, TP2, TP3):
                    then(v.scalar_tensor_tensor(out=ph[:, 4:6], in0=ph[:, 2:4], scalar=-part, in1=ph[:, 0:2] if part == TP1 else ph[:, 4:6], op0=ALU.mult, op1=ALU.add))
                lim = 3.1415925
                signal(v.tensor_scalar(ph[:, 4:6], ph[:, 4:6], lim, -lim, ALU.min, ALU.max), "angles", 1)

            v.wait_ge(sem("kidx_set"), 2)
            then(v.tensor_copy(kidx[:], kidx_i[:]))
            v.wait_ge(sem("ld_small"), 16 * 10)
            v.memset(cw[:, 0:1], float(W0))
            then(v.memset(att[0][:], 0.0))
            v.memset(mx[:], 0.0).then_inc(sem("max_free"), 2)
            v.memset(flags[:], 0.0).then_inc(sem("probs_free"), 2)
            v.wait_ge(sem("max_free"), 2)
            v.wait_ge(sem("probs_free"), 2)
            v.wait_ge(sem("qkv"), 2)
            signal(v.tensor_scalar(qT[:], ps[:, 2, 0:NATT], cols[:, ROW_BQ:ROW_BQ + 1], float(HD ** -0.25), ALU.add, ALU.mult), "qT", 1)

            def grouped(t, nj):
                return t[:, 0:nj * HEADS, :]

            def each(ap8, nj):
                return ap8.unsqueeze(1).to_broadcast([P, nj * HEADS, HD])

            def per(ap, nj):
                return ap[:, 0:nj * HEADS].unsqueeze(2).to_broadcast([P, nj * HEADS, HD])

            def head_norm(bank, bias, weight, nj, tscale=None):
                gi, gc, gs = grouped(gl_in, nj), grouped(gl_c, nj), grouped(gl_s, nj)
                n = nj * HEADS
                then(v.tensor_tensor(gi, ps[:, bank, 0:n * HD].rearrange("p (g o) -> p g o", o=HD), each(small[:, bias, :], nj), ALU.add))
                then(v.tensor_reduce(gl_m[:, 0:n], gi, AX.X, ALU.add))
                then(v.tensor_scalar(gl_m[:, 0:n], gl_m[:, 0:n], 1.0 / HD, None, ALU.mult))
                then(v.tensor_tensor(gc, gi, per(gl_m, nj), ALU.subtract))
                then(v.tensor_tensor(gs, gc, gc, ALU.mult))
                then(v.tensor_reduce(rs_v[:, 0:n], gs, AX.X, ALU.add))
                then(v.tensor_scalar(rs_v[:, 0:n], rs_v[:, 0:n], 1.0 / HD, LN_EPS, ALU.mult, ALU.add))
                rsqrt(rs_v[:, 0:n], gl_m[:, 0:n], n)
                if tscale is not None:
                    then(v.tensor_scalar(gl_m[:, 0:n], gl_m[:, 0:n], tscale, float(np.float32(1 / np.sqrt(HD))), ALU.mult, ALU.mult))
                then(v.tensor_tensor(gc, gc, per(gl_m, nj), ALU.mult))
                then(v.tensor_tensor(gc, gc, each(small[:, weight, :], nj), ALU.mult))

            def slot(s, nj):
                return stack[:, 0:nj * HEADS, s * SLOT:(s + 1) * SLOT]

            def split(nj, firsts, copies):
                gc, r1 = grouped(gl_c, nj), grouped(gl_s, nj)
                then(v.tensor_copy(slot(firsts[0], nj), gc))
                then(v.tensor_tensor(r1, gc, slot(firsts[0], nj), ALU.subtract))
                then(v.tensor_copy(slot(firsts[1], nj), r1))
                then(v.tensor_tensor(r1, r1, slot(firsts[1], nj), ALU.subtract))
                then(v.tensor_copy(slot(firsts[2], nj), r1))
                for a, b in copies:
                    ins = v.tensor_copy(slot(b, nj), slot(a, nj))
                return ins

            recurrence_maps()
            v.wait_ge(sem("kp"), 1)
            head_norm(4, 1, 4, NA)
            signal(split(NA, K_FIRST, K_COPIES), "k_stack", 1)
            v.wait_ge(sem("vp"), 1)
            then(v.tensor_tensor(vpx[:, :, :, 0:HD].rearrange("p j h o -> p (j h) o"), ps[:, 5, 0:NATT].rearrange("p (g o) -> p g o", o=HD), each(small[:, 2, :], NA), ALU.add))
            v.wait_ge(sem("mod_made"), 2)
            then(v.memset(oT, 0.0))
            then(v.tensor_copy(tsc[:, 0:1], scal[:, 2:3]))
            then(v.tensor_scalar(tsc[:, 1:2], tsc[:, 0:1], 0.005, None, ALU.add))
            then(v.tensor_scalar(tsc[:, 2:3], tsc[:, 1:2], 0.005, None, ALU.add))
            then(v.tensor_scalar(rs_v[:, 0:3], tsc[:, 0:3], 1e-37, None, ALU.max))
            rsqrt(rs_v[:, 0:3], tsc[:, 3:6], 3)
            then(v.tensor_scalar(rs_v[:, 0:3], tsc[:, 0:3], 0.0, None, ALU.is_gt))
            then(v.tensor_scalar(tsc[:, 3:6], tsc[:, 3:6], -1.0, None, ALU.add))
            then(v.tensor_tensor(tsc[:, 3:6], tsc[:, 3:6], rs_v[:, 0:3], ALU.mult))
            then(v.tensor_scalar(tsc[:, 3:6], tsc[:, 3:6], 1.0, None, ALU.add))
            v.wait_ge(sem("ks_zero"), 1)
            for g in range(4):
                v.wait_ge(sem("kstackT"), g + 1)
                ins = v.tensor_copy(ks[0:STK, 4 * g:4 * g + 4:2, :], psb[0:STK, g, 0:2 * NATT].rearrange("p (a n) -> p a n", a=2))
            signal(ins, "ks_set", 1)
            v.memset(stack[:, :, 1:4], 0.0)
            then(v.memset(stack[:, :, 0:1], 1.0))

            def stack_copies(n):
                for g in range(2):
                    v.wait_ge(sem("stackT"), 4 * n + g + 1)
                    v.tensor_copy(qs[:, 2 * g:2 * g + 2, :], psb[:, g, 0:2 * NATT].rearrange("p (a n) -> p a n", a=2)
                                  ).then_inc(sem("qs_vec"), 1)

            def lowest(lgt, m, dst, lo, hi):
                n = hi - lo
                bc = lambda t: t.unsqueeze(2).to_broadcast([P, n, NE])
                c = cand[:, lo:hi, :]
                then(v.tensor_reduce(m, lgt, AX.X, ALU.max))
                then(v.tensor_tensor(c, lgt, bc(m), ALU.is_equal))
                then(v.tensor_tensor(c, c, e_rank[:].unsqueeze(1).to_broadcast([P, n, NE]), ALU.mult))
                then(v.tensor_reduce(posf[:, lo:hi], c, AX.X, ALU.max))
                then(v.tensor_tensor(dst, c, bc(posf[:, lo:hi]), ALU.is_equal))

            def read_logits(g):
                lo, hi, experts = GROUPS[g]
                n = hi - lo
                pl = ps[:, 2, 0:n * NE].rearrange("p (j e) -> p j e", e=NE)
                if experts == 2:
                    v.wait_ge(sem("hT_used_" + g), -(-n // 4))
                    signal(v.tensor_copy(lg[:, lo:hi, :], pl), "lg_read_" + g, 1)
                else:
                    v.wait_ge(sem("hT_used_" + g), 1)
                    then(v.tensor_tensor(lg[:, lo:hi, :], pl, br_row[:].unsqueeze(1).to_broadcast([P, n, NE]), ALU.add))

            def choose(g):
                lo, hi, experts = GROUPS[g]
                n = hi - lo
                s = slice(lo, hi)
                lowest(lg[:, s, :], top[:, 0, s], first[0][:, s, :], lo, hi)
                if experts == 2:
                    then(v.scalar_tensor_tensor(out=lg2[:, s, :], in0=first[0][:, s, :], scalar=-3e38, in1=lg[:, s, :], op0=ALU.mult, op1=ALU.add))
                    lowest(lg2[:, s, :], top[:, 1, s], first[1][:, s, :], lo, hi)
                    signal(v.tensor_tensor(chosen[:, s, :], first[0][:, s, :], first[1][:, s, :], ALU.add), "chosen_" + g, 1)
                    signal(v.tensor_tensor(top[:, 2, s], top[:, 1, s], top[:, 0, s], ALU.subtract), "top_gap_" + g, 1)
                else:
                    signal(v.tensor_copy(chosen[:, s, :], first[0][:, s, :]), "chosen_" + g, 1)
                    signal(v.tensor_tensor(lg2[:], lg[:], top[:, 0, :].unsqueeze(2).to_broadcast([P, NT, NE]), ALU.subtract), "lg_shifted", 1)

            def read_counts(g):
                lo, hi, experts = GROUPS[g]
                m = (hi - lo) * NE
                v.wait_ge(sem("counts_" + g), 1)
                v.tensor_copy(pose[:, lo:hi, :], ps[:, 3, 0:m].rearrange("p (j e) -> p j e", e=NE))
                signal(v.tensor_copy(tot_f[:, 0:m].rearrange("p (e j) -> p e j", e=NE),
                                     ps[:, 4, 0:m].rearrange("p (j e) -> p e j", e=NE)), "counts_read_" + g, 1)

            def place(g):
                lo, hi, experts = GROUPS[g]
                n = hi - lo
                t0, t1 = SORTED[g]
                T = t1 - t0
                s = slice(lo, hi)
                fl = lambda t: t[:, 0:NE * n]
                ej = lambda t: fl(t).rearrange("p (e j) -> p e j", e=NE)
                inc, tot, cmp_t = ej(inc_f), ej(tot_f), ej(cmp_f)
                then(v.tensor_tensor_scan(fl(inc_f), keep[g][:].rearrange("p e j -> p (e j)"), fl(tot_f), 0.0, ALU.mult, ALU.add))
                then(v.tensor_tensor(cmp_t, inc[:, :, n - 1:n].to_broadcast([P, NE, n]), step128[:, 0:n].unsqueeze(1).to_broadcast([P, NE, n]), ALU.is_gt))
                then(v.tensor_reduce(ntile[:], cmp_t, AX.X, ALU.add))
                then(v.tensor_tensor_scan(tend[:], ones[:, 0:NE], ntile[:], float(t0), ALU.mult, ALU.add))
                then(v.tensor_tensor(tbase[:], tend[:], ntile[:], ALU.subtract))
                then(v.tensor_scalar(tbase[:], tbase[:], float(P), None, ALU.mult))
                then(v.tensor_tensor(inc, inc, tot, ALU.subtract))
                then(v.tensor_tensor(inc, inc, tbase[:].unsqueeze(2).to_broadcast([P, NE, n]), ALU.add))
                then(v.tensor_tensor(pose[:, s, :], pose[:, s, :], inc.rearrange("p e j -> p j e"), ALU.add))
                then(v.tensor_tensor(cmp_e[:, t0:t1, :], tidx[:, t0:t1].unsqueeze(2).to_broadcast([P, T, NE]), tend[:].unsqueeze(1).to_broadcast([P, T, NE]), ALU.is_ge))
                then(v.tensor_reduce(eidf[:, t0:t1], cmp_e[:, t0:t1, :], AX.X, ALU.add))
                then(v.tensor_scalar(eid[:, t0:t1], eidf[:, t0:t1], float(NE - 1), None, ALU.min))
                for k in range(experts):
                    then(v.tensor_tensor(cand[:, s, :], pose[:, s, :], first[k][:, s, :], ALU.mult))
                    then(v.tensor_reduce(posf[:, s], cand[:, s, :], AX.X, ALU.add))
                    ins = v.tensor_copy(posu[:, k, s], posf[:, s])
                    if k < experts - 1:
                        then(ins)
                signal(ins, "slots_" + g, 1)

            def gates(g):
                lo, hi, experts = GROUPS[g]
                s = slice(lo, hi)
                if experts == 2:
                    v.wait_ge(sem("gap_exp_" + g), 1)
                    then(v.tensor_scalar(gate[:, 1, s], top[:, 2, s], 1.0, None, ALU.add))
                    then(v.reciprocal(gate[:, 0, s], gate[:, 1, s]))
                    then(v.tensor_tensor(gate[:, 1, s], top[:, 2, s], gate[:, 0, s], ALU.mult))
                else:
                    v.wait_ge(sem("lg_exp"), 1)
                    then(v.tensor_reduce(posf[:], lg2[:], AX.X, ALU.add))
                    then(v.reciprocal(gate[:, 0, :], posf[:]))

            up_, dn_, conv_ = 0, 2, 4

            def attend(it):
                nj, nw = -(-WINDOWS[it] // P), WINDOWS[it]
                n = nj * HEADS
                if it:
                    for p0, h0 in ((0, 0), (STK, 1)):
                        ins = v.tensor_scalar(ks[p0:p0 + 1, h0::2, WMIN:NATT], kidx[p0:p0 + 1, WMIN:NATT].unsqueeze(1).to_broadcast([1, HEADS // 2, NATT - WMIN]),
                                              cw[p0:p0 + 1, it:it + 1], MASKED, ALU.is_ge, ALU.mult)
                    signal(ins, "ks_set", it + 1)
                then(v.tensor_scalar(rowm[:], ridx[:], cw[:, it:it + 1], None, ALU.is_lt))
                v.wait_ge(sem("qp"), it + 1)
                head_norm(7, 0, 3, nj, tsc[:, 3 + it:4 + it])
                if it:
                    then(v.memset(stack[:, :, 1:4], 0.0))
                if it == 1:
                    read_logits("far")
                if it == 2:
                    read_counts("far")
                signal(split(nj, Q_FIRST, Q_COPIES), "q_stack", 2 * it + 1)
                stack_copies(2 * it)
                with v.Fori(0, HEADS // 2) as i:
                    for b in range(2):
                        v.wait_ge(sem("s_ready"), 2 * i + (HEADS * it + b + 1))
                        v.tensor_reduce(mx[:, 0:nj, bass.ds(2 * i + b, 1)], ps[:, 3 * b:3 * b + nj, 0:nw], AX.X, ALU.max
                                        ).then_inc(sem("max_free"), 1)
                v.wait_ge(sem("max_free"), 2 + HEADS * (it + 1))
                m, r = mx[:, 0:nj, :].rearrange("p j h -> p (j h)"), mr[:, 0:n]
                for k in range(3):
                    dst = stack[:, 0:n, 1 + k]
                    src = m if k == 0 else r
                    ins = v.tensor_copy(dst, src)
                    if k < 2:
                        then(ins)
                        then(v.tensor_tensor(r, src, dst, ALU.subtract))
                signal(ins, "q_stack", 2 * it + 2)
                stack_copies(2 * it + 1)
                if it == 0:
                    clamp_gates(0)
                    v.wait_ge(sem("ld_x_rest"), 16)
                    then(v.tensor_tensor(ahn[:, 0, :], bo_row[:], modrow[0][:, GA, :], ALU.mult))
                    then(v.tensor_tensor(x[:, NA:NT, :], x[:, NA:NT, :], rowwise(ahn[:, 0, :], NT - NA), ALU.add))
                    v.wait_ge(sem("tables_set"), 4 + len(GROUPS))
                    layernorm(x, xn, NA, NT, "rows_far")
                    recurrence_angles()
                    v.wait_ge(sem("late_read"), 6)
                    clamp_gates(1)
                elif it == 1:
                    choose("far")
                    v.wait_ge(sem("decay_exp"), 1)
                    then(v.tensor_scalar(decay[:, 1:2], decay[:, 0:1], 1.0, None, ALU.add))
                    then(v.reciprocal(decay[:, 1:2], decay[:, 1:2]))
                else:
                    place("far")
                    gates("far")
                v.wait_ge(sem("o_turned"), it + 1)
                o = ps[:, 0:nj, :].rearrange("p j (h s) -> p (j h) s", s=OROW)
                then(v.tensor_scalar(den[:, 0:n], o[:, :, HD], 0.5, None, ALU.max))
                then(v.reciprocal(den[:, 0:n], den[:, 0:n]))
                a3 = att[it][:].rearrange("p j (h o) -> p (j h) o", o=HD)[:, 0:n, :]
                then(v.tensor_tensor(a3, o[:, :, 0:HD], per(den, nj), ALU.mult))
                then(v.tensor_tensor(att[it][:, 0:nj, :], att[it][:, 0:nj, :], rowm[:, 0:nj].unsqueeze(2).to_broadcast([P, nj, D]), ALU.mult))
                if it == 2:
                    return
                af = att[it][:].rearrange("p j c -> p (j c)")
                if it:
                    then(v.tensor_tensor(att_d[:], af, att[it - 1][:].rearrange("p j c -> p (j c)"), ALU.subtract))
                    af = att_d[:]
                signal(v.tensor_reduce(asum[:], af, AX.X, ALU.add, apply_absolute_value=True), "asum", it + 1)
                v.wait_ge(sem("change"), it + 1)
                df = diff[:, it:it + 1]
                then(v.tensor_scalar(df, ps[:, 7, 0:1], 1.0 / (N * D), None, ALU.mult))
                up, dn = flags[:, up_ + it:up_ + it + 1], flags[:, dn_ + it:dn_ + it + 1]
                v.tensor_scalar(up, df, 0.05, None, ALU.is_gt)
                then(v.tensor_scalar(dn, df, 0.001, None, ALU.is_lt))
                nxt = cw[:, it + 1:it + 2]
                if it == 0:
                    then(v.tensor_scalar(nxt, up, float(_up(W0) - W0), float(W0), ALU.mult, ALU.add))
                    then(v.scalar_tensor_tensor(out=nxt, in0=dn, scalar=float(_down(W0) - W0), in1=nxt, op0=ALU.mult, op1=ALU.add))
                else:
                    def change(f, dst):
                        base, a, b = f(W0) - W0, f(_up(W0)) - _up(W0), f(_down(W0)) - _down(W0)
                        then(v.tensor_scalar(dst, flags[:, up_:up_ + 1], float(a - base), float(base), ALU.mult, ALU.add))
                        then(v.scalar_tensor_tensor(out=dst, in0=flags[:, dn_:dn_ + 1], scalar=float(b - base), in1=dst, op0=ALU.mult, op1=ALU.add))
                    change(_up, tsc[:, 6:7])
                    change(_down, tsc[:, 7:8])
                    then(v.scalar_tensor_tensor(out=nxt, in0=tsc[:, 6:7], scalar=up, in1=cw[:, it:it + 1], op0=ALU.mult, op1=ALU.add))
                    then(v.scalar_tensor_tensor(out=nxt, in0=tsc[:, 7:8], scalar=dn, in1=nxt, op0=ALU.mult, op1=ALU.add))
                    then(v.scalar_tensor_tensor(out=tsc[:, 6:7], in0=df, scalar=scal[:, 1:2], in1=scal[:, 0:1], op0=ALU.mult, op1=ALU.add))
                    then(v.tensor_tensor(flags[:, conv_:conv_ + 1], df, tsc[:, 6:7], ALU.is_lt))
                    then(v.tensor_scalar(flags[:, conv_ + 1:conv_ + 2], flags[:, conv_:conv_ + 1], -1.0, 1.0, ALU.mult, ALU.add))
                v.wait_ge(sem("attT"), it + 1)
                signal(v.tensor_tensor(qT[:], qT[:], ps[:, 5, 0:NATT], ALU.add), "qT", it + 2)

            for it in range(3):
                attend(it)
            then(v.tensor_scalar(att[1][:], att[1][:], flags[:, conv_:conv_ + 1], None, ALU.mult))
            signal(v.scalar_tensor_tensor(out=att[2][:], in0=att[2][:], scalar=flags[:, conv_ + 1:conv_ + 2], in1=att[1][:], op0=ALU.mult, op1=ALU.add), "att_final", 1)
            v.wait_ge(sem("attT"), 3)
            signal(v.tensor_copy(kT[:], ps[:, 5, 0:NATT]), "attT_copied", 1)
            v.wait_ge(sem("att_out"), 1)
            then(v.tensor_tensor(ah[:], ps[:, 7, 0:NATT].rearrange("p (j c) -> p j c", c=D), rowwise(bo_row[:], NA), ALU.add))
            then(v.tensor_tensor(ah[:], ah[:], rowwise(modrow[0][:, GA, :], NA), ALU.mult))
            then(v.tensor_tensor(x[:, 0:NA, :], x[:, 0:NA, :], ah[:], ALU.add))

            def experts(l):
                T = NTILE[l]
                regs = [v.alloc_register(f"v_expert{l}_{c}") for c in range(RING + 1)]

                def ids(k, n):
                    v.reg_load(regs[0:n], eid[0:1, bass.ds(RING * k, n)])
                    return [v.snap(r, min_val=0, max_val=NE - 1) for r in regs[0:n]]

                def bias_up(k, c, e):
                    if not isinstance(k, int) or RING * k + c >= 2:
                        v.wait_ge(sem(f"hT_ready{l}"), RING * k + (c - 1))
                    v.wait_ge(sem(f"h_ready{l}"), RING * k + (c + 1))
                    v.tensor_tensor(hb[:, c % 2, :], ps[:, c % 2, :], b_in[:, bass.ds(e, 1), :], ALU.add
                                    ).then_inc(sem(f"hb_ready{l}"), 1)

                def bias_down(k, c, e):
                    if l or not isinstance(k, int) or k > 0:
                        v.wait_ge(sem(f"ys_stored{c % RING}"), 16 * (k + earlier(l, c % RING)))
                    v.wait_ge(sem(f"o_ready{l}"), RING * k + (c + 1))
                    v.tensor_tensor(ys[:, c % RING, :], ps[:, 6 + c % 2, 0:D], b_out[:, bass.ds(e, 1), :], ALU.add
                                    ).then_inc(sem(f"ys_ready{l}"), 1)

                v.wait_ge(sem(f"ld_experts{l}"), 64)
                e = ids(0, 1)
                bias_up(0, 0, e[0])
                e = ids(0, RING)
                for c in range(1, RING):
                    bias_up(0, c, e[c])
                    bias_down(0, c - 1, e[c - 1])
                nloop = (T - RING) // RING
                with v.Fori(0, nloop) as k0:
                    k = k0 + 1
                    v.reg_load(regs[0:RING + 1], eid[0:1, bass.ds(RING * k - 1, RING + 1)])
                    e = [v.snap(r, min_val=0, max_val=NE - 1) for r in regs]
                    bias_up(k, 0, e[1])
                    bias_down(k0, RING - 1, e[0])
                    for c in range(1, RING):
                        bias_up(k, c, e[c + 1])
                        bias_down(k, c - 1, e[c])
                base = RING * (nloop + 1)
                n = T - base
                v.reg_load(regs[0:n + 1], eid[0:1, bass.ds(base - 1, n + 1)])
                e = [v.snap(r, min_val=0, max_val=NE - 1) for r in regs[0:n + 1]]
                for c in range(n):
                    bias_up(nloop + 1, c, e[c + 1])
                    if c == 0:
                        bias_down(nloop, RING - 1, e[0])
                    else:
                        bias_down(nloop + 1, c - 1, e[c])
                bias_down(nloop + 1, n - 1, e[n])

            def add_ffn(g, l):
                for q, (lo, hi) in enumerate(CHUNKS[g]):
                    s = slice(lo, hi)
                    v.wait_ge(sem(f"gathered_{g}{q}"), 16 * (hi - lo) * GROUPS[g][2])
                    for j in range(lo, hi):
                        ins = v.tensor_scalar(y0[:, j, :], y0[:, j, :], gate[:, 0, j:j + 1], None, ALU.mult)
                    then(ins)
                    if l == 0:
                        for j in range(lo, hi):
                            ins = v.scalar_tensor_tensor(out=y0[:, j, :], in0=y1[:, j, :], scalar=gate[:, 1, j:j + 1], in1=y0[:, j, :], op0=ALU.mult, op1=ALU.add)
                        then(ins)
                    then(v.tensor_tensor(y0[:, s, :], y0[:, s, :], rowwise(modrow[l][:, GB, :], hi - lo), ALU.mult))
                    ins = v.tensor_tensor(x[:, s, :], x[:, s, :], y0[:, s, :], ALU.add)
                    if l:
                        signal(ins, "x_final", q + 1)
                    else:
                        then(ins)

            layernorm(x, xn, 0, NA, "rows_near")
            read_logits("near")
            choose("near")
            read_counts("near")
            place("near")
            gates("near")
            experts(0)
            add_ffn("far", 0)
            add_ffn("near", 0)
            layernorm(x, xn, 0, NT, "rows_ready1a")
            v.wait_ge(sem("rotations"), 1)
            flat = lambda t: t[:, :, :].rearrange("p j c -> p (j c)")
            for g in range(4):
                s = slice(512 * g, 512 * g + 512)
                v.wait_ge(sem("modes_in"), g + 1)
                ins = v.tensor_tensor(flat(y0)[:, s], ps[:, 2 + g, :], rotx[:, s], ALU.mult)
            then(ins)
            then(v.tensor_tensor_scan(flat(y1), decay[:, 1:2].to_broadcast([P, N]), flat(y0), 0.0, ALU.mult, ALU.add))
            v.tensor_tensor(flat(y0), flat(y1), rotx[:, 1:N + 1], ALU.mult).then_inc(sem("rotated_back"), 1)
            signal(v.tensor_tensor(flat(xn), flat(y1), roty[:, 1:N + 1], ALU.mult), "rotated_back", 2)
            for g in range(4):
                s = slice(4 * g, 4 * g + 4)
                v.wait_ge(sem("modes_out"), g + 1)
                then(v.tensor_tensor(y1[:, s, :], ps[:, 2 + g, :].rearrange("p (j c) -> p j c", c=D), rowwise(modrow[1][:, GA, :], 4), ALU.mult))
                then(v.tensor_tensor(x[:, s, :], x[:, s, :], y1[:, s, :], ALU.add))
            layernorm(x, xn, 0, NT)
            then(v.tensor_tensor(y0[:], xn[:], rowwise(modrow[1][:, CB, :], NT), ALU.mult))
            signal(v.tensor_tensor(y0[:], y0[:], rowwise(modrow[1][:, SB, :], NT), ALU.add), "rows_ready1f", 1)
            layernorm(y0, xn, 0, NT, "rows_all")
            read_logits("all")
            choose("all")
            read_counts("all")
            place("all")
            gates("all")
            experts(1)
            add_ffn("all", 1)


_OUT = ("out", (1, N, D))
_SCRATCH = (("rows0", (T0 * P, D)), ("rows1", (T1 * P, D)), ("back0", (T0 * P, D)), ("back1", (T1 * P, D)))


def kernel(**inputs):
    import concourse.bacc as bacc
    from concourse.bass_utils import run_bass_kernel_spmd

    nc = bacc.Bacc("TRN2", target_bir_lowering=False, num_devices=1)
    arrays, aps = {}, {}
    for name, value in inputs.items():
        a = np.ascontiguousarray(value)
        if a.ndim == 0:
            a = a.reshape(1)
        arrays["in_" + name] = a
        aps[name] = nc.dram_tensor("in_" + name, a.shape, mybir.dt.from_np(a.dtype), kind="ExternalInput").ap()
    out = nc.dram_tensor(_OUT[0], _OUT[1], F32, kind="ExternalOutput").ap()
    scratch = [nc.dram_tensor(name, shape, F32, kind="Internal").ap() for name, shape in _SCRATCH]
    build_adaln(nc, aps, out, *scratch)
    r = run_bass_kernel_spmd(nc, [arrays], core_ids=[0])
    return r.results[0][_OUT[0]]
```

```python
from contextlib import ExitStack

import numpy as np
import concourse.bass as bass
from concourse import mybir

F32 = mybir.dt.float32
BF16 = mybir.dt.bfloat16
I32 = mybir.dt.int32
U32 = mybir.dt.uint32
ALU = mybir.AluOpType
ACT = mybir.ActivationFunctionType
AX = mybir.AxisListType

P = 128
D = 128
N = 2048
NT = N // P
HEADS, HD = 16, 8
NE, HID = 8, 512
NB = HID // P
NF = 32
LN_EPS = 1e-5

W0 = 256


def _up(w):
    return int(np.float32(w) * np.float32(1.1))


def _down(w):
    return int(np.float32(w) * np.float32(0.9))


WINDOWS = [W0, _up(W0), _up(_up(W0))]
WMIN = _down(_down(W0))
NA = -(-WINDOWS[2] // P)
NATT = NA * P
MASKED = -1e30
RSQRT_MAGIC = float(0x5F3759DF)

def tiles_bound(rows):
    return (rows + NE * (P - 1)) // P


GROUPS = {"far": (NA, NT, 2), "near": (0, NA, 2), "all": (0, NT, 1)}
TFAR = tiles_bound(2 * (N - NATT))
TNEAR = tiles_bound(2 * NATT)
T0 = TFAR + TNEAR
T1 = tiles_bound(N)
SORTED = {"far": (0, TFAR), "near": (TFAR, T0), "all": (0, T1)}
TMAX = 48
CHUNKS = {"far": [(a, min(a + 4, NT)) for a in range(NA, NT, 4)], "near": [(0, NA)],
          "all": [(a, a + 4) for a in range(0, NT, 4)]}
ARRIVAL = CHUNKS["far"] + CHUNKS["near"]
RING = 4
REST = D + 2
ROW1 = D + REST

SLOT = 8
STK = 64
OROW = 32
Q_FIRST = {0: 1, 1: 4, 2: 6}
K_FIRST = {0: 1, 1: 2, 2: 3}
Q_COPIES = [(1, 2), (1, 3), (4, 5)]
K_COPIES = [(1, 4), (2, 5), (1, 6)]

ROW_C0, ROW_C1, ROW_BQ, ROW_BV, ROW_LNA, ROW_LNB, ROW_G, ROW_B, ROW_ROUTER = 0, 1, 2, 3, 4, 5, 6, 7, 8
NROW = ROW_ROUTER + NE
SA, CA, GA, SB, CB, GB = range(6)

TWO_PI = 2 * np.pi
TP1 = 6.28125
TP2 = float(np.float32(round((TWO_PI - TP1) * 2 ** 21) / 2 ** 21))
TP3 = float(np.float32(TWO_PI - TP1 - TP2))


def build_adaln(nc, A, out, rows0, rows1, back0):
    ctx = ExitStack()
    with ctx:
        def sb(name, shape, dt=F32):
            return ctx.enter_context(nc.sbuf_tensor(name, shape, dt))

        sems = {}

        def sem(name):
            if name not in sems:
                sems[name] = ctx.enter_context(nc.semaphore(name))
            return sems[name]

        token_rows = sb("token_rows", [P, NT, ROW1])
        xn = token_rows[:, :, 0:D]
        x = token_rows[:, :, D:2 * D]
        feat = sb("feat", [P, HEADS * NATT // 2])
        hT = feat[:, 0:N]
        y0 = sb("y0", [P, NT, D])
        wide = sb("wide", [P, 2 * NA * NATT])
        y1 = wide[:, 0:N].rearrange("p (j c) -> p j c", c=D)
        w_in = sb("w_in", [P, NE, HID])
        w_out = sb("w_out", [P, NE * NB, D])
        b_inr = sb("b_inr", [NE * NB, 2, P])
        b_in = sb("b_in", [P, 2, NE, NB])
        b_out = sb("b_out", [P, NE, D])
        ident = sb("ident", [P, P])
        identb = sb("identb", [P, P], BF16)
        ones = sb("ones", [P, P])
        onesb = sb("onesb", [P, P], BF16)
        before = sb("before", [P, P], BF16)
        zeros = sb("zeros", [P, 512])
        rows = sb("rows", [NROW, P])
        cols = sb("cols", [P, NROW])
        wmod = sb("wmod", [P, 2, 6 * D])
        modrow = [sb(f"modrow{l}", [P, 6, D]) for l in range(2)]
        modcol = [sb(f"modcol{l}", [P, 6]) for l in range(2)]
        silu = sb("silu", [P, 3, 2])
        siluw = sb("siluw", [P, 2, P])
        gsign = sb("gsign", [P, 2, D])
        stats = sb("stats", [P, NT, 6])
        mv = sb("mv", [P, NT, 2])
        rstd = sb("rstd", [P, NT])
        nmr = sb("nmr", [P, NT])
        rs_v = sb("rs_v", [P, 48])
        rs_a = sb("rs_a", [P, 48])
        rs_y = sb("rs_y", [P, 48])
        wnat = sb("wnat", [P, 4, D])
        wT = sb("wT", [P, 4, D])
        ln = sb("ln", [3 * HD, HD])
        lT = sb("lT", [HD, 3 * HD])
        lmean = sb("lmean", [P, 2])
        pick = sb("pick", [HD, HEADS, HD])
        blockm = sb("blockm", [P, HEADS, HD])
        bd = sb("bd", [P, 3, HEADS, HD])
        small = sb("small", [P, 5, HD])
        scal = sb("scal", [P, 3])
        bo_row = sb("bo_row", [P, D])
        br_row = sb("br_row", [P, NE])
        ah = sb("ah", [P, NA, D])
        ahn = sb("ahn", [P, NA, D])
        n2T = sb("n2T", [P, NATT])
        qT = sb("qT", [P, NATT])
        kT = sb("kT", [P, NATT])
        vT = sb("vT", [P, NATT])
        gl_c = sb("gl_c", [P, NA * HEADS, HD])
        gl_s = sb("gl_s", [P, NA * HEADS, HD])
        gl_m = sb("gl_m", [P, NA * HEADS])
        stack = sb("stack", [P, NA * HEADS, STK], BF16)
        qs = sb("qs", [P, HEADS // 2, NATT], BF16)
        ks = feat[:].bitcast(BF16).rearrange("p (h n) -> p h n", h=HEADS)
        vpx = sb("vpx", [P, NA, HEADS, HD + 1])
        probs = wide[:].rearrange("p (b j n) -> p b j n", b=2, j=NA)
        v_now = sb("v_now", [P, 4, NA, OROW])
        oT = wmod[:].rearrange("p l c -> p (l c)").rearrange("p (g n) -> p g n", g=HEADS // 4)
        mx = sb("mx", [P, NA, HEADS])
        mr = sb("mr", [P, NA * HEADS])
        den = sb("den", [P, NA * HEADS])
        att = [sb(f"att{i}", [P, NA, D]) for i in range(3)]
        att_d = sb("att_d", [P, NA * D])
        asum = sb("asum", [P, 1])
        diff = sb("diff", [P, 2])
        flags = sb("flags", [P, 8])
        cw = sb("cw", [P, 3])
        tsc = sb("tsc", [P, 8])
        kidx_i = sb("kidx_i", [P, NATT], I32)
        kidx = sb("kidx", [P, NATT])
        ridx = sb("ridx", [P, NA])
        rowm = sb("rowm", [P, NA])
        lg = sb("lg", [P, NT, NE])
        lg2 = sb("lg2", [P, NT, NE])
        cand = sb("cand", [P, NT, NE])
        first = [sb(f"first{k}", [P, NT, NE]) for k in range(2)]
        top = sb("top", [P, 3, NT])
        gate = sb("gate", [P, 2, NT])
        chosen = sb("chosen", [P, NT, NE], BF16)
        e_rank = sb("e_rank", [P, NE])
        tot_f = sb("tot", [P, NE * NT])
        inc_f = sb("inc", [P, NE * NT])
        keep = {g: sb(f"keep_{g}", [P, NE, hi - lo]) for g, (lo, hi, _) in GROUPS.items()}
        pose = sb("pose", [P, NT, NE])
        step128 = sb("step128", [P, NT])
        cmp_f = sb("cmp_t", [P, NE * NT])
        ntile = sb("ntile", [P, NE])
        tend = sb("tend", [P, NE])
        tbase = sb("tbase", [P, NE])
        posf = sb("posf", [P, NT])
        posu = sb("posu", [P, 2, NT], U32)
        tidx = sb("tidx", [P, TMAX])
        cmp_e = sb("cmp_e", [P, TMAX, NE])
        eidf = sb("eidf", [P, TMAX])
        eid = sb("eid", [P, TMAX], I32)
        xs = sb("xs", [P, RING, D])
        rest = sb("rest", [P, RING, REST])
        target = sb("target", [P, RING], U32)
        xsT = sb("xsT", [P, 2, P])
        w_now = sb("w_now", [P, 2, HID])
        hb = sb("hb", [P, 2, HID])
        hg = sb("hg", [P, RING, HID])
        hTr = hg[:, 2:4, :]
        ys = sb("ys", [P, RING, D])
        rotx = sb("rotx", [P, N + 1])
        roty = sb("roty", [P, N + 1])
        win_n = sb("win_n", [P, D])
        winT = sb("winT", [P, D])
        wo_s = sb("wo_s", [P, 2 * NF])
        wo_n = sb("wo_n", [P, 2, 4 * NF])
        wrl = sb("wrl", [P, NE])
        tmp_c = y0[:].rearrange("p j c -> p (j c)")[:, 0:N // 2]
        tmp_s = y0[:].rearrange("p j c -> p (j c)")[:, N // 2:N]
        turn = sb("turn", [P, 8])
        wox = sb("wox", [P, D])
        woy = sb("woy", [P, D])
        fcol = sb("fcol", [P, 2])
        ph = sb("ph", [P, 12])
        phi = sb("phi", [P, 4], I32)
        decay = sb("decay", [P, 2])

        ps = ctx.enter_context(nc.psum_tensor("ps", [P, 8, 512], F32))
        psb = ps[:].bitcast(BF16)

        block = ctx.enter_context(nc.Block())

        def load(eng, dst, src, what):
            eng.dma_start(dst, src).then_inc(sem("ld_" + what), 16)

        def col(ap):
            return ap.rearrange("(a n) -> a n", a=1)

        x_tiles = A["L0_attn_x"].rearrange("a (j p) c -> p (a j) c", p=P)
        out_rows = out.rearrange("a n c -> (a n) c")
        NTILE = {0: T0, 1: T1}
        ROWS = {0: rows0, 1: rows1}
        TURN_BANK = {"far": 0, "near": 3}

        def tiles_before(l):
            return T0 if l else 0

        def earlier(l, r):
            return len(range(r, T0, RING)) if l else 0

        WIDTH = {0: D, 1: ROW1}

        def load_experts(eng, l):
            names = (("L0_ffn_w_fc", "L0_ffn_w_proj", "L0_ffn_b_proj"), ("L1_ffn_W1", "L1_ffn_W2", "L1_ffn_b2"))[l]
            eng.dma_start(w_in[:], A[names[0]].rearrange("e c h -> c e h")).then_inc(sem(f"ld_experts{l}"), 16)
            eng.dma_start(w_out[:], A[names[1]].rearrange("e (b p) c -> p (e b) c", p=P)).then_inc(sem(f"ld_experts{l}"), 16)
            eng.dma_start(b_out[:], A[names[2]].partition_broadcast(P)).then_inc(sem(f"ld_experts{l}"), 16)

        def clear_rows(eng, l):
            flat = ROWS[l].rearrange("(p r) c -> p (r c)", p=P)
            left, at = flat.shape[1], 0
            while left:
                n = min(left, 512)
                eng.dma_start(flat[:, at:at + n], zeros[:, 0:n]).then_inc(sem(f"cleared{l}"), 16)
                at, left = at + n, left - n

        def clears(l):
            return -(-NTILE[l] * WIDTH[l] // 512)

        @block.sync
        def _(sp):
            load(sp, x[:, 0:NA, :], x_tiles[:, 0:NA, :], "x_attn")
            for r, a in ((ROW_C0, A["L0_c"]), (ROW_C1, A["L1_c"]), (ROW_BQ, col(A["L0_attn_bq"])),
                         (ROW_BV, col(A["L0_attn_bv"])), (ROW_LNA, col(A["L0_attn_lna_w"])),
                         (ROW_LNB, col(A["L0_attn_lnb_w"])), (ROW_G, col(A["L1_ffn_ln_g"])),
                         (ROW_B, col(A["L1_ffn_ln_b"]))):
                load(sp, rows[r:r + 1, :], a, "rows")
            load(sp, rows[ROW_ROUTER:NROW, :], A["L0_ffn_router_w"], "rows")
            load(sp, wmod[:, 0, :], A["L0_wmod"], "wmod0")
            for k, w in enumerate(("Wq", "Wk", "Wv", "Wo")):
                load(sp, wnat[:, k, :], A["L0_attn_" + w], "wnat")
            for k, name in enumerate(("lq_b", "lk_b", "lv_b", "lnc_w", "lnd_w")):
                load(sp, small[:, k, :], A["L0_attn_" + name].partition_broadcast(P), "small")
            for f in range(4):
                load(sp, fcol[f * NF:(f + 1) * NF, 0:1], A["L1_attn_frequencies"].rearrange("(n a) -> n a", a=1), "recur")
                load(sp, fcol[f * NF:(f + 1) * NF, 1:2], A["L1_attn_log_decay"].rearrange("(n a) -> n a", a=1), "recur")
            for f, r in enumerate((0, 1, 1, 0)):
                load(sp, win_n[f * NF:(f + 1) * NF, :], A["L1_attn_W_in"][r * NF:(r + 1) * NF, :], "recur")
            load(sp, wo_s[:], A["L1_attn_W_out"], "recur")
            load(sp, wrl[:], A["L1_ffn_Wr"], "recur")
            for l, name in enumerate(("L0_ffn_b_fc", "L1_ffn_b1")):
                load(sp, b_inr[:, l, :], A[name].rearrange("e (b p) -> (e b) p", p=P), "recur")
            load(sp, wmod[:, 1, :], A["L1_wmod"], "wmod1")
            load(sp, x[:, NA:NT, :], x_tiles[:, NA:NT, :], "x_rest")
            sp.wait_ge(sem("zeros_set"), 1)
            clear_rows(sp, 0)
            clear_rows(sp, 1)
            load_experts(sp, 0)

            def sorted_tiles(l):
                T = NTILE[l]
                src = ROWS[l].rearrange("(t p) c -> p t c", p=P)
                dst = back0.rearrange("(t p) c -> p t c", p=P)

                def load_tile(k, c):
                    sp.dma_start(xs[:, c % RING, :], src[:, bass.ds(RING * k + c, 1), 0:D]).then_inc(
                        sem(f"xs_loaded{c % RING}"), 16)

                def store_tile(k, c):
                    sp.dma_start(dst[:, bass.ds(RING * k + c, 1), :], ys[:, c % RING, :]).then_inc(
                        sem(f"ys_stored{c % RING}"), 16)

                def load_rest(k, c):
                    sp.dma_start(rest[:, c % RING, :], src[:, bass.ds(RING * k + c, 1), D:ROW1]).then_inc(
                        sem(f"rest_loaded{c % RING}"), 16)

                def step(k, c):
                    sp.wait_ge(sem("xs_used"), RING * k + (c + 1) + tiles_before(l))
                    load_tile(k, c + RING)

                def finish(k, c):
                    sp.wait_ge(sem("ys_ready"), RING * k + (c + 1) + tiles_before(l))
                    if l == 0:
                        store_tile(k, c)
                    else:
                        load_rest(k + 1, c)

                def rounds(lo, hi):
                    with sp.Fori(lo, hi) as k:
                        for c in range(RING):
                            step(k, c)
                            finish(k - 1, c)

                def wait_scattered(g):
                    lo, hi, experts = GROUPS[g]
                    sp.wait_ge(sem("scattered_" + g), 16 * (hi - lo) * experts)

                wait_scattered(("far", "all")[l])
                for c in range(RING):
                    load_tile(0, c)
                    if l:
                        load_rest(0, c)
                for c in range(RING):
                    step(0, c)
                whole = (T - RING) // RING
                if l == 0:
                    turn = (TFAR - RING) // RING
                    rounds(1, turn)
                    wait_scattered("near")
                    rounds(turn, whole)
                else:
                    rounds(1, whole)
                for t in range(RING * whole, T + RING * (1 - l)):
                    if t + RING < T:
                        step(0, t)
                    finish(0, t - RING)

            sorted_tiles(0)
            sp.wait_ge(sem("ys_ready"), T0)
            sp.wait_ge(sem("gathered_near0"), 16 * NA * 2)
            load_experts(sp, 1)
            sorted_tiles(1)

        @block.gpsimd
        def _(pool):
            pool.memset(zeros[:], 0.0).then_inc(sem("zeros_set"), 1)
            pool.memset(ident[:], 0.0).then_inc(sem("p_fill"), 1)
            pool.memset(ones[:], 1.0).then_inc(sem("p_fill"), 1)
            pool.memset(blockm[:], 1.0).then_inc(sem("p_fill"), 1)
            pool.memset(pick[:], 0.0).then_inc(sem("p_fill"), 1)
            for g in GROUPS:
                pool.memset(keep[g][:], 1.0).then_inc(sem("p_fill"), 1)
            pool.memset(ks[:, :, :], 0.0).then_inc(sem("ks_zero"), 1)
            pool.wait_ge(sem("p_fill"), 4 + len(GROUPS))
            pool.affine_select(out=ident[:], in_=ident[:], compare_op=ALU.not_equal, fill=1.0, base=0,
                               pattern=[[-1, P]], channel_multiplier=1).then_inc(sem("ident_set"), 1)
            pool.affine_select(out=pick[:], in_=pick[:], compare_op=ALU.not_equal, fill=1.0, base=0,
                               pattern=[[0, HEADS], [-1, HD]], channel_multiplier=1).then_inc(sem("pick_set"), 1)
            pool.affine_select(out=blockm[:], in_=blockm[:], compare_op=ALU.is_ge, fill=0.0, base=0,
                               pattern=[[-HD, HEADS], [0, HD]], channel_multiplier=1).then_inc(sem("p_block"), 1)
            pool.wait_ge(sem("p_block"), 1)
            pool.affine_select(out=blockm[:], in_=blockm[:], compare_op=ALU.is_ge, fill=0.0, base=HD - 1,
                               pattern=[[HD, HEADS], [0, HD]], channel_multiplier=-1).then_inc(sem("pick_set"), 1)
            pool.affine_select(out=before[:], in_=ones[:], compare_op=ALU.is_gt, fill=0.0, base=0,
                               pattern=[[1, P]], channel_multiplier=-1).then_inc(sem("tables_set"), 1)
            for g, (lo, hi, _) in GROUPS.items():
                pool.affine_select(out=keep[g][:], in_=keep[g][:], compare_op=ALU.is_gt, fill=0.0, base=0,
                                   pattern=[[0, NE], [1, hi - lo]], channel_multiplier=0).then_inc(sem("tables_set"), 1)
            pool.iota(kidx_i[:], pattern=[[1, NATT]], base=0, channel_multiplier=0).then_inc(sem("kidx_set"), 1)
            exact = dict(allow_small_or_imprecise_dtypes=True)
            pool.iota(ridx[:], pattern=[[P, NA]], base=0, channel_multiplier=1, **exact).then_inc(sem("kidx_set"), 1)
            pool.iota(e_rank[:], pattern=[[-1, NE]], base=NE, channel_multiplier=0, **exact).then_inc(sem("tables_set"), 1)
            pool.iota(step128[:], pattern=[[P, NT]], base=0, channel_multiplier=0, **exact).then_inc(sem("tables_set"), 1)
            pool.iota(token_rows[:, :, ROW1 - 1], pattern=[[P, NT]], base=-N, channel_multiplier=1, **exact).then_inc(sem("tables_set"), 1)
            pool.iota(tidx[:], pattern=[[1, TMAX]], base=0, channel_multiplier=0, **exact).then_inc(sem("tables_set"), 1)

            for k, name in enumerate(("threshold", "factor", "temp_base")):
                load(pool, scal[:, k:k + 1], A["L0_attn_" + name].partition_broadcast(P), "scalars")
            load(pool, bo_row[:], A["L0_attn_bo"].partition_broadcast(P), "scalars")
            load(pool, br_row[:], A["L1_ffn_br"].partition_broadcast(P), "scalars")

            def scatter_rows(g, l):
                lo, hi, experts = GROUPS[g]
                pool.wait_ge(sem("slots_" + g), 1)
                pool.wait_ge(sem("rows_" + g), len(CHUNKS[g]) if l else 1)
                if l:
                    pool.wait_ge(sem("gates_all"), 1)
                pool.wait_ge(sem(f"cleared{l}"), 16 * clears(l))
                for j in range(lo, hi):
                    for k in range(experts):
                        pool.indirect_dma_start(ROWS[l], bass.IndirectOffsetOnAxis(ap=posu[:, k, j:j + 1], axis=0),
                                                token_rows[:, j, 0:WIDTH[l]], None).then_inc(sem("scattered_" + g), 16)

            def gather_rows(g):
                for r in range(RING):
                    pool.wait_ge(sem(f"ys_stored{r}"), 16 * len(range(r, SORTED[g][1], RING)))
                for q, (lo, hi) in enumerate(CHUNKS[g]):
                    for j in range(lo, hi):
                        for k in range(GROUPS[g][2]):
                            pool.indirect_dma_start((y0, y1)[k][:, j, :], None, back0[0:SORTED[g][1] * P, :],
                                                    bass.IndirectOffsetOnAxis(ap=posu[:, k, j:j + 1], axis=0)
                                                    ).then_inc(sem(f"gathered_{g}{q}"), 16)

            steps = [0]

            def then(ins):
                steps[0] += 1
                ins.then_inc(sem("p_step"), 1)
                pool.wait_ge(sem("p_step"), steps[0])

            H = P // 2
            pool.wait_ge(sem("mod_made"), 2)
            pool.memset(oT, 0.0).then_inc(sem("oT_clear"), 1)
            pool.wait_ge(sem("tables_set"), 5 + len(GROUPS))
            then(pool.memset(rotx[0:H, 0:1], 1.0))
            then(pool.memset(rotx[H:P, 0:1], 0.0))
            then(pool.memset(roty[0:H, 0:1], 0.0))
            then(pool.memset(roty[H:P, 0:1], -1.0))
            pool.wait_ge(sem("sines"), 1)
            then(pool.tensor_copy(turn[:, 0:1], ph[:, 7:8]))
            then(pool.tensor_copy(turn[:, 1:2], ph[:, 6:7]))
            c_, s_, cc, ss, t_ = (turn[:, k:k + 1] for k in range(5))

            def unit():
                then(pool.tensor_tensor(cc, c_, c_, ALU.mult))
                then(pool.tensor_tensor(ss, s_, s_, ALU.mult))
                then(pool.tensor_tensor(t_, cc, ss, ALU.add))
                then(pool.tensor_scalar(t_, t_, -0.5, 1.5, ALU.mult, ALU.add))
                then(pool.tensor_tensor(c_, c_, t_, ALU.mult))
                then(pool.tensor_tensor(s_, s_, t_, ALU.mult))

            unit()
            L = 1
            while L <= N:
                n = min(L, N + 1 - L)
                X, Y, tc, ts = rotx[:, 0:n], roty[:, 0:n], tmp_c[:, 0:n], tmp_s[:, 0:n]
                pool.tensor_scalar(tc, X, c_, None, ALU.mult)
                then(pool.tensor_scalar(ts, Y, s_, None, ALU.mult))
                then(pool.tensor_tensor(rotx[:, L:L + n], tc, ts, ALU.subtract))
                pool.tensor_scalar(tc, X, s_, None, ALU.mult)
                then(pool.tensor_scalar(ts, Y, c_, None, ALU.mult))
                ins = pool.tensor_tensor(roty[:, L:L + n], tc, ts, ALU.add)
                L *= 2
                if L > N:
                    ins.then_inc(sem("rotations"), 1)
                    break
                then(ins)
                then(pool.tensor_tensor(cc, c_, c_, ALU.mult))
                then(pool.tensor_tensor(ss, s_, s_, ALU.mult))
                then(pool.tensor_tensor(t_, c_, s_, ALU.mult))
                then(pool.tensor_tensor(c_, cc, ss, ALU.subtract))
                then(pool.tensor_tensor(s_, t_, t_, ALU.add))
                unit()
            pool.wait_ge(sem("rotations"), 1)

            def gate_weights(l):
                pool.wait_ge(sem(f"ld_experts{l}"), 48)
                pool.wait_ge(sem("gates_clamped"), l + 1)
                gb = modrow[l][:, GB, :].unsqueeze(1)
                pool.tensor_tensor(w_out[:], w_out[:], gb.to_broadcast([P, NE * NB, D]), ALU.mult).then_inc(sem("out_gated"), 1)
                pool.tensor_tensor(b_out[:], b_out[:], gb.to_broadcast([P, NE, D]), ALU.mult).then_inc(sem("out_gated"), 1)

            gate_weights(0)
            scatter_rows("far", 0)
            scatter_rows("near", 0)
            gather_rows("far")
            gather_rows("near")
            gate_weights(1)
            scatter_rows("all", 1)

            for t in range(T1):
                r = t % RING
                pool.wait_ge(sem("ys_ready"), t + 1 + tiles_before(1))
                pool.indirect_dma_start(out_rows, bass.IndirectOffsetOnAxis(ap=target[:, r:r + 1], axis=0),
                                        ys[:, r, :], None, bounds_check=N - 1, oob_is_err=False
                                        ).then_inc(sem(f"ys_sent{r}"), 16)
            for r in range(RING):
                pool.wait_ge(sem(f"ys_sent{r}"), 16 * len(range(r, T1, RING)))

        @block.scalar
        def _(act):
            for k, name in enumerate(("lq_w", "lk_w", "lv_w")):
                load(act, ln[k * HD:(k + 1) * HD, :], A["L0_attn_" + name], "lmaps")

            act.wait_ge(sem("cols_set"), 1)
            act.activation(silu[:, 0, :], cols[:, 0:2], ACT.Exp, scale=-1.0).then_inc(sem("silu_exp"), 1)
            act.wait_ge(sem("qkv"), 1)
            act.activation(kT[:], ps[:, 1, 0:NATT], ACT.Copy, scale=float(HD ** -0.25)).then_inc(sem("kT"), 1)
            act.wait_ge(sem("qkv"), 3)
            act.activation(vT[:], ps[:, 3, 0:NATT], ACT.Identity, bias=cols[:, ROW_BV:ROW_BV + 1]).then_inc(sem("vT"), 1)
            act.wait_ge(sem("mod_made"), 2)
            mr_f = modrow[1][:].rearrange("p a c -> p (a c)")
            act.copy(mr_f[:, 0:512], ps[:, 1, :]).then_inc(sem("late_read"), 1)
            act.copy(mr_f[:, 512:768], ps[:, 2, 0:256]).then_inc(sem("late_read"), 1)
            act.copy(modcol[1][:], ps[:, 3, 0:6]).then_inc(sem("late_read"), 1)
            act.wait_ge(sem("t_recur"), 1)
            for k, t in enumerate((winT, wox, woy)):
                act.copy(t[:], ps[:, 0, k * D:(k + 1) * D]).then_inc(sem("late_read"), 1)
            act.copy(b_in[:].rearrange("p l e b -> p (l e b)"), ps[:, 0, 3 * D:3 * D + 2 * NE * NB]).then_inc(sem("late_read"), 1)
            act.wait_ge(sem("ks_zero"), 1)
            for g in range(4):
                act.wait_ge(sem("kstackT"), g + 1)
                act.copy(ks[STK:P, 4 * g + 1:4 * g + 4:2, :], psb[STK:P, g, 0:2 * NATT].rearrange("p (a n) -> p a n", a=2)
                         ).then_inc(sem("ks_odd"), 1)

            def softmax_exp(it):
                nj, nw = -(-WINDOWS[it] // P), WINDOWS[it]

                def head(i, q):
                    h = 4 * i + q
                    b = q % 2
                    act.wait_ge(sem("probs_free"), 4 * i + (HEADS * it + q + 1))
                    act.copy(v_now[:, q, :, 0:HD + 1], vpx[:, :, bass.ds(h, 1), :])
                    act.wait_ge(sem("st_ready"), 4 * i + (HEADS * it + q + 1))
                    act.activation(probs[:, b, 0:nj, 0:nw], ps[:, 3 * b:3 * b + nj, 0:nw], ACT.Exp
                                   ).then_inc(sem("probs_ready"), 1)

                def take(i):
                    act.wait_ge(sem("probs_free"), 4 * i + (HEADS * it + 6))
                    act.wait_ge(sem("oT_clear"), 1)
                    act.copy(oT[:, bass.ds(i, 1), 0:nw], ps[:, 6, 0:nw]).then_inc(sem("o_taken"), 1)

                for q in range(4):
                    head(0, q)
                with act.Fori(0, HEADS // 4 - 1) as i:
                    head(i + 1, 0)
                    take(i)
                    for q in range(1, 4):
                        head(i + 1, q)
                take(HEADS // 4 - 1)

            def stack_copies(n, nj):
                for g in (1, 3):
                    act.wait_ge(sem("stackT"), 4 * n + g + 1)
                    act.copy(qs[:, 2 * g:2 * g + 2, 0:nj * P], psb[:, g, 0:2 * NATT].rearrange("p (a n) -> p a n", a=2)[:, :, 0:nj * P]
                             ).then_inc(sem("qs_act"), 1)

            def router_rows(g):
                lo, hi, _ = GROUPS[g]
                for q in range(-(-(hi - lo) // 4)):
                    n = min(4, hi - lo - 4 * q) * P
                    act.wait_ge(sem("turned_" + g), q + 1)
                    if q >= 2:
                        act.wait_ge(sem("hT_used_" + g), q - 1)
                    act.activation(hTr[:, q % 2, 0:n], ps[:, TURN_BANK[g] + q % 2, 0:n], ACT.Identity, scale=modcol[0][:, CB:CB + 1],
                                   bias=modcol[0][:, SB:SB + 1]).then_inc(sem("hT_" + g), 1)

            def gap_exp(g):
                lo, hi, _ = GROUPS[g]
                act.wait_ge(sem("top_gap_" + g), 1)
                act.activation(top[:, 2, lo:hi], top[:, 2, lo:hi], ACT.Exp).then_inc(sem("gap_exp_" + g), 1)

            for it in range(3):
                if it == 1:
                    act.wait_ge(sem("angles"), 1)
                    act.activation(ph[:, 6:8], ph[:, 4:6], ACT.Sin).then_inc(sem("sines"), 1)
                    act.activation(decay[:, 0:1], fcol[:, 1:2], ACT.Exp, scale=-1.0).then_inc(sem("decay_exp"), 1)
                    router_rows("far")
                if it == 2:
                    gap_exp("far")
                stack_copies(2 * it, -(-WINDOWS[it] // P))
                stack_copies(2 * it + 1, -(-WINDOWS[it] // P))
                softmax_exp(it)

            def normalise(dst, src, lo, hi, done):
                for j in range(lo, hi):
                    ins = act.activation(dst[:, j, :], src[:, j, :], ACT.Identity, scale=rstd[:, j:j + 1], bias=nmr[:, j:j + 1])
                ins.then_inc(sem(done), 1)

            def experts(l):
                T = NTILE[l]
                fn = (ACT.Gelu_apprx_tanh, ACT.Relu)[l]
                sc, bi = ((modcol[0][:, CB:CB + 1], modcol[0][:, SB:SB + 1]),
                          (cols[:, ROW_G:ROW_G + 1], cols[:, ROW_B:ROW_B + 1]))[l]

                def modulate(k, c):
                    t = RING * k + c
                    act.wait_ge(sem("xs_used"), t + 1 + tiles_before(l))
                    if not isinstance(t, int) or t >= 2:
                        act.wait_ge(sem("h_ready"), t - 1 + tiles_before(l))
                    act.activation(xsT[:, c % 2, :], ps[:, 4 + c % 2, 0:P], ACT.Identity, scale=sc, bias=bi
                                   ).then_inc(sem("xsT_ready"), 1)

                def nonlinear(k, c):
                    t = RING * k + c
                    act.wait_ge(sem("hb_ready"), t + 1 + tiles_before(l))
                    if not isinstance(t, int) or t >= RING:
                        act.wait_ge(sem("o_ready"), t - (RING - 1) + tiles_before(l))
                    act.activation(hg[:, c % RING, :], hb[:, c % 2, :], fn).then_inc(sem("hg_ready"), 1)

                modulate(0, 0)
                modulate(0, 1)
                if l == 0:
                    router_rows("near")
                    nonlinear(0, 0)
                    nonlinear(0, 1)
                    modulate(0, 2)
                    modulate(0, 3)
                else:
                    for c in (0, 1):
                        modulate(0, c + 2)
                        nonlinear(0, c)
                for c in (2, 3):
                    modulate(0, c + 2)
                    nonlinear(0, c)
                rounds = (T - 2) // RING
                with act.Fori(1, rounds) as k:
                    for c in range(RING):
                        modulate(k, c + 2)
                        nonlinear(k, c)
                for t in range(RING * rounds, T):
                    if t + 2 < T:
                        modulate(0, t + 2)
                    nonlinear(0, t)

            experts(0)
            def turned_a(q):
                lo, hi = ARRIVAL[q]
                act.wait_ge(sem("turned1a"), q + 1)
                act.activation(hT[:, lo * P:hi * P], ps[:, q % 2, 0:(hi - lo) * P], ACT.Identity, scale=modcol[1][:, CA:CA + 1],
                               bias=modcol[1][:, SA:SA + 1]).then_inc(sem("hT1a"), 1)

            def gated(q, name):
                lo, hi = ARRIVAL[q]
                act.wait_ge(sem("gathered_" + name), 16 * (hi - lo) * 2)
                for k, y in enumerate((y0, y1)):
                    for j in range(lo, hi):
                        ins = act.activation(y[:, j, :], y[:, j, :], ACT.Copy, scale=gate[:, k, j:j + 1])
                ins.then_inc(sem("gated"), 1)

            nfar = len(CHUNKS["far"])
            gap_exp("near")
            act.wait_ge(sem("gates_near"), 1)
            for q in range(nfar):
                gated(q, f"far{q}")
            act.wait_ge(sem("stats_a"), 1)
            normalise(xn, x, *ARRIVAL[0], "rows1a")
            gated(nfar, "near0")
            for q in range(1, nfar):
                normalise(xn, x, *ARRIVAL[q], "rows1a")
                turned_a(q - 1)
            turned_a(nfar - 1)
            act.wait_ge(sem("stats_a"), 2)
            normalise(xn, x, *ARRIVAL[nfar], "rows1a")
            turned_a(nfar)
            act.wait_ge(sem("stats_f"), 1)
            for lo, hi in CHUNKS["all"]:
                normalise(y0, x, lo, hi, "normed1f")
            for q in range(NT // 4):
                act.wait_ge(sem("turned1f"), q + 1)
                act.copy(hT[:, 512 * q:512 * q + 512], ps[:, q % 2, :]).then_inc(sem("hT1f"), 1)
            act.wait_ge(sem("stats_f"), 2)
            for lo, hi in CHUNKS["all"]:
                normalise(xn, y0, lo, hi, "rows_all")
            act.wait_ge(sem("lg_shifted"), 1)
            act.activation(lg2[:], lg2[:], ACT.Exp).then_inc(sem("lg_exp"), 1)
            experts(1)

        @block.tensor
        def _(pe):
            pe.wait_ge(sem("ident_set"), 1)
            pe.wait_ge(sem("ld_rows"), 16 * 9)
            pe.transpose(ps[:, 0, 0:NROW], rows[:], ident[0:NROW, 0:NROW]).then_inc(sem("t_cols"), 1)

            def modulation(l, b0, b1, b2):
                pe.wait_ge(sem(f"ld_wmod{l}"), 16)
                pe.matmul(ps[:, b0, :], siluw[:, l, :], wmod[:, l, 0:512], start=True, stop=True).then_inc(sem("mod_first"), 1)
                for c in range(6):
                    pe.matmul(ps[:, b2, c:c + 1], wmod[:, l, c * D:(c + 1) * D], silu[:, 2, l:l + 1],
                              start=True, stop=True)
                pe.matmul(ps[:, b1, 0:256], siluw[:, l, :], wmod[:, l, 512:768], start=True, stop=True
                          ).then_inc(sem("mod_made"), 1)

            pe.wait_ge(sem("ld_lmaps"), 48)
            pe.transpose(ps[0:HD, 2, 64:64 + 3 * HD], ln[:], ident[0:3 * HD, 0:3 * HD]).then_inc(sem("t_lT"), 1)
            pe.wait_ge(sem("silu_set"), 1)
            modulation(0, 3, 4, 5)
            pe.wait_ge(sem("ld_wnat"), 64)
            for k in range(4):
                mm = pe.transpose(ps[:, 1, k * D:(k + 1) * D], wnat[:, k, :], ident[:])
            mm.then_inc(sem("t_wT"), 1)
            pe.wait_ge(sem("pick_set"), 2)
            pe.wait_ge(sem("lT_set"), 1)
            pe.matmul(ps[:, 2, 0:3 * HD], pick[:], lT[:], start=True, stop=True).then_inc(sem("t_bd"), 1)

            pe.wait_ge(sem("n2"), 1)
            for j in range(NA):
                mm = pe.transpose(ps[:, 0, j * P:(j + 1) * P], ahn[:, j, :], ident[:])
            mm.then_inc(sem("t_n2"), 1)
            pe.wait_ge(sem("n2T"), 1)
            pe.wait_ge(sem("wT_set"), 1)
            pe.wait_ge(sem("mod_read"), 1)
            pe.wait_ge(sem("bd_set"), 1)
            for k, bank in ((1, 1), (0, 2), (2, 3)):
                pe.matmul(ps[:, bank, 0:NATT], wT[:, k, :], n2T[:], start=True, stop=True).then_inc(sem("qkv"), 1)

            def heads_map(k, srcT, bank, when, value, done):
                pe.wait_ge(sem(when), value)
                for j in range(NA):
                    mm = pe.matmul(ps[:, bank, j * D:(j + 1) * D], srcT[:, j * P:(j + 1) * P],
                                   bd[:, k, :, :].rearrange("p h o -> p (h o)"), start=True, stop=True)
                mm.then_inc(sem(done), 1)

            pe.wait_ge(sem("mod_read"), 2)
            heads_map(1, kT, 4, "kT", 1, "kp")
            heads_map(0, qT, 7, "qT", 1, "qp")
            heads_map(2, vT, 5, "vT", 1, "vp")
            modulation(1, 1, 2, 3)
            pe.wait_ge(sem("recur_rows"), 1)
            pe.wait_ge(sem("ld_recur"), 16 * 16)
            pe.transpose(ps[:, 0, 0:D], win_n[:], ident[:])
            pe.transpose(ps[:, 0, D:2 * D], wo_n[:, 0, :], ident[:])
            pe.transpose(ps[:, 0, 2 * D:3 * D], wo_n[:, 1, :], ident[:])
            nb = NE * NB
            pe.transpose(ps[:, 0, 3 * D:3 * D + nb], b_inr[:, 0, :], ident[0:nb, 0:nb])
            pe.transpose(ps[:, 0, 3 * D + nb:3 * D + 2 * nb], b_inr[:, 1, :], ident[0:nb, 0:nb]).then_inc(sem("t_recur"), 1)
            pe.wait_ge(sem("late_read"), 7)

            def turn_stack(name, nj):
                for g in range(4):
                    for a in range(2):
                        for j in range(nj):
                            pr = 2 * g + a
                            mm = pe.transpose(psb[:, g, a * NATT + j * P:a * NATT + (j + 1) * P],
                                              stack[:, j * HEADS + 2 * pr:j * HEADS + 2 * pr + 2, :].rearrange("p h s -> p (h s)"),
                                              identb[:])
                    mm.then_inc(sem(name), 1)

            pe.wait_ge(sem("k_stack"), 1)
            turn_stack("kstackT", NA)

            def attend(it):
                nj, nw = -(-WINDOWS[it] // P), WINDOWS[it]
                pe.wait_ge(sem("q_stack"), 2 * it + 1)
                if it == 0:
                    pe.wait_ge(sem("ks_set"), 1)
                    pe.wait_ge(sem("ks_odd"), 4)
                if it == 1:
                    pe.wait_ge(sem("lg_read_far"), 1)
                if it == 2:
                    pe.wait_ge(sem("counts_read_far"), 1)
                turn_stack("stackT", nj)
                pe.wait_ge(sem("qs_vec"), 2 * (2 * it + 1))
                pe.wait_ge(sem("qs_act"), 2 * (2 * it + 1))
                pe.wait_ge(sem("ks_set"), it + 1)
                pe.wait_ge(sem("ks_odd"), 4)
                with pe.Fori(0, HEADS // 2) as i:
                    for b in range(2):
                        pe.wait_ge(sem("max_free"), 2 * i + (HEADS * it + b + 1))
                        for j in range(nj):
                            mm = pe.matmul(ps[:, 3 * b + j, 0:nw], qs[:, bass.ds(i, 1), j * P:(j + 1) * P],
                                           ks[:, bass.ds(2 * i + b, 1), 0:nw], start=True, stop=True)
                        mm.then_inc(sem("s_ready"), 1)
                pe.wait_ge(sem("q_stack"), 2 * it + 2)
                turn_stack("stackT", nj)
                pe.wait_ge(sem("qs_vec"), 2 * (2 * it + 2))
                pe.wait_ge(sem("qs_act"), 2 * (2 * it + 2))
                def scores_t(i, q):
                    pair, b = 2 * i + q // 2, q % 2
                    if not (isinstance(i, int) and HEADS * it + 4 * i + q < 2):
                        pe.wait_ge(sem("probs_ready"), 4 * i + (HEADS * it + q - 1))
                    for j in range(nj):
                        mm = pe.matmul(ps[:, 3 * b + j, 0:nw], ks[:, bass.ds(4 * i + q, 1), j * P:(j + 1) * P],
                                       qs[:, bass.ds(pair, 1), 0:nw], start=True, stop=True)
                    mm.then_inc(sem("st_ready"), 1)

                def weigh(i, q):
                    if q == 0 and not (isinstance(i, int) and i == 0):
                        pe.wait_ge(sem("o_taken"), i + (HEADS // 4 * it))
                    pe.wait_ge(sem("probs_ready"), 4 * i + (HEADS * it + q + 1))
                    for jk in range(nj):
                        mm = pe.matmul(ps[q * OROW:(q + 1) * OROW, 6, 0:nw], v_now[:, q, jk, :], probs[:, q % 2, jk, 0:nw],
                                       start=(jk == 0), stop=(jk == nj - 1))
                    mm.then_inc(sem("probs_free"), 1)

                scores_t(0, 0)
                scores_t(0, 1)
                weigh(0, 0)
                scores_t(0, 2)
                weigh(0, 1)
                scores_t(0, 3)
                with pe.Fori(0, HEADS // 4 - 1) as i:
                    weigh(i, 2)
                    scores_t(i + 1, 0)
                    weigh(i, 3)
                    scores_t(i + 1, 1)
                    weigh(i + 1, 0)
                    scores_t(i + 1, 2)
                    weigh(i + 1, 1)
                    scores_t(i + 1, 3)
                weigh(HEADS // 4 - 1, 2)
                weigh(HEADS // 4 - 1, 3)
                pe.wait_ge(sem("o_taken"), HEADS // 4 * (it + 1))
                for j in range(nj):
                    for g in range(HEADS // 4):
                        mm = pe.transpose(ps[:, j, g * P:(g + 1) * P], oT[:, g, j * P:(j + 1) * P], ident[:])
                mm.then_inc(sem("o_turned"), 1)
                if it < 2:
                    pe.wait_ge(sem("att_done"), it + 1)
                    for j in range(NA):
                        mm = pe.transpose(ps[:, 5, j * P:(j + 1) * P], att[it][:, j, :], ident[:])
                    mm.then_inc(sem("attT"), 1)
                    pe.wait_ge(sem("asum"), it + 1)
                    pe.matmul(ps[:, 6, 0:1], ones[:], asum[:], start=True, stop=True).then_inc(sem("change"), 1)
                    heads_map(0, qT, 7, "qT", it + 2, "qp")

            def router0(g):
                lo, hi, _ = GROUPS[g]
                pe.wait_ge(sem("rows_" + g), 1)
                steps = -(-(hi - lo) // 4)

                def turn(q):
                    if q >= 2:
                        pe.wait_ge(sem("hT_" + g), q - 1)
                    for j in range(4 * q, min(4 * q + 4, hi - lo)):
                        mm = pe.transpose(ps[:, TURN_BANK[g] + q % 2, (j % 4) * P:(j % 4 + 1) * P], xn[:, lo + j, :], ident[:])
                    mm.then_inc(sem("turned_" + g), 1)

                turn(0)
                for q in range(steps):
                    if q + 1 < steps:
                        turn(q + 1)
                    pe.wait_ge(sem("hT_" + g), q + 1)
                    for j in range(4 * q, min(4 * q + 4, hi - lo)):
                        mm = pe.matmul(ps[:, 2, j * NE:(j + 1) * NE], hTr[:, q % 2, (j % 4) * P:(j % 4 + 1) * P],
                                       cols[:, ROW_ROUTER:NROW], start=True, stop=True)
                    mm.then_inc(sem("hT_used_" + g), 1)

            def count(g):
                lo, hi, _ = GROUPS[g]
                pe.wait_ge(sem("chosen_" + g), 1)
                ch = chosen[:, lo:hi, :].rearrange("p j e -> p (j e)")
                pe.matmul(ps[:, 3, 0:(hi - lo) * NE], before[:], ch, start=True, stop=True)
                pe.matmul(ps[:, 4, 0:(hi - lo) * NE], onesb[:], ch, start=True, stop=True).then_inc(sem("counts_" + g), 1)

            attend(0)
            router0("far")
            attend(1)
            count("far")
            attend(2)
            pe.wait_ge(sem("att_done"), 3)
            for j in range(NA):
                mm = pe.transpose(ps[:, 5, j * P:(j + 1) * P], att[2][:, j, :], ident[:])
            mm.then_inc(sem("attT"), 1)
            pe.wait_ge(sem("attT_copied"), 1)
            for j in range(NA):
                mm = pe.matmul(ps[:, 7, j * D:(j + 1) * D], kT[:, j * P:(j + 1) * P], wT[:, 3, :], start=True, stop=True)
            mm.then_inc(sem("att_out"), 1)

            def router1(g):
                pe.wait_ge(sem("hT1f"), g + 1)
                for j in range(4 * g, 4 * g + 4):
                    mm = pe.matmul(ps[:, 2, j * NE:(j + 1) * NE], hT[:, j * P:(j + 1) * P], wrl[:], start=True, stop=True)
                return mm

            def experts(l):
                T = NTILE[l]
                regs = [pe.alloc_register(f"pe_expert{l}_{c}") for c in range(RING + 2)]

                def ids(first, n):
                    pe.reg_load(regs[0:n], eid[0:1, bass.ds(first, n)])
                    return [pe.snap(r, min_val=0, max_val=NE - 1) for r in regs[0:n]]

                def turn_x(k, c):
                    pe.wait_ge(sem(f"xs_loaded{c % RING}"), 16 * (k + (c // RING + 1 + earlier(l, c % RING))))
                    pe.transpose(ps[:, 4 + c % 2, 0:P], xs[:, c % RING, :], ident[:]).then_inc(sem("xs_used"), 1)

                def up(k, c):
                    t = RING * k + c
                    pe.wait_ge(sem("xsT_ready"), t + 1 + tiles_before(l))
                    pe.wait_ge(sem("w_ready"), t + 1 + tiles_before(l))
                    if not isinstance(t, int) or t >= RING:
                        pe.wait_ge(sem("hb_ready"), t - (RING - 1) + tiles_before(l))
                    for n in range(NB):
                        mm = pe.matmul(ps[:, c % RING, n * P:(n + 1) * P], w_now[:, c % 2, n * P:(n + 1) * P], xsT[:, c % 2, :],
                                       start=True, stop=True)
                    mm.then_inc(sem("h_ready"), 1)

                def down(k, c, e):
                    t = RING * k + c
                    pe.wait_ge(sem("hg_ready"), t + 1 + tiles_before(l))
                    if not isinstance(t, int) or t >= 2:
                        pe.wait_ge(sem("ys_ready"), t - 1 + tiles_before(l))
                    for n in range(NB):
                        mm = pe.matmul(ps[:, 6 + c % 2, 0:D], hg[:, c % RING, n * P:(n + 1) * P],
                                       w_out[:, bass.ds(e * NB + n, 1), :], start=(n == 0), stop=(n == NB - 1))
                    mm.then_inc(sem("o_ready"), 1)

                pe.wait_ge(sem("slots_" + ("far", "all")[l]), 1)
                pe.wait_ge(sem(f"ld_experts{l}"), 48)
                pe.wait_ge(sem("out_gated"), 2 * (l + 1))
                turn_x(0, 0)
                turn_x(0, 1)
                up(0, 0)
                up(0, 1)
                e = ids(0, 2)
                if l == 0:
                    router0("near")
                    down(0, 0, e[0])
                    count("near")
                    down(0, 1, e[1])
                    pe.wait_ge(sem("counts_read_near"), 1)
                turn_x(0, 2)
                turn_x(0, 3)
                for c in (2, 3):
                    up(0, c)
                    turn_x(0, c + 2)
                    if l:
                        down(0, c - 2, e[c - 2])
                rounds = (T - 2) // RING
                with pe.Fori(1, rounds) as k:
                    e = ids(RING * k - 2, RING)
                    for c in range(RING):
                        up(k, c)
                        turn_x(k, c + 2)
                        down(k, c - 2, e[c])
                first = RING * rounds
                e = ids(first - 2, T - first + 2)
                for t in range(first, T + 2):
                    if t < T:
                        up(0, t)
                    if t + 2 < T:
                        turn_x(0, t + 2)
                    down(0, t - 2, e[t - first])

            experts(0)
            def turn_a(q):
                lo, hi = ARRIVAL[q]
                pe.wait_ge(sem("rows1a"), q + 1)
                if q >= 2:
                    pe.wait_ge(sem("hT1a"), q - 1)
                for j in range(lo, hi):
                    mm = pe.transpose(ps[:, q % 2, (j - lo) * P:(j - lo + 1) * P], xn[:, j, :], ident[:])
                mm.then_inc(sem("turned1a"), 1)

            def modes_in(q):
                lo, hi = ARRIVAL[q]
                pe.wait_ge(sem("hT1a"), q + 1)
                pe.matmul(ps[:, 2 + q, 0:(hi - lo) * P], winT[:], hT[:, lo * P:hi * P], start=True, stop=True
                          ).then_inc(sem("modes_in"), 1)

            nfar = len(CHUNKS["far"])
            for q in range(nfar):
                turn_a(q)
                if q:
                    modes_in(q - 1)
            modes_in(nfar - 1)
            turn_a(nfar)
            modes_in(nfar)
            y0f = y0[:].rearrange("p j c -> p (j c)")
            for g in range(4):
                pe.wait_ge(sem("rotated_back"), 2 * (g + 1))
                for j in range(4):
                    t = 4 * g + j
                    pe.matmul(ps[:, 2 + g, j * D:(j + 1) * D], y0f[:, t * P:(t + 1) * P], wox[:], start=True, stop=False)
                    mm = pe.matmul(ps[:, 2 + g, j * D:(j + 1) * D], hT[:, t * P:(t + 1) * P], woy[:], start=False, stop=True)
                mm.then_inc(sem("modes_out"), 1)
            for q in range(NT // 4):
                pe.wait_ge(sem("rows1f"), q + 1)
                for j in range(4):
                    mm = pe.transpose(ps[:, q % 2, j * P:(j + 1) * P], y0[:, 4 * q + j, :], ident[:])
                mm.then_inc(sem("turned1f"), 1)
                for g in ((), (0,), (1, 2), ())[q]:
                    router1(g)
            router1(NT // 4 - 1).then_inc(sem("hT_used_all"), 1)
            count("all")
            experts(1)

        @block.vector
        def _(v):
            steps = [0]

            def then(ins):
                steps[0] += 1
                ins.then_inc(sem("v_step"), 1)
                v.wait_ge(sem("v_step"), steps[0])

            def signal(ins, name, value):
                ins.then_inc(sem(name), 1)
                v.wait_ge(sem(name), value)

            def rsqrt(src, dst, n):
                yv, a = rs_y[:, 0:n], rs_a[:, 0:n]
                then(v.tensor_scalar(yv.bitcast(I32), src.bitcast(I32), -0.5, RSQRT_MAGIC, ALU.mult, ALU.add))
                for k in range(3):
                    then(v.scalar_tensor_tensor(out=a, in0=yv, scalar=-0.5, in1=yv, op0=ALU.mult, op1=ALU.mult))
                    then(v.tensor_tensor(a, a, src, ALU.mult))
                    then(v.scalar_tensor_tensor(out=dst if k == 2 else yv, in0=a, scalar=1.5, in1=yv, op0=ALU.add, op1=ALU.mult))

            def row_sums(src, lo, hi):
                for j in range(lo, hi):
                    ins = v.bn_stats(stats[:, j, :], src[:, j, :])
                then(ins)
                for j in range(lo, hi):
                    ins = v.bn_aggr(mv[:, j, :], stats[:, j, :])
                then(ins)

            def row_scales(lo, hi):
                then(v.tensor_scalar(rs_v[:, 0:hi - lo], mv[:, lo:hi, 1], LN_EPS, None, ALU.add))
                rsqrt(rs_v[:, 0:hi - lo], rstd[:, lo:hi], hi - lo)

            def for_scalar(lo, hi, done, value):
                signal(v.scalar_tensor_tensor(out=nmr[:, lo:hi], in0=mv[:, lo:hi, 0], scalar=-1.0, in1=rstd[:, lo:hi], op0=ALU.mult, op1=ALU.mult), done, value)

            def layernorm(src, dst, lo, hi, done=None):
                row_sums(src, lo, hi)
                row_scales(lo, hi)
                for j in range(lo, hi):
                    ins = v.tensor_scalar(dst[:, j, :], src[:, j, :], mv[:, j, 0:1], rstd[:, j:j + 1], ALU.subtract, ALU.mult)
                if done:
                    signal(ins, done, 1)
                else:
                    then(ins)

            def rowwise(ap, n):
                return ap.unsqueeze(1).to_broadcast([P, n, D])

            then(v.memset(onesb[:], 1.0))
            then(v.memset(v_now[:], 0.0))
            then(v.memset(stack[:], 0.0))
            then(v.memset(stack[:, :, 1:4], -1.0))
            then(v.memset(vpx[:], 1.0))
            v.wait_ge(sem("ld_x_attn"), 16)
            layernorm(x, xn, 0, NA)
            v.wait_ge(sem("t_cols"), 1)
            signal(v.tensor_copy(cols[:], ps[:, 0, 0:NROW]), "cols_set", 1)
            v.wait_ge(sem("silu_exp"), 1)
            then(v.tensor_scalar(silu[:, 1, :], silu[:, 0, :], 1.0, None, ALU.add))
            then(v.reciprocal(silu[:, 1, :], silu[:, 1, :]))
            then(v.tensor_tensor(silu[:, 2, :], silu[:, 1, :], cols[:, 0:2], ALU.mult))
            for l in range(2):
                ins = v.tensor_scalar(siluw[:, l, :], ones[:], silu[:, 2, l:l + 1], None, ALU.mult)
            ins.then_inc(sem("silu_set"), 1)
            v.wait_ge(sem("t_lT"), 1)
            then(v.tensor_copy(lT[:], ps[0:HD, 2, 64:64 + 3 * HD]))
            qk = lT[:, 0:2 * HD].rearrange("d (k o) -> d k o", k=2)
            then(v.tensor_reduce(lmean[0:HD, :], qk, AX.X, ALU.add))
            v.scalar_tensor_tensor(out=qk, in0=lmean[0:HD, :].unsqueeze(2).to_broadcast([HD, 2, HD]), scalar=-1.0 / HD, in1=qk,
                                   op0=ALU.mult, op1=ALU.add).then_inc(sem("lT_set"), 1)
            then(v.tensor_copy(identb[:], ident[:]))
            v.wait_ge(sem("mod_first"), 1)
            m0 = modrow[0][:].rearrange("p a c -> p (a c)")
            signal(v.tensor_copy(m0[:, 0:512], ps[:, 3, :]), "mod_read", 1)
            then(v.scalar_tensor_tensor(out=ah[:], in0=rowwise(modrow[0][:, CA, :], NA), scalar=1.0, in1=xn[:, 0:NA, :], op0=ALU.add, op1=ALU.mult))
            then(v.tensor_tensor(ah[:], ah[:], rowwise(modrow[0][:, SA, :], NA), ALU.add))
            layernorm(ah, ahn, 0, NA, "n2")
            v.wait_ge(sem("t_wT"), 1)
            v.tensor_scalar(wT[:, 0, :], ps[:, 1, 0:D], cols[:, ROW_LNA:ROW_LNA + 1], None, ALU.mult)
            for k in (1, 2):
                v.tensor_scalar(wT[:, k, :], ps[:, 1, k * D:(k + 1) * D], cols[:, ROW_LNB:ROW_LNB + 1], None, ALU.mult)
            signal(v.tensor_copy(wT[:, 3, :], ps[:, 1, 3 * D:4 * D]), "wT_set", 1)
            v.wait_ge(sem("t_n2"), 1)
            signal(v.tensor_copy(n2T[:], ps[:, 0, 0:NATT]), "n2T", 1)
            v.wait_ge(sem("t_bd"), 1)
            for k in range(3):
                ins = v.tensor_tensor(bd[:, k, :, :], blockm[:], ps[:, 2, k * HD:(k + 1) * HD].unsqueeze(1).to_broadcast([P, HEADS, HD]), ALU.mult)
            signal(ins, "bd_set", 1)
            v.wait_ge(sem("mod_made"), 1)
            v.tensor_copy(modcol[0][:], ps[:, 5, 0:6])
            signal(v.tensor_copy(m0[:, 512:768], ps[:, 4, 0:256]), "mod_read", 2)

            def clamp_gates(l):
                for c in (CA, CB):
                    v.tensor_scalar(modrow[l][:, c, :], modrow[l][:, c, :], 1.0, None, ALU.add)
                    v.tensor_scalar(modcol[l][:, c:c + 1], modcol[l][:, c:c + 1], 1.0, None, ALU.add)
                g = modrow[l][:, GA:GB + 1:GB - GA, :]
                then(v.tensor_scalar(gsign[:], g, 0.0, 2.0, ALU.is_ge, ALU.mult))
                then(v.tensor_scalar(gsign[:], gsign[:], -1.0, None, ALU.add))
                then(v.scalar_tensor_tensor(out=g, in0=g, scalar=-1.0, in1=g, op0=ALU.mult, op1=ALU.max))
                signal(v.scalar_tensor_tensor(out=g, in0=g, scalar=0.25, in1=gsign[:], op0=ALU.max, op1=ALU.mult), "gates_clamped", l + 1)

            def recurrence_maps():
                v.wait_ge(sem("ld_recur"), 16 * 16)
                then(v.tensor_scalar(win_n[96:128, :], win_n[96:128, :], -1.0, None, ALU.mult))
                wr, wi = wo_s[:, 0:NF], wo_s[:, NF:2 * NF]
                for a, parts in enumerate((((wr, 1.0), (wi, 1.0), (wi, 1.0), (wr, -1.0)),
                                           ((wi, 1.0), (wr, -1.0), (wr, -1.0), (wi, -1.0)))):
                    for q, (src, sign) in enumerate(parts):
                        ins = v.tensor_scalar(wo_n[:, a, q * NF:(q + 1) * NF], src, sign, None, ALU.mult)
                ins.then_inc(sem("recur_rows"), 1)

            def recurrence_angles():
                then(v.tensor_scalar(ph[:, 0:1], fcol[:, 0:1], float(np.float32(0.1)), None, ALU.mult))
                then(v.tensor_scalar(ph[:, 1:2], ph[:, 0:1], float(np.pi / 2), None, ALU.add))
                then(v.tensor_scalar(phi[:, 0:2], ph[:, 0:2], float(1 / TWO_PI), None, ALU.mult))
                then(v.tensor_copy(ph[:, 2:4], phi[:, 0:2]))
                for part in (TP1, TP2, TP3):
                    then(v.scalar_tensor_tensor(out=ph[:, 4:6], in0=ph[:, 2:4], scalar=-part, in1=ph[:, 0:2] if part == TP1 else ph[:, 4:6], op0=ALU.mult, op1=ALU.add))
                lim = 3.1415925
                signal(v.tensor_scalar(ph[:, 4:6], ph[:, 4:6], lim, -lim, ALU.min, ALU.max), "angles", 1)

            v.wait_ge(sem("kidx_set"), 2)
            then(v.tensor_copy(kidx[:], kidx_i[:]))
            v.wait_ge(sem("ld_small"), 16 * 5)
            v.wait_ge(sem("lT_set"), 1)
            then(v.tensor_reduce(lmean[:], small[:, 0:2, :], AX.X, ALU.add))
            then(v.scalar_tensor_tensor(out=small[:, 0:2, :], in0=lmean[:].unsqueeze(2).to_broadcast([P, 2, HD]), scalar=-1.0 / HD, in1=small[:, 0:2, :],
                                        op0=ALU.mult, op1=ALU.add))
            then(v.tensor_tensor(small[:, 4, :], small[:, 3, :], small[:, 4, :], ALU.mult))
            v.memset(cw[:, 0:1], float(W0))
            then(v.memset(att[0][:], 0.0))
            v.memset(mx[:], 0.0).then_inc(sem("max_free"), 2)
            v.memset(flags[:], 0.0).then_inc(sem("probs_free"), 2)
            v.wait_ge(sem("max_free"), 2)
            v.wait_ge(sem("probs_free"), 2)
            v.wait_ge(sem("qkv"), 2)
            signal(v.tensor_scalar(qT[:], ps[:, 2, 0:NATT], cols[:, ROW_BQ:ROW_BQ + 1], float(HD ** -0.25), ALU.add, ALU.mult), "qT", 1)
            v.wait_ge(sem("ld_scalars"), 16 * 5)
            then(v.tensor_copy(tsc[:, 0:1], scal[:, 2:3]))
            then(v.tensor_scalar(tsc[:, 1:2], tsc[:, 0:1], 0.005, None, ALU.add))
            then(v.tensor_scalar(tsc[:, 2:3], tsc[:, 1:2], 0.005, None, ALU.add))
            then(v.tensor_scalar(rs_v[:, 0:3], tsc[:, 0:3], 1e-37, None, ALU.max))
            rsqrt(rs_v[:, 0:3], tsc[:, 3:6], 3)
            then(v.tensor_scalar(rs_v[:, 0:3], tsc[:, 0:3], 0.0, None, ALU.is_gt))
            then(v.tensor_scalar(tsc[:, 3:6], tsc[:, 3:6], -1.0, None, ALU.add))
            then(v.tensor_tensor(tsc[:, 3:6], tsc[:, 3:6], rs_v[:, 0:3], ALU.mult))
            then(v.tensor_scalar(tsc[:, 3:6], tsc[:, 3:6], 1.0, None, ALU.add))

            def grouped(t, nj):
                return t[:, 0:nj * HEADS, :]

            def each(ap8, nj):
                return ap8.unsqueeze(1).to_broadcast([P, nj * HEADS, HD])

            def per(ap, nj):
                return ap[:, 0:nj * HEADS].unsqueeze(2).to_broadcast([P, nj * HEADS, HD])

            def head_norm(bank, bias, nj, weight=None, tscale=None):
                gc, gs = grouped(gl_c, nj), grouped(gl_s, nj)
                n = nj * HEADS
                then(v.tensor_tensor(gc, ps[:, bank, 0:n * HD].rearrange("p (g o) -> p g o", o=HD), each(small[:, bias, :], nj), ALU.add))
                then(v.tensor_tensor(gs, gc, gc, ALU.mult))
                then(v.tensor_reduce(rs_v[:, 0:n], gs, AX.X, ALU.add))
                then(v.tensor_scalar(rs_v[:, 0:n], rs_v[:, 0:n], 1.0 / HD, LN_EPS, ALU.mult, ALU.add))
                rsqrt(rs_v[:, 0:n], gl_m[:, 0:n], n)
                if tscale is not None:
                    then(v.tensor_scalar(gl_m[:, 0:n], gl_m[:, 0:n], tscale, float(np.float32(1 / np.sqrt(HD))), ALU.mult, ALU.mult))
                then(v.tensor_tensor(gc, gc, per(gl_m, nj), ALU.mult))
                if weight is not None:
                    then(v.tensor_tensor(gc, gc, each(small[:, weight, :], nj), ALU.mult))

            def slot(s, nj):
                return stack[:, 0:nj * HEADS, s * SLOT:(s + 1) * SLOT]

            def split(nj, firsts, copies):
                gc, r1 = grouped(gl_c, nj), grouped(gl_s, nj)
                then(v.tensor_copy(slot(firsts[0], nj), gc))
                then(v.tensor_tensor(r1, gc, slot(firsts[0], nj), ALU.subtract))
                then(v.tensor_copy(slot(firsts[1], nj), r1))
                then(v.tensor_tensor(r1, r1, slot(firsts[1], nj), ALU.subtract))
                then(v.tensor_copy(slot(firsts[2], nj), r1))
                for a, b in copies:
                    ins = v.tensor_copy(slot(b, nj), slot(a, nj))
                return ins

            recurrence_maps()
            v.wait_ge(sem("kp"), 1)
            head_norm(4, 1, NA, weight=4)
            signal(split(NA, K_FIRST, K_COPIES), "k_stack", 1)
            v.wait_ge(sem("vp"), 1)
            then(v.tensor_tensor(vpx[:, :, :, 0:HD].rearrange("p j h o -> p (j h) o"), ps[:, 5, 0:NATT].rearrange("p (g o) -> p g o", o=HD), each(small[:, 2, :], NA), ALU.add))
            v.wait_ge(sem("ks_zero"), 1)
            for g in range(4):
                v.wait_ge(sem("kstackT"), g + 1)
                ins = v.tensor_copy(ks[0:STK, 4 * g:4 * g + 4:2, :], psb[0:STK, g, 0:2 * NATT].rearrange("p (a n) -> p a n", a=2))
            signal(ins, "ks_set", 1)
            v.memset(stack[:, :, 1:4], 0.0)
            then(v.memset(stack[:, :, 0:1], 1.0))

            def stack_copies(n, nj):
                for g in (0, 2):
                    v.wait_ge(sem("stackT"), 4 * n + g + 1)
                    v.tensor_copy(qs[:, 2 * g:2 * g + 2, 0:nj * P], psb[:, g, 0:2 * NATT].rearrange("p (a n) -> p a n", a=2)[:, :, 0:nj * P]
                                  ).then_inc(sem("qs_vec"), 1)

            def lowest(lgt, m, dst, lo, hi):
                n = hi - lo
                bc = lambda t: t.unsqueeze(2).to_broadcast([P, n, NE])
                c = cand[:, lo:hi, :]
                then(v.tensor_reduce(m, lgt, AX.X, ALU.max))
                then(v.tensor_tensor(c, lgt, bc(m), ALU.is_equal))
                then(v.tensor_tensor(c, c, e_rank[:].unsqueeze(1).to_broadcast([P, n, NE]), ALU.mult))
                then(v.tensor_reduce(posf[:, lo:hi], c, AX.X, ALU.max))
                then(v.tensor_tensor(dst, c, bc(posf[:, lo:hi]), ALU.is_equal))

            def read_logits(g):
                lo, hi, experts = GROUPS[g]
                n = hi - lo
                pl = ps[:, 2, 0:n * NE].rearrange("p (j e) -> p j e", e=NE)
                if experts == 2:
                    v.wait_ge(sem("hT_used_" + g), -(-n // 4))
                    signal(v.tensor_copy(lg[:, lo:hi, :], pl), "lg_read_" + g, 1)
                else:
                    v.wait_ge(sem("hT_used_" + g), 1)
                    then(v.tensor_tensor(lg[:, lo:hi, :], pl, br_row[:].unsqueeze(1).to_broadcast([P, n, NE]), ALU.add))

            def choose(g):
                lo, hi, experts = GROUPS[g]
                n = hi - lo
                s = slice(lo, hi)
                lowest(lg[:, s, :], top[:, 0, s], first[0][:, s, :], lo, hi)
                if experts == 2:
                    then(v.scalar_tensor_tensor(out=lg2[:, s, :], in0=first[0][:, s, :], scalar=-3e38, in1=lg[:, s, :], op0=ALU.mult, op1=ALU.add))
                    lowest(lg2[:, s, :], top[:, 1, s], first[1][:, s, :], lo, hi)
                    signal(v.tensor_tensor(chosen[:, s, :], first[0][:, s, :], first[1][:, s, :], ALU.add), "chosen_" + g, 1)
                    signal(v.tensor_tensor(top[:, 2, s], top[:, 1, s], top[:, 0, s], ALU.subtract), "top_gap_" + g, 1)
                else:
                    signal(v.tensor_copy(chosen[:, s, :], first[0][:, s, :]), "chosen_" + g, 1)
                    signal(v.tensor_tensor(lg2[:], lg[:], top[:, 0, :].unsqueeze(2).to_broadcast([P, NT, NE]), ALU.subtract), "lg_shifted", 1)

            def read_counts(g):
                lo, hi, experts = GROUPS[g]
                m = (hi - lo) * NE
                v.wait_ge(sem("counts_" + g), 1)
                v.tensor_copy(pose[:, lo:hi, :], ps[:, 3, 0:m].rearrange("p (j e) -> p j e", e=NE))
                signal(v.tensor_copy(tot_f[:, 0:m].rearrange("p (e j) -> p e j", e=NE),
                                     ps[:, 4, 0:m].rearrange("p (j e) -> p e j", e=NE)), "counts_read_" + g, 1)

            def place(g):
                lo, hi, experts = GROUPS[g]
                n = hi - lo
                t0, t1 = SORTED[g]
                s = slice(lo, hi)
                fl = lambda t: t[:, 0:NE * n]
                ej = lambda t: fl(t).rearrange("p (e j) -> p e j", e=NE)
                inc, tot, cmp_t = ej(inc_f), ej(tot_f), ej(cmp_f)
                then(v.tensor_tensor_scan(fl(inc_f), keep[g][:].rearrange("p e j -> p (e j)"), fl(tot_f), 0.0, ALU.mult, ALU.add))
                then(v.tensor_tensor(cmp_t, inc[:, :, n - 1:n].to_broadcast([P, NE, n]), step128[:, 0:n].unsqueeze(1).to_broadcast([P, NE, n]), ALU.is_gt))
                v.tensor_tensor(inc, inc, tot, ALU.subtract)
                then(v.tensor_reduce(ntile[:], cmp_t, AX.X, ALU.add))
                then(v.tensor_tensor_scan(tend[:], ones[:, 0:NE], ntile[:], float(t0), ALU.mult, ALU.add))
                then(v.tensor_tensor(tbase[:], tend[:], ntile[:], ALU.subtract))
                then(v.scalar_tensor_tensor(out=inc, in0=tbase[:].unsqueeze(2).to_broadcast([P, NE, n]), scalar=float(P), in1=inc,
                                            op0=ALU.mult, op1=ALU.add))
                then(v.tensor_tensor(pose[:, s, :], pose[:, s, :], inc.rearrange("p e j -> p j e"), ALU.add))
                for k in range(experts):
                    then(v.tensor_tensor(cand[:, s, :], pose[:, s, :], first[k][:, s, :], ALU.mult))
                    then(v.tensor_reduce(posf[:, s], cand[:, s, :], AX.X, ALU.add))
                    ins = v.tensor_copy(posu[:, k, s], posf[:, s])
                    if k < experts - 1:
                        then(ins)
                signal(ins, "slots_" + g, 1)

            def tile_experts(g):
                t0, t1 = SORTED[g]
                T = t1 - t0
                then(v.tensor_tensor(cmp_e[:, t0:t1, :], tidx[:, t0:t1].unsqueeze(2).to_broadcast([P, T, NE]), tend[:].unsqueeze(1).to_broadcast([P, T, NE]), ALU.is_ge))
                then(v.tensor_reduce(eidf[:, t0:t1], cmp_e[:, t0:t1, :], AX.X, ALU.add))
                then(v.tensor_scalar(eid[:, t0:t1], eidf[:, t0:t1], float(NE - 1), None, ALU.min))

            def gates(g):
                lo, hi, experts = GROUPS[g]
                s = slice(lo, hi)
                if experts == 2:
                    v.wait_ge(sem("gap_exp_" + g), 1)
                    then(v.tensor_scalar(gate[:, 1, s], top[:, 2, s], 1.0, None, ALU.add))
                    then(v.reciprocal(gate[:, 0, s], gate[:, 1, s]))
                    signal(v.tensor_tensor(gate[:, 1, s], top[:, 2, s], gate[:, 0, s], ALU.mult), "gates_" + g, 1)
                else:
                    v.wait_ge(sem("lg_exp"), 1)
                    then(v.tensor_reduce(posf[:], lg2[:], AX.X, ALU.add))
                    signal(v.reciprocal(token_rows[:, :, 2 * D], posf[:]), "gates_all", 1)

            up_, dn_, conv_ = 0, 2, 4

            def attention_scaled(it):
                nj = -(-WINDOWS[it] // P)
                n = nj * HEADS
                v.wait_ge(sem("o_turned"), it + 1)
                o = ps[:, 0:nj, :].rearrange("p j (h s) -> p (j h) s", s=OROW)
                then(v.tensor_scalar(den[:, 0:n], o[:, :, HD], 0.5, None, ALU.max))
                then(v.reciprocal(den[:, 0:n], den[:, 0:n]))
                a3 = att[it][:].rearrange("p j (h o) -> p (j h) o", o=HD)[:, 0:n, :]
                d3 = den[:, 0:n].rearrange("p (j h) -> p j h", h=HEADS)
                then(v.tensor_tensor(d3, d3, rowm[:, 0:nj].unsqueeze(2).to_broadcast([P, nj, HEADS]), ALU.mult))
                ins = v.tensor_tensor(a3, o[:, :, 0:HD], per(den, nj), ALU.mult)
                if it == 2:
                    then(ins)
                else:
                    signal(ins, "att_done", it + 1)

            def attend(it):
                nj, nw = -(-WINDOWS[it] // P), WINDOWS[it]
                n = nj * HEADS
                if it:
                    for p0, h0 in ((0, 0), (STK, 1)):
                        ins = v.tensor_scalar(ks[p0:p0 + 1, h0::2, WMIN:nw], kidx[p0:p0 + 1, WMIN:nw].unsqueeze(1).to_broadcast([1, HEADS // 2, nw - WMIN]),
                                              cw[p0:p0 + 1, it:it + 1], MASKED, ALU.is_ge, ALU.mult)
                    signal(ins, "ks_set", it + 1)
                then(v.tensor_scalar(rowm[:], ridx[:], cw[:, it:it + 1], None, ALU.is_lt))
                v.wait_ge(sem("qp"), it + 1)
                head_norm(7, 0, nj, tscale=tsc[:, 3 + it:4 + it])
                if it:
                    then(v.memset(stack[:, :, 1:4], 0.0))
                signal(split(nj, Q_FIRST, Q_COPIES), "q_stack", 2 * it + 1)
                if it == 1:
                    read_logits("far")
                if it == 2:
                    read_counts("far")
                stack_copies(2 * it, nj)
                with v.Fori(0, HEADS // 2) as i:
                    for b in range(2):
                        v.wait_ge(sem("s_ready"), 2 * i + (HEADS * it + b + 1))
                        v.tensor_reduce(mx[:, 0:nj, bass.ds(2 * i + b, 1)], ps[:, 3 * b:3 * b + nj, 0:nw], AX.X, ALU.max
                                        ).then_inc(sem("max_free"), 1)
                v.wait_ge(sem("max_free"), 2 + HEADS * (it + 1))
                m, r = mx[:, 0:nj, :].rearrange("p j h -> p (j h)"), mr[:, 0:n]
                for k in range(3):
                    dst = stack[:, 0:n, 1 + k]
                    src = m if k == 0 else r
                    ins = v.tensor_copy(dst, src)
                    if k < 2:
                        then(ins)
                        then(v.tensor_tensor(r, src, dst, ALU.subtract))
                signal(ins, "q_stack", 2 * it + 2)
                stack_copies(2 * it + 1, nj)
                if it == 0:
                    clamp_gates(0)
                    v.wait_ge(sem("ld_x_rest"), 16)
                    v.tensor_tensor(wT[:, 3, :], wT[:, 3, :], modrow[0][:, GA, :], ALU.mult)
                    then(v.tensor_tensor(ahn[:, 0, :], bo_row[:], modrow[0][:, GA, :], ALU.mult))
                    then(v.tensor_tensor(x[:], x[:], rowwise(ahn[:, 0, :], NT), ALU.add))
                    v.wait_ge(sem("tables_set"), 5 + len(GROUPS))
                    layernorm(x, xn, NA, NT, "rows_far")
                    recurrence_angles()
                    v.wait_ge(sem("ks_odd"), 4)
                    v.memset(ks[0:1, 0::2, WINDOWS[1]:NATT], MASKED)
                    then(v.memset(ks[STK:STK + 1, 1::2, WINDOWS[1]:NATT], MASKED))
                elif it == 1:
                    choose("far")
                    def change(f, dst):
                        base, a, b = f(W0) - W0, f(_up(W0)) - _up(W0), f(_down(W0)) - _down(W0)
                        then(v.tensor_scalar(dst, flags[:, up_:up_ + 1], float(a - base), float(base), ALU.mult, ALU.add))
                        then(v.scalar_tensor_tensor(out=dst, in0=flags[:, dn_:dn_ + 1], scalar=float(b - base), in1=dst, op0=ALU.mult, op1=ALU.add))
                    change(_up, tsc[:, 6:7])
                    change(_down, tsc[:, 7:8])
                    v.wait_ge(sem("decay_exp"), 1)
                    then(v.tensor_scalar(decay[:, 1:2], decay[:, 0:1], 1.0, None, ALU.add))
                    then(v.reciprocal(decay[:, 1:2], decay[:, 1:2]))
                    v.wait_ge(sem("late_read"), 7)
                    clamp_gates(1)
                    v.tensor_tensor(wox[:], wox[:], modrow[1][:, GA, :], ALU.mult)
                    then(v.tensor_tensor(woy[:], woy[:], modrow[1][:, GA, :], ALU.mult))
                else:
                    place("far")
                    tile_experts("far")
                    gates("far")
                    then(v.scalar_tensor_tensor(out=tsc[:, 6:7], in0=diff[:, 1:2], scalar=scal[:, 1:2], in1=scal[:, 0:1], op0=ALU.mult, op1=ALU.add))
                    then(v.tensor_tensor(flags[:, conv_:conv_ + 1], diff[:, 1:2], tsc[:, 6:7], ALU.is_lt))
                    then(v.tensor_scalar(flags[:, conv_ + 1:conv_ + 2], flags[:, conv_:conv_ + 1], -1.0, 1.0, ALU.mult, ALU.add))
                    v.tensor_scalar(att[1][:], att[1][:], flags[:, conv_:conv_ + 1], None, ALU.mult)
                    then(v.tensor_scalar(rowm[:], rowm[:], flags[:, conv_ + 1:conv_ + 2], None, ALU.mult))
                    return
                attention_scaled(it)
                af = att[it][:].rearrange("p j c -> p (j c)")
                if it:
                    then(v.tensor_tensor(att_d[:], af, att[it - 1][:].rearrange("p j c -> p (j c)"), ALU.subtract))
                    af = att_d[:]
                signal(v.tensor_reduce(asum[:], af, AX.X, ALU.add, apply_absolute_value=True), "asum", it + 1)
                v.wait_ge(sem("attT"), it + 1)
                signal(v.tensor_tensor(qT[:], qT[:], ps[:, 5, 0:NATT], ALU.add), "qT", it + 2)
                v.wait_ge(sem("change"), it + 1)
                df = diff[:, it:it + 1]
                then(v.tensor_scalar(df, ps[:, 6, 0:1], 1.0 / (N * D), None, ALU.mult))
                up, dn = flags[:, up_ + it:up_ + it + 1], flags[:, dn_ + it:dn_ + it + 1]
                v.tensor_scalar(up, df, 0.05, None, ALU.is_gt)
                then(v.tensor_scalar(dn, df, 0.001, None, ALU.is_lt))
                nxt = cw[:, it + 1:it + 2]
                if it == 0:
                    then(v.tensor_scalar(nxt, up, float(_up(W0) - W0), float(W0), ALU.mult, ALU.add))
                    then(v.scalar_tensor_tensor(out=nxt, in0=dn, scalar=float(_down(W0) - W0), in1=nxt, op0=ALU.mult, op1=ALU.add))
                else:
                    then(v.scalar_tensor_tensor(out=nxt, in0=tsc[:, 6:7], scalar=up, in1=cw[:, it:it + 1], op0=ALU.mult, op1=ALU.add))
                    then(v.scalar_tensor_tensor(out=nxt, in0=tsc[:, 7:8], scalar=dn, in1=nxt, op0=ALU.mult, op1=ALU.add))

            def attention_out():
                signal(v.tensor_tensor(att[2][:], att[2][:], att[1][:], ALU.add), "att_done", 3)
                v.wait_ge(sem("attT"), 3)
                signal(v.tensor_copy(kT[:], ps[:, 5, 0:NATT]), "attT_copied", 1)
                v.wait_ge(sem("att_out"), 1)
                then(v.tensor_tensor(x[:, 0:NA, :], x[:, 0:NA, :], ps[:, 7, 0:NATT].rearrange("p (j c) -> p j c", c=D), ALU.add))

            def add_ffn(q):
                lo, hi = ARRIVAL[q]
                s = slice(lo, hi)
                v.wait_ge(sem("gated"), q + 1)
                then(v.tensor_tensor(x[:, s, :], x[:, s, :], y0[:, s, :], ALU.add))
                then(v.tensor_tensor(x[:, s, :], x[:, s, :], y1[:, s, :], ALU.add))
                row_sums(x, lo, hi)

            def experts(l):
                T = NTILE[l]
                rounds = (T - 2) // RING
                first = RING * rounds
                regs = [v.alloc_register(f"v_expert{l}_{c}") for c in range(max(RING + 4, T - first + 2))]

                def ids(start, n):
                    v.reg_load(regs[0:n], eid[0:1, bass.ds(start, n)])
                    return [v.snap(r, min_val=0, max_val=NE - 1) for r in regs[0:n]]

                def lay_out(c, e):
                    v.tensor_copy(w_now[:, c % 2, :], w_in[:, bass.ds(e, 1), :].rearrange("p e h -> p (e h)")).then_inc(sem("w_ready"), 1)

                def bias_up(k, c, e):
                    t = RING * k + c
                    v.wait_ge(sem("h_ready"), t + 1 + tiles_before(l))
                    if not isinstance(t, int) or t >= 2:
                        v.wait_ge(sem("hg_ready"), t - 1 + tiles_before(l))
                    v.tensor_tensor(hb[:, c % 2, :].rearrange("p (b t) -> p b t", b=NB), ps[:, c % RING, :].rearrange("p (b t) -> p b t", b=NB),
                                    b_in[:, l, bass.ds(e, 1), :].rearrange("p e b -> p (e b)").unsqueeze(2).to_broadcast([P, NB, P]), ALU.add
                                    ).then_inc(sem("hb_ready"), 1)

                def bias_down(k, c, e):
                    t = RING * k + c
                    if not isinstance(t, int) or t >= RING:
                        v.wait_ge(sem(("ys_stored", "ys_sent")[l] + str(c % RING)), 16 * (k + c // RING))
                    v.wait_ge(sem("o_ready"), t + 1 + tiles_before(l))
                    y = ys[:, c % RING, :]
                    ins = v.tensor_tensor(y, ps[:, 6 + c % 2, 0:D], b_out[:, bass.ds(e, 1), :], ALU.add)
                    if l == 0:
                        ins.then_inc(sem("ys_ready"), 1)
                        return
                    ins.then_inc(sem("ys_biased"), 1)
                    v.wait_ge(sem(f"rest_loaded{c % RING}"), 16 * (k + (c // RING + 1)))
                    r = rest[:, c % RING, :]
                    v.tensor_scalar(target[:, c % RING:c % RING + 1], r[:, D + 1:D + 2], float(N), None, ALU.add)
                    v.wait_ge(sem("ys_biased"), t + 1)
                    v.scalar_tensor_tensor(out=y, in0=y, scalar=r[:, D:D + 1], in1=r[:, 0:D], op0=ALU.mult, op1=ALU.add
                                           ).then_inc(sem("ys_ready"), 1)

                v.wait_ge(sem(f"ld_experts{l}"), 48)
                v.wait_ge(sem("out_gated"), 2 * (l + 1))
                e = ids(0, RING + 2)
                lay_out(0, e[0])
                lay_out(1, e[1])
                if l == 0:
                    attention_scaled(2)
                    attention_out()
                    layernorm(x, xn, 0, NA, "rows_near")
                for c in range(RING):
                    if l == 0 and c == 2:
                        read_logits("near")
                        choose("near")
                        read_counts("near")
                        place("near")
                        tile_experts("near")
                    bias_up(0, c, e[c])
                    lay_out(c + 2, e[c + 2])
                    if c >= 2:
                        bias_down(0, c - 2, e[c - 2])
                with v.Fori(1, rounds) as k:
                    e = ids(RING * k - 2, RING + 4)
                    for c in range(RING):
                        bias_up(k, c, e[c + 2])
                        lay_out(c + 2, e[c + 4])
                        bias_down(k, c - 2, e[c])
                e = ids(first - 2, T - first + 2)
                for t in range(first, T + 2):
                    if t < T:
                        bias_up(0, t, e[t - first + 2])
                    if t + 2 < T:
                        lay_out(t + 2, e[t - first + 4])
                    bias_down(0, t - 2, e[t - first])

            for it in range(3):
                attend(it)
            experts(0)
            gates("near")
            nfar = len(CHUNKS["far"])
            for q in range(nfar):
                add_ffn(q)
            row_scales(NA, NT)
            for_scalar(NA, NT, "stats_a", 1)
            add_ffn(nfar)
            row_scales(0, NA)
            for_scalar(0, NA, "stats_a", 2)
            v.wait_ge(sem("rotations"), 1)
            z, rx = (t.rearrange("p j c -> p (j c)") for t in (y1, y0[:]))
            ry = hT
            for q, (lo, hi) in enumerate(ARRIVAL):
                s = slice(lo * P, hi * P)
                v.wait_ge(sem("modes_in"), q + 1)
                ins = v.tensor_tensor(rx[:, s], ps[:, 2 + q, 0:(hi - lo) * P], rotx[:, s], ALU.mult)
            then(ins)
            for g in range(4):
                a, b = 512 * g, 512 * (g + 1)
                then(v.tensor_tensor_scan(z[:, a:b], decay[:, 1:2].to_broadcast([P, b - a]), rx[:, a:b], z[:, a - 1:a] if g else 0.0, ALU.mult, ALU.add))
                v.tensor_tensor(rx[:, a:b], z[:, a:b], rotx[:, a + 1:b + 1], ALU.mult).then_inc(sem("rotated_back"), 1)
                signal(v.tensor_tensor(ry[:, a:b], z[:, a:b], roty[:, a + 1:b + 1], ALU.mult), "rotated_back", 2 * (g + 1))
            for g in range(4):
                s = slice(4 * g, 4 * g + 4)
                v.wait_ge(sem("modes_out"), g + 1)
                then(v.tensor_tensor(x[:, s, :], x[:, s, :], ps[:, 2 + g, :].rearrange("p (j c) -> p j c", c=D), ALU.add))
                row_sums(x, 4 * g, 4 * g + 4)
            row_scales(0, NT)
            for_scalar(0, NT, "stats_f", 1)
            for q, (lo, hi) in enumerate(CHUNKS["all"]):
                s = slice(lo, hi)
                v.wait_ge(sem("normed1f"), q + 1)
                then(v.tensor_tensor(y0[:, s, :], y0[:, s, :], rowwise(modrow[1][:, CB, :], hi - lo), ALU.mult))
                signal(v.tensor_tensor(y0[:, s, :], y0[:, s, :], rowwise(modrow[1][:, SB, :], hi - lo), ALU.add), "rows1f", q + 1)
                row_sums(y0, lo, hi)
            row_scales(0, NT)
            for_scalar(0, NT, "stats_f", 2)
            read_logits("all")
            choose("all")
            read_counts("all")
            place("all")
            gates("all")
            tile_experts("all")
            experts(1)


_OUT = ("out", (1, N, D))
_SCRATCH = (("rows0", (T0 * P, D)), ("rows1", (T1 * P, ROW1)), ("back0", (T0 * P, D)))


def kernel(**inputs):
    import concourse.bacc as bacc
    from concourse.bass_utils import run_bass_kernel_spmd

    nc = bacc.Bacc("TRN2", target_bir_lowering=False, num_devices=1)
    arrays, aps = {}, {}
    for name, value in inputs.items():
        a = np.ascontiguousarray(value)
        if a.ndim == 0:
            a = a.reshape(1)
        arrays["in_" + name] = a
        aps[name] = nc.dram_tensor("in_" + name, a.shape, mybir.dt.from_np(a.dtype), kind="ExternalInput").ap()
    out = nc.dram_tensor(_OUT[0], _OUT[1], F32, kind="ExternalOutput").ap()
    scratch = [nc.dram_tensor(name, shape, F32, kind="Internal").ap() for name, shape in _SCRATCH]
    build_adaln(nc, aps, out, *scratch)
    r = run_bass_kernel_spmd(nc, [arrays], core_ids=[0])
    return r.results[0][_OUT[0]]
```
